# Optimizing a Trainium2 kernel written in Bass

```python
import numpy as np
import jax
import jax.numpy as jnp

def _softmax(x, axis=-1):
    return jax.nn.softmax(x, axis=axis)
def _gelu(x):
    return jax.nn.gelu(x, approximate=True)
def _silu(x):
    return jax.nn.silu(x)
def _sigmoid(x):
    return jax.nn.sigmoid(x)
def _layernorm(x, axis=-1, eps=1e-5):
    m = jnp.mean(x, axis=axis, keepdims=True)
    v = jnp.var(x, axis=axis, keepdims=True)
    return (x - m) / jnp.sqrt(v + eps)
def _scatter_add(tgt, idx, src, axis=0):
    return tgt.at[idx].add(src)
def _segment_sum(src, seg, n):
    return jax.ops.segment_sum(src, seg, n)

kernel_name = 'mk_adj_resnorm_d4_adj_128_ffbc93'

def setup_inputs(seed: int = 0):
    np.random.seed(seed)
    _w = jnp.asarray
    def _rec_inputs():
        import jax
        import jax.numpy as jnp
        _gk = jax.random.key(seed)
        x = -0.0005207 + 1.001 * jax.random.normal(jax.random.fold_in(_gk, 1), (16, 1024, 128), jnp.float32)
        _a = jax.random.bernoulli(jax.random.fold_in(_gk, 2), 0.03125, (16, 1024, 1024))
        adj = _a.astype(jnp.int32)
        return x, adj
    x, adj = _rec_inputs()
    def _L0_gnn_setup():
        import jax, jax.numpy as jnp
        import numpy as np
        NEG_INF = -1000000000.0
        LEAKY_ALPHA = 0.2
        key = jax.random.key(seed)
        k1, k2, k3, k4 = jax.random.split(key, 4)
        B, N, F, U = (8, 2048, 128, 128)
        X = jax.random.normal(k1, (B, N, F), dtype=jnp.float32)
        A = jax.random.randint(k2, (B, N, N), 0, 2, dtype=jnp.int32)
        W = jax.random.normal(k3, (F, U), dtype=jnp.float32) * 0.1
        a = jax.random.normal(k4, (2 * U, 1), dtype=jnp.float32) * 0.1
        return {'X': X, 'A': A, 'W': W, 'a': a}
    _L0_gnn_all = _L0_gnn_setup()
    _L0_gnn_in = {k: v for k, v in _L0_gnn_all.items() if k in ('W', 'a', )}
    del _L0_gnn_all

    def _L1_gnn_setup():
        import jax, jax.numpy as jnp
        import numpy as np
        B, N = (4, 2048)
        IN_F, OUT_F, H = (128, 128, 8)
        HD = OUT_F // H
        ALPHA = 0.2
        TIME_DECAY = 0.1
        key = jax.random.key(seed)
        k1, k2, k3, k4, k5 = jax.random.split(key, 5)
        node_features = jax.random.normal(k1, (B, N, IN_F), dtype=jnp.float32)
        adj_matrix = jax.random.randint(k2, (B, N, N), 0, 2, dtype=jnp.int32)
        time_matrix = jax.random.uniform(k3, (B, N, N), dtype=jnp.float32)

        def xavier(k, shape, fan_in, fan_out):
            bound = 1.414 * np.sqrt(6.0 / (fan_in + fan_out))
            return jax.random.uniform(k, shape, minval=-bound, maxval=bound, dtype=jnp.float32)
        W = xavier(k4, (H, IN_F, HD), IN_F, HD)
        a = xavier(k5, (H, 2 * HD, 1), 2 * HD, 1)
        return {'node_features': node_features, 'adj_matrix': adj_matrix, 'time_matrix': time_matrix, 'W': W, 'a': a}
    _L1_gnn_all = _L1_gnn_setup()
    _L1_gnn_in = {k: v for k, v in _L1_gnn_all.items() if k in ('W', 'a', )}
    del _L1_gnn_all

    def _L2_gnn_setup():
        import jax, jax.numpy as jnp
        import numpy as np
        NUM_RELATIONS = 8
        INPUT_DIM = 128
        HIDDEN_DIM = 128
        LN_EPS = 1e-05
        key = jax.random.key(seed)
        k0, k1, k2, k3, k4 = jax.random.split(key, 5)
        B, T = (4, 2048)
        node_features = jax.random.normal(k0, (B, T, INPUT_DIM), dtype=jnp.float32)
        spatial_matrix = jax.random.randint(k1, (B, T, T), 0, NUM_RELATIONS, dtype=jnp.int32)
        bound = float(np.sqrt(6.0 / (INPUT_DIM + HIDDEN_DIM)))
        rel_weights = jax.random.uniform(k2, (NUM_RELATIONS, INPUT_DIM, HIDDEN_DIM), jnp.float32, -bound, bound)
        lin_bound = float(1.0 / np.sqrt(INPUT_DIM))
        self_w = jax.random.uniform(k3, (HIDDEN_DIM, INPUT_DIM), jnp.float32, -lin_bound, lin_bound)
        self_b = jax.random.uniform(k4, (HIDDEN_DIM,), jnp.float32, -lin_bound, lin_bound)
        ln_gamma = jnp.ones((HIDDEN_DIM,), jnp.float32)
        ln_beta = jnp.zeros((HIDDEN_DIM,), jnp.float32)
        return {'node_features': node_features, 'spatial_matrix': spatial_matrix, 'rel_weights': rel_weights, 'self_w': self_w, 'self_b': self_b, 'ln_gamma': ln_gamma, 'ln_beta': ln_beta}
    _L2_gnn_all = _L2_gnn_setup()
    _L2_gnn_in = {k: v for k, v in _L2_gnn_all.items() if k in ('rel_weights', 'self_w', 'self_b', 'ln_gamma', 'ln_beta', )}
    del _L2_gnn_all

    def _L3_gnn_setup():
        import jax, jax.numpy as jnp
        import numpy as np
        NEG_INF = -9000000000000000.0
        key = jax.random.key(seed)
        k1, k2, k3 = jax.random.split(key, 3)
        B, S, F = (8, 2048, 128)
        H, D = (4, 32)
        features = jax.random.normal(k1, (B, S, F), dtype=jnp.float32)
        adj_matrix = jax.random.randint(k2, (B, S, S), 0, 2, dtype=jnp.int32)
        limit = float(np.sqrt(6.0 / (F + D)))
        W = jax.random.uniform(k3, (H, F, D), dtype=jnp.float32, minval=-limit, maxval=limit)
        return {'features': features, 'adj_matrix': adj_matrix, 'W': W}
    _L3_gnn_all = _L3_gnn_setup()
    _L3_gnn_in = {k: v for k, v in _L3_gnn_all.items() if k in ('W', )}
    del _L3_gnn_all

    return {
        "x": x,
        "adj": adj,
        "L0_gnn_W": _L0_gnn_in["W"],
        "L0_gnn_a": _L0_gnn_in["a"],
        "L1_gnn_W": _L1_gnn_in["W"],
        "L1_gnn_a": _L1_gnn_in["a"],
        "L2_gnn_rel_weights": _L2_gnn_in["rel_weights"],
        "L2_gnn_self_w": _L2_gnn_in["self_w"],
        "L2_gnn_self_b": _L2_gnn_in["self_b"],
        "L2_gnn_ln_gamma": _L2_gnn_in["ln_gamma"],
        "L2_gnn_ln_beta": _L2_gnn_in["ln_beta"],
        "L3_gnn_W": _L3_gnn_in["W"],
    }

def reference(x, adj, L0_gnn_W, L0_gnn_a, L1_gnn_W, L1_gnn_a, L2_gnn_rel_weights, L2_gnn_self_w, L2_gnn_self_b, L2_gnn_ln_gamma, L2_gnn_ln_beta, L3_gnn_W):
    import jax
    import jax.numpy as jnp
    def _L0_gnn_ref(X, A, W, a):
        import jax, jax.numpy as jnp
        import numpy as np
        NEG_INF = -1000000000.0
        LEAKY_ALPHA = 0.2
        H = jnp.einsum('bnf,fu->bnu', X, W)
        U = H.shape[-1]
        a_src = a[:U, 0]
        a_dst = a[U:, 0]
        s = H @ a_src
        t = H @ a_dst
        e = s[:, :, None] + t[:, None, :]
        e = jax.nn.leaky_relu(e, negative_slope=LEAKY_ALPHA)
        mask = jnp.where(A > 0, 0.0, NEG_INF).astype(e.dtype)
        attention = jax.nn.softmax(e + mask, axis=-1)
        H_out = jnp.einsum('bij,bju->biu', attention, H)
        return jax.nn.relu(H_out)

    def _L1_gnn_ref(node_features, adj_matrix, time_matrix, W, a):
        import jax, jax.numpy as jnp
        import numpy as np
        B, N = (4, 2048)
        IN_F, OUT_F, H = (128, 128, 8)
        HD = OUT_F // H
        ALPHA = 0.2
        TIME_DECAY = 0.1
        current_time = jnp.max(time_matrix)
        time_weights = jnp.exp(-TIME_DECAY * (current_time - time_matrix))
        h = jnp.einsum('bni,hio->bhno', node_features, W)
        a_src = a[:, :HD, 0]
        a_dst = a[:, HD:, 0]
        e_i = jnp.einsum('bhnd,hd->bhn', h, a_src)
        e_j = jnp.einsum('bhnd,hd->bhn', h, a_dst)
        e = e_i[:, :, :, None] + e_j[:, :, None, :]
        e = jax.nn.leaky_relu(e, negative_slope=ALPHA)
        e = e * time_weights[:, None, :, :]
        mask = adj_matrix[:, None, :, :] == 0
        e = jnp.where(mask, -jnp.inf, e)
        attention = jax.nn.softmax(e, axis=-1)
        out = jnp.einsum('bhij,bhjo->bhio', attention, h)
        out = jnp.transpose(out, (0, 2, 1, 3)).reshape(node_features.shape[0], node_features.shape[1], -1)
        return jax.nn.elu(out)

    def _L2_gnn_ref(node_features, spatial_matrix, rel_weights, self_w, self_b, ln_gamma, ln_beta):
        import jax, jax.numpy as jnp
        import numpy as np
        NUM_RELATIONS = 8
        INPUT_DIM = 128
        HIDDEN_DIM = 128
        LN_EPS = 1e-05
        num_relations = rel_weights.shape[0]
        dtype = node_features.dtype
        B, T, _ = node_features.shape
        agg = jnp.zeros((B, T, rel_weights.shape[2]), dtype=dtype)
        for r in range(1, num_relations):
            mask = (spatial_matrix == r).astype(dtype)
            degree = jnp.clip(mask.sum(axis=2, keepdims=True), 1e-06, None)
            neighbors = jnp.einsum('bts,bsd->btd', mask / degree, node_features)
            agg = agg + neighbors @ rel_weights[r]
        self_feat = node_features @ self_w.T + self_b
        out = agg + self_feat
        mean = out.mean(axis=-1, keepdims=True)
        var = out.var(axis=-1, keepdims=True)
        out = (out - mean) * jax.lax.rsqrt(var + LN_EPS) * ln_gamma + ln_beta
        return jax.nn.relu(out)

    def _L3_gnn_ref(features, adj_matrix, W):
        import jax, jax.numpy as jnp
        import numpy as np
        NEG_INF = -9000000000000000.0
        D = W.shape[-1]
        Wh = jnp.einsum('bsf,hfd->bhsd', features, W)
        scores = jnp.einsum('bhsd,bhtd->bhst', Wh, Wh) / jnp.sqrt(jnp.float32(D))
        scores = jnp.where(adj_matrix[:, None, :, :] > 0, scores, NEG_INF)
        attn = jax.nn.softmax(scores, axis=-1)
        h = jnp.einsum('bhst,bhtd->bhsd', attn, Wh)
        B, H, S, _ = h.shape
        return jnp.transpose(h, (0, 2, 1, 3)).reshape(B, S, H * D)

    x = _layernorm(x + _L0_gnn_ref(x, adj, L0_gnn_W, L0_gnn_a), axis=-1)
    x = _layernorm(x + _L1_gnn_ref(x, adj, adj, L1_gnn_W, L1_gnn_a), axis=-1)
    x = _layernorm(x + _L2_gnn_ref(x, adj, L2_gnn_rel_weights, L2_gnn_self_w, L2_gnn_self_b, L2_gnn_ln_gamma, L2_gnn_ln_beta), axis=-1)
    x = _layernorm(x + _L3_gnn_ref(x, adj, L3_gnn_W), axis=-1)
    return x


_drawn_inputs = setup_inputs


def setup_inputs(seed=0):
    import zlib

    import numpy as np

    out = dict(_drawn_inputs(seed))
    spreads = {'L2_gnn_ln_gamma': (1.0, 0.2), 'L2_gnn_ln_beta': (0.0, 0.1)}
    factors = {}
    for name, (base, spread) in spreads.items():
        noise = np.random.default_rng([zlib.crc32(name.encode()), seed]).standard_normal(out[name].shape)
        drawn = base * np.exp(spread * noise) if base else spread * noise
        out[name] = jnp.asarray(drawn.astype(out[name].dtype))
    for name, factor in factors.items():
        out[name] = (out[name] * factor).astype(out[name].dtype)
    return out
```

```python
from contextlib import ExitStack

import concourse.bass as bass
from concourse import mybir

ALU = mybir.AluOpType
ACT = mybir.ActivationFunctionType
AX_X = mybir.AxisListType.X
BF16 = mybir.dt.bfloat16
F32 = mybir.dt.float32

P = 128
SLOPE = 0.2
EPS = 1e-5
BIG = 2.0 ** 100
PARTS = 3


class Signal:

    def __init__(self, sem, per_batch):
        self.sem, self.per_batch = sem, per_batch

    def of(self, b, k=None):
        return b * self.per_batch + (self.per_batch if k is None else k)

    def any_before(self, b):
        return not (isinstance(b, int) and b <= 0)

    def before(self, b):
        return b * self.per_batch


class Steps:

    def __init__(self, sem):
        self.sem, self.count, self.per_batch = sem, 0, None

    def begin(self, b):
        if self.count and self.per_batch is None:
            self.per_batch = self.count
        assert self.per_batch is None or self.count == self.per_batch
        self.b, self.count = b, 0

    def step(self):
        self.count += 1
        return self.count if self.per_batch is None else self.b * self.per_batch + self.count


def graph_stack(nc, x, adj, L0_gnn_W, L0_gnn_a, L1_gnn_W, L1_gnn_a, L2_gnn_rel_weights, L2_gnn_self_w,
                L2_gnn_self_b, L2_gnn_ln_gamma, L2_gnn_ln_beta, L3_gnn_W, out):
    NB, N, D = x.shape
    T = N // P
    H1, _, O1 = L1_gnn_W.shape
    H3, _, O3 = L3_gnn_W.shape
    HALF = N // 2
    C1 = O1 + 1
    C3 = O3 + 1
    U1, U3 = H1 * T, H3 * T
    PER = 3
    GROUPS = [range(g, min(g + PER, T)) for g in range(0, T, PER)]
    ROOT = float(O3) ** -0.5
    B_RING, P_RING, P0_RING, R_RING = 6, 4, 3, 3
    nc.disable_value_cache = True
    assert D == P and H1 * O1 == D and H3 * O3 == D and N == 1024 and NB % 2 == 0

    with ExitStack() as ctx:
        def sb(name, shape, dt=F32):
            return ctx.enter_context(nc.sbuf_tensor(name, shape, dt))

        def signal(name, per_batch):
            return Signal(ctx.enter_context(nc.semaphore(name)), per_batch)

        def sem(name):
            return ctx.enter_context(nc.semaphore(name))

        ident = sb("ident", [P, P])
        identb = sb("identb", [P, P], BF16)
        ones = sb("ones", [P, P])
        half_neg = sb("half_neg", [P, T])
        a0_row = sb("a0_row", [P, 2, D])
        a1_row = sb("a1_row", [P, H1, 2 * O1])
        w_tmp = sb("w_tmp", [P, D])
        rhs0 = sb("rhs0", [P, D + 2])
        src0 = sb("src0", [P, P])
        dst0 = sb("dst0", [P, P])
        rhs1 = sb("rhs1", [P, D + 2 * H1])
        src1 = sb("src1", [P, H1, P])
        self_w = sb("self_w", [P, D])
        rhs2 = sb("rhs2", [P, 2 * D])
        bias2 = sb("bias2", [P, D])
        gamma2 = sb("gamma2", [P, D])
        beta2 = sb("beta2", [P, D])
        rhs3 = sb("rhs3", [P, D])

        AT = sb("AT", [P, 2, T, N], BF16)
        x2 = sb("x2", [P, 2, T, D])

        A_rows = sb("A_rows", [P, T, N], BF16)
        x0 = sb("x0", [P, T, D])
        T0 = sb("T0", [P, 1])
        T0neg = sb("T0neg", [P, 1])
        T0neg2 = sb("T0neg2", [P, 1])
        v0 = sb("v0", [P, T])
        v0s = sb("v0s", [P, T])
        h0 = sb("h0", [P, T, D + 1])
        weight0 = sb("weight0", [P, P0_RING, N])
        rec0 = sb("rec0", [P, T])
        yf = sb("yf", [P, T, D])
        x1 = sb("x1", [P, T, D])
        h1 = sb("h1", [P, T, H1, C1])
        st1 = sb("st1", [P, T, 2 * H1])
        tmax1 = sb("tmax1", [P, H1])
        tcol1 = sb("tcol1", [H1, 1])
        tdiag1 = sb("tdiag1", [H1, H1])
        T1 = sb("T1", [P, H1])
        tneg1 = sb("tneg1", [P, T, H1])
        tbig1 = sb("tbig1", [P, T, H1])
        dt1 = sb("dt1", [P, T, H1])
        zs1 = sb("zs1", [P, T, H1])
        v1 = sb("v1", [P, 2, T, H1])
        c1 = sb("c1", [P, T, H1])
        vh = sb("vh", [P, T, H1, 2, C1])
        vh_rest = sb("vh_rest", [P, T, H1, 2, C1])
        vh_parts = sb("vh_parts", [P, T, H1, 2, PARTS, C1], BF16)
        s1row = sb("s1row", [P, 2, N])
        ramp = sb("ramp", [P, R_RING, N], BF16)
        rec1 = sb("rec1", [P, T, H1])
        xfT = sb("xfT", [P, N])
        x0T = x1T = xfT
        edges = weight0[:].rearrange("p r n -> p (r n)").bitcast(BF16).rearrange(
            "p (r n) -> p r n", n=N)
        elu = weight0[:, 0, :].rearrange("p (t d) -> p t d", t=T)
        c0 = s1row[:, 0, :]
        sumB = vh
        sumA = vh_rest[:, :, :, 0, :]
        fstat = sb("fstat", [P, T, 6])
        fsmall = sb("fsmall", [P, 6, T])

        deg2 = sb("deg2", [P, T])
        yb = sb("yb", [P, T, D])
        x3 = sb("x3", [P, T, D])
        w3 = sb("w3", [P, T * H3, C3])
        cutT = sb("cutT", [P, H3, 2, N], BF16)
        q3 = sb("q3", [P, T * H3])
        qmax3 = sb("qmax3", [P, H3])
        qcol3 = sb("qcol3", [H3, 1])
        qdiag3 = sb("qdiag3", [H3, H3])
        shift3 = sb("shift3", [P, H3])
        weight3 = sb("weight3", [P, P_RING, N])
        rec3 = sb("rec3", [P, H3, T])
        xbT = sb("xbT", [P, N])
        x2T = x3T = xbT
        x4 = yb
        cutT_all = cutT[:].rearrange("p h a n -> p (h a n)")
        y2_hi = cutT_all[:, 0:T * (D + 1)].rearrange("p (t d) -> p t d", t=T)
        y2_lo = cutT_all[:, T * (D + 1):T * (3 * D + 1)].rearrange(
            "p (t k d) -> p t k d", t=T, k=2)
        self2 = cutT_all[:, 4 * N:6 * N].bitcast(F32).rearrange("p (t d) -> p t d", t=T)
        rest2 = cutT_all[:, 6 * N:8 * N].bitcast(F32).rearrange("p (t d) -> p t d", t=T)
        rest3 = rest2.rearrange("p t (h o) -> p (t h) o", h=H3)
        ring3 = weight3[:].rearrange("p r n -> p (r n)").bitcast(BF16).rearrange(
            "p (w t k o) -> p w t k o", w=2, t=T * H3, k=4)
        cutA, cutB = ring3[:, 0], ring3[:, 1]
        bstat = sb("bstat", [P, T, 6])
        bsmall = sb("bsmall", [P, 6, T])

        fp = ctx.enter_context(nc.psum_tensor("fp", [P, 3, HALF], F32))
        kp = ctx.enter_context(nc.psum_tensor("kp", [P, 5, HALF], F32))
        fp_pair = fp[:, 1:3, :].rearrange("p a b -> p (a b)")
        score_bank = [kp[:, 1 + 2 * r:3 + 2 * r, :].rearrange("p a b -> p (a b)") for r in range(2)]

        def thirds(psum, g, width):
            n = len(GROUPS[g])
            return psum[:, g, 0:n * width].rearrange("p (t c) -> p t c", t=n)

        def tiles(g):
            return slice(GROUPS[g][0], GROUPS[g][-1] + 1)

        w_loaded = sem("w_loaded")
        consts_made = sem("consts_made")
        self_turned = sem("self_turned")
        weights_ready = sem("weights_ready")
        turnstile = sem("turnstile")
        a_loaded = signal("a_loaded", 16)
        x_loaded = signal("x_loaded", 16)
        a_turned = signal("a_turned", T)
        at_act = signal("at_act", T // 2)
        at_dve = signal("at_dve", T // 2)
        x0_turned = signal("x0_turned", 1)
        x0T_ready = signal("x0T_ready", 1)
        t0_spread = signal("t0_spread", 1)
        T0_ready = signal("T0_ready", 1)
        s0_spread = signal("s0_spread", 1)
        z0_ready = signal("z0_ready", 1)
        c0_ready = signal("c0_ready", 1)
        h0_made = signal("h0_made", 1)
        h0_ready = signal("h0_ready", 1)
        weight0_ready = signal("weight0_ready", T)
        weight0_used = signal("weight0_used", T)
        x1_ready = signal("x1_ready", 1)
        x1_turned = signal("x1_turned", 1)
        x1T_ready = signal("x1T_ready", 1)
        h1_made = signal("h1_made", 1)
        h1_ready = signal("h1_ready", 1)
        st1_ready = signal("st1_ready", 1)
        tmax1_ready = signal("tmax1_ready", 1)
        tmax1_turned = signal("tmax1_turned", 1)
        tdiag1_ready = signal("tdiag1_ready", 1)
        T1_spread = signal("T1_spread", 1)
        z1_ready = signal("z1_ready", 1)
        v1_ready = signal("v1_ready", 1)
        vh_ready = signal("vh_ready", 1)
        sumA_made = signal("sumA_made", 1)
        sumA_ready = signal("sumA_ready", 1)
        s1_spread = signal("s1_spread", 2 * H1)
        s1_ready = signal("s1_ready", 2 * H1)
        ramp_ready = signal("ramp_ready", U1 // 2)
        edges_ready = signal("edges_ready", U1)
        edges_used = signal("edges_used", U1)
        sumB_ready = signal("sumB_ready", H1)
        elu_min = signal("elu_min", 1)
        elu_exp = signal("elu_exp", 1)
        x2_ready = signal("x2_ready", 1)
        fvar_ready = signal("fvar_ready", 2)
        frstd_ready = signal("frstd_ready", 2)
        x2_turned = signal("x2_turned", 1)
        x2T_ready = signal("x2T_ready", 1)
        y2_made = signal("y2_made", 1)
        y2_ready = signal("y2_ready", 1)
        sum2_made = signal("sum2_made", 1)
        bvar_ready = signal("bvar_ready", 3)
        brstd_ready = signal("brstd_ready", 3)
        x3_ready = signal("x3_ready", 1)
        x3_turned = signal("x3_turned", 1)
        x3T_ready = signal("x3T_ready", 1)
        w3_made = signal("w3_made", 1)
        w3_ready = signal("w3_ready", 1)
        qmax_ready = signal("qmax_ready", 1)
        qmax_turned = signal("qmax_turned", 1)
        qdiag_ready = signal("qdiag_ready", 1)
        q_spread = signal("q_spread", 1)
        shift_ready = signal("shift_ready", 1)
        cut_turned = signal("cut_turned", 2 * H3)
        cutT_act = signal("cutT_act", H3)
        cutT_dve = signal("cutT_dve", H3)
        scores_made = signal("scores_made", U3)
        exp3_ready = signal("exp3_ready", U3)
        weight3_ready = signal("weight3_ready", U3)
        weight3_used = signal("weight3_used", U3)
        sum3_ready = signal("sum3_ready", H3)
        x4_ready = signal("x4_ready", 1)
        stored = signal("stored", 16)
        dve_setup = sem("dve_setup")
        dve_front = sem("dve_front")
        dve_back = sem("dve_back")

        block = ctx.enter_context(nc.Block())

        def schedule(eng, body):
            body(0, 0, None)
            body(1, 1, 0)
            with eng.Fori(2, NB - 1, 2) as i:
                body(0, i, i - 1)
                body(1, i + 1, i)
            body(0, None, NB - 1)

        def rows(dram, b):
            return dram[bass.ds(b, 1)].rearrange("b (t p) d -> p (b t) d", p=P)

        @block.sync
        def _(sp):
            loads = [
                (rhs0[:, 0:D], L0_gnn_W),
                (a0_row[:], L0_gnn_a.rearrange("(k u) o -> o k u", k=2).broadcast_to([P, 2, D])),
                (rhs1[:, 0:D].rearrange("p (h o) -> p h o", h=H1), L1_gnn_W.rearrange("h f o -> f h o")),
                (a1_row[:], L1_gnn_a.rearrange("h k o -> o h k").broadcast_to([P, H1, 2 * O1])),
                (rhs2[:, 0:D], L2_gnn_rel_weights[1]),
                (self_w[:], L2_gnn_self_w),
                (bias2[:], L2_gnn_self_b.rearrange("(a d) -> a d", a=1).broadcast_to([P, D])),
                (gamma2[:], L2_gnn_ln_gamma.rearrange("(a d) -> a d", a=1).broadcast_to([P, D])),
                (beta2[:], L2_gnn_ln_beta.rearrange("(a d) -> a d", a=1).broadcast_to([P, D])),
                (rhs3[:].rearrange("p (h o) -> p h o", h=H3), L3_gnn_W.rearrange("h f o -> f h o")),
            ]
            for dst, src in loads:
                sp.dma_start(dst, src).then_inc(w_loaded, 16)

            def body(parity, f, k):
                if f is not None:
                    if x1_ready.any_before(f):
                        sp.wait_ge(x1_ready.sem, x1_ready.before(f))
                    sp.sem_inc(turnstile, 1)
                    sp.dma_start(x0[:], rows(x, f)).then_inc(x_loaded.sem, 16)
                if k is not None:
                    sp.wait_ge(x4_ready.sem, x4_ready.of(k))
                    sp.sem_inc(turnstile, 1)
                    sp.dma_start(rows(out, k), x4[:]).then_inc(stored.sem, 16)

            schedule(sp, body)
            sp.wait_ge(stored.sem, stored.of(NB - 1))

        @block.gpsimd
        def _(pool):
            pool.memset(ones[:], 1.0).then_inc(consts_made, 1)
            pool.memset(half_neg[:], -0.5).then_inc(consts_made, 1)
            pool.wait_ge(consts_made, 2)
            pool.affine_select(out=ident[:], in_=ones[:], compare_op=ALU.is_equal, fill=0.0, base=0,
                               pattern=[[-1, P]], channel_multiplier=1).then_inc(consts_made, 1)

            def rstd(signal_in, signal_out, small, b, n):
                pool.wait_ge(signal_in.sem, signal_in.of(b, n + 1))
                pool.tensor_tensor(small[:, 5, :], small[:, 4, :], half_neg[:], ALU.pow) \
                    .then_inc(signal_out.sem, 1)

            def body(parity, f, k):
                if f is not None:
                    if a_turned.any_before(f):
                        pool.wait_ge(a_turned.sem, a_turned.before(f))
                    pool.sem_inc(turnstile, 1)
                    pool.dma_start(A_rows[:], adj[bass.ds(f, 1)].rearrange("b (t p) n -> p (b t) n", p=P)) \
                        .then_inc(a_loaded.sem, 16)
                if k is not None:
                    rstd(bvar_ready, brstd_ready, bsmall, k, 0)
                    rstd(bvar_ready, brstd_ready, bsmall, k, 1)
                if f is not None:
                    rstd(fvar_ready, frstd_ready, fsmall, f, 0)
                    rstd(fvar_ready, frstd_ready, fsmall, f, 1)
                if k is not None:
                    rstd(bvar_ready, brstd_ready, bsmall, k, 2)

            schedule(pool, body)

        @block.tensor
        def _(pe):
            def turn_rows(src, dst, done):
                for t in range(T):
                    last = pe.transpose(dst[:, t * P:(t + 1) * P], src[:, t, :], ident[:])
                last.then_inc(done.sem, 1)

            def project(xT, rhs, width, dst, done):
                for g in range(len(GROUPS)):
                    for n, t in enumerate(GROUPS[g]):
                        last = pe.matmul(dst[:, g, n * width:(n + 1) * width], xT[:, t * P:(t + 1) * P], rhs,
                                         start=True, stop=True)
                last.then_inc(done.sem, 1)

            def spread(lhsT, rhs, dst):
                for n in range(2):
                    last = pe.matmul(dst[:, n * HALF:(n + 1) * HALF], lhsT, rhs[:, n * HALF:(n + 1) * HALF],
                                     start=True, stop=True)
                return last

            def turn_adjacency(b, parity):
                pe.wait_ge(a_loaded.sem, a_loaded.of(b))
                for jt in range(T):
                    if jt == 0:
                        if sumB_ready.any_before(b):
                            pe.wait_ge(sumB_ready.sem, sumB_ready.before(b))
                    elif jt >= 3:
                        before = jt - 3
                        copied = at_dve if before % 2 else at_act
                        pe.wait_ge(copied.sem, copied.of(b, before // 2 + 1))
                    dst = fp[:, jt % 3, :].bitcast(BF16)
                    for t in range(T):
                        last = pe.transpose(dst[:, t * P:(t + 1) * P], A_rows[:, t, jt * P:(jt + 1) * P], identb[:])
                    last.then_inc(a_turned.sem, 1)

            def layer0_prepare(b):
                pe.wait_ge(x_loaded.sem, x_loaded.of(b))
                pe.wait_ge(at_act.sem, at_act.of(b))
                pe.wait_ge(at_dve.sem, at_dve.of(b))
                turn_rows(x0, fp_pair, x0_turned)
                pe.wait_ge(x0T_ready.sem, x0T_ready.of(b))
                spread(dst0[:], x0T, fp_pair).then_inc(t0_spread.sem, 1)
                pe.wait_ge(T0_ready.sem, T0_ready.of(b))
                spread(src0[:], x0T, fp_pair).then_inc(s0_spread.sem, 1)
                pe.wait_ge(z0_ready.sem, z0_ready.of(b))
                project(x0T, rhs0[:], D + 2, fp, h0_made)

            def layer0_sum(b):
                pe.wait_ge(h0_ready.sem, h0_ready.of(b))
                for jt in range(T):
                    pe.wait_ge(weight0_ready.sem, weight0_ready.of(b, jt + 1))
                    for g in range(len(GROUPS)):
                        for n, t in enumerate(GROUPS[g]):
                            last = pe.matmul(fp[:, g, n * (D + 1):(n + 1) * (D + 1)],
                                             weight0[:, jt % P0_RING, t * P:(t + 1) * P], h0[:, jt, :],
                                             start=(jt == 0 and n == 0), stop=(jt == T - 1), skip_group_check=True)
                    last.then_inc(weight0_used.sem, 1)

            def layer1_prepare(b, parity):
                pe.wait_ge(x1_ready.sem, x1_ready.of(b))
                turn_rows(x1, fp_pair, x1_turned)
                pe.wait_ge(x1T_ready.sem, x1T_ready.of(b))
                project(x1T, rhs1[:], D + 2 * H1, fp, h1_made)
                pe.wait_ge(tmax1_ready.sem, tmax1_ready.of(b))
                pe.wait_ge(h1_ready.sem, h1_ready.of(b))
                pe.transpose(fp[0:H1, 0, 0:P], tmax1[:], ident[:]).then_inc(tmax1_turned.sem, 1)
                pe.wait_ge(tdiag1_ready.sem, tdiag1_ready.of(b))
                pe.matmul(fp[:, 1, 0:H1], ones[0:H1, :], tdiag1[:], start=True, stop=True) \
                    .then_inc(T1_spread.sem, 1)
                pe.wait_ge(vh_ready.sem, vh_ready.of(b))
                for g in range(len(GROUPS)):
                    for n, t in enumerate(GROUPS[g]):
                        for jt in range(T):
                            for k in range(PARTS):
                                last = pe.matmul(fp[:, g, n * H1 * C1:(n + 1) * H1 * C1].rearrange(
                                                     "p (h c) -> p h c", h=H1),
                                                 AT[:, parity, jt, t * P:(t + 1) * P], vh_parts[:, jt, :, 1, k, :],
                                                 start=(jt == 0 and k == 0), stop=(jt == T - 1 and k == PARTS - 1))
                last.then_inc(sumA_made.sem, 1)
                pe.wait_ge(sumA_ready.sem, sumA_ready.of(b))

            def spread_s1(b, n):
                if n:
                    pe.wait_ge(s1_ready.sem, s1_ready.of(b, n))
                h, half = n // 2, n % 2
                pe.matmul(fp[:, 0, :], src1[:, h, :], x1T[:, half * HALF:(half + 1) * HALF],
                          start=True, stop=True).then_inc(s1_spread.sem, 1)

            def layer1_unit(b, u):
                h, jt = u // T, u % T
                pe.wait_ge(edges_ready.sem, edges_ready.of(b, u + 1))
                if jt == 0 and h:
                    pe.wait_ge(sumB_ready.sem, sumB_ready.of(b, h))
                for t in range(T):
                    col = (t % 4) * P
                    last = pe.matmul(fp[:, 1 + t // 4, col:col + 2 * PARTS * C1],
                                     edges[:, u % B_RING, t * P:(t + 1) * P],
                                     vh_parts[:, jt, h, :, :, :].rearrange("p a k c -> p (a k c)"),
                                     start=(jt == 0 and t % 4 == 0), stop=(jt == T - 1), skip_group_check=True)
                last.then_inc(edges_used.sem, 1)

            def layer2(b, parity):
                pe.wait_ge(x2_ready.sem, x2_ready.of(b))
                if sum3_ready.any_before(b):
                    pe.wait_ge(sum3_ready.sem, sum3_ready.before(b))
                turn_rows(x2[:, parity], score_bank[0], x2_turned)
                pe.wait_ge(x2T_ready.sem, x2T_ready.of(b))
                for t in range(T):
                    last = pe.matmul(kp[:, 1 + t // 2, (t % 2) * 2 * D:(t % 2 + 1) * 2 * D],
                                     x2T[:, t * P:(t + 1) * P], rhs2[:], start=True, stop=True)
                last.then_inc(y2_made.sem, 1)
                pe.wait_ge(y2_ready.sem, y2_ready.of(b))
                for g in range(len(GROUPS)):
                    for n, t in enumerate(GROUPS[g]):
                        col = n * (D + 1)
                        for jt in range(T):
                            lhsT = AT[:, parity, jt, t * P:(t + 1) * P]
                            pe.matmul(kp[:, g, col:col + D + 1], lhsT, y2_hi[:, jt, :], start=(jt == 0), stop=False,
                                      skip_group_check=True)
                            for k in range(2):
                                last = pe.matmul(kp[:, g, col:col + D], lhsT, y2_lo[:, jt, k, :], start=False,
                                                 stop=(jt == T - 1 and k == 1), skip_group_check=True)
                last.then_inc(sum2_made.sem, 1)

            def layer3_prepare(b):
                pe.wait_ge(x3_ready.sem, x3_ready.of(b))
                turn_rows(x3, score_bank[0], x3_turned)
                pe.wait_ge(x3T_ready.sem, x3T_ready.of(b))
                for t in range(T):
                    last = pe.matmul(kp[:, 3 + t // 4, (t % 4) * D:(t % 4 + 1) * D], x3T[:, t * P:(t + 1) * P],
                                     rhs3[:], start=True, stop=True)
                last.then_inc(w3_made.sem, 1)
                pe.wait_ge(qmax_ready.sem, qmax_ready.of(b))
                pe.transpose(kp[0:H3, 0, 0:P], qmax3[:], ident[:]).then_inc(qmax_turned.sem, 1)
                pe.wait_ge(qdiag_ready.sem, qdiag_ready.of(b))
                pe.matmul(kp[:, 0, P:P + H3], ones[0:H3, :], qdiag3[:], start=True, stop=True) \
                    .then_inc(q_spread.sem, 1)
                pe.wait_ge(w3_ready.sem, w3_ready.of(b))
                for n in range(2 * H3):
                    h, which = n // 2, n % 2
                    if n >= 4:
                        pe.wait_ge((cutT_dve if which else cutT_act).sem, (cutT_dve if which else cutT_act).of(b, h - 1))
                    dst = kp[:, 1 + n % 4, :].bitcast(BF16)
                    cut = (cutB if which else cutA).rearrange("p (t h) k o -> p t h (k o)", h=H3)
                    for t in range(T):
                        last = pe.transpose(dst[:, t * P:(t + 1) * P], cut[:, t, h, :], identb[:])
                    last.then_inc(cut_turned.sem, 1)
                pe.wait_ge(cutT_act.sem, cutT_act.of(b))
                pe.wait_ge(cutT_dve.sem, cutT_dve.of(b))
                pe.wait_ge(shift_ready.sem, shift_ready.of(b))

            def layer3_scores(b, w):
                h, jt = w // T, w % T
                if w >= 2:
                    pe.wait_ge(exp3_ready.sem, exp3_ready.of(b, w - 1))
                tile = slice(jt * P, (jt + 1) * P)
                for n in range(2):
                    cols = slice(n * HALF, (n + 1) * HALF)
                    pe.matmul(score_bank[w % 2][:, cols], cutT[:, h, 1, tile], cutT[:, h, 0, cols],
                              start=True, stop=False)
                    last = pe.matmul(score_bank[w % 2][:, cols], cutT[0:2 * O3, h, 0, tile],
                                     cutT[0:2 * O3, h, 1, cols], start=False, stop=True)
                last.then_inc(scores_made.sem, 1)

            def layer3_values(b, w):
                h, jt = w // T, w % T
                pe.wait_ge(weight3_ready.sem, weight3_ready.of(b, w + 1))
                if jt == 0 and h:
                    pe.wait_ge(sum3_ready.sem, sum3_ready.of(b, h))
                for t in range(T):
                    last = pe.matmul(kp[:, 0, t * C3:(t + 1) * C3], weight3[:, w % P_RING, t * P:(t + 1) * P],
                                     w3[:, jt * H3 + h, :], start=(jt == 0 and t == 0), stop=(jt == T - 1),
                                     skip_group_check=True)
                last.then_inc(weight3_used.sem, 1)

            pe.wait_ge(w_loaded, 160)
            pe.wait_ge(consts_made, 3)
            pe.transpose(fp[:, 0, 0:P], self_w[:], ident[:]).then_inc(self_turned, 1)
            pe.wait_ge(weights_ready, 1)

            def body(parity, f, k):
                if f is not None:
                    turn_adjacency(f, parity)
                    layer0_prepare(f)
                if k is not None:
                    layer2(k, 1 - parity)
                if f is not None:
                    layer0_sum(f)
                if k is not None:
                    layer3_prepare(k)
                if f is not None:
                    layer1_prepare(f, parity)
                    for n in range(4):
                        spread_s1(f, n)
                for s in range(U3 + 2):
                    if k is not None and s < U3:
                        layer3_scores(k, s)
                    if f is not None and 1 <= s <= U3:
                        layer1_unit(f, 2 * s - 2)
                        layer1_unit(f, 2 * s - 1)
                        if s % 4 == 0 and 2 * (s // 4) + 3 < 2 * H1:
                            spread_s1(f, 2 * (s // 4) + 2)
                            spread_s1(f, 2 * (s // 4) + 3)
                    if k is not None and s >= 2:
                        layer3_values(k, s - 2)

            schedule(pe, body)

        @block.scalar
        def _(act):
            def copy(dst, src):
                return act.activation(dst, src, ACT.Copy)

            def adjacency(b, parity):
                for jt in range(0, T, 2):
                    act.wait_ge(a_turned.sem, a_turned.of(b, jt + 1))
                    if jt == 0:
                        if sum2_made.any_before(b - 1):
                            act.wait_ge(sum2_made.sem, sum2_made.before(b - 1))
                        if weight3_ready.any_before(b - 1):
                            act.wait_ge(weight3_ready.sem, weight3_ready.before(b - 1))
                    copy(AT[:, parity, jt, :], fp[:, jt % 3, :].bitcast(BF16)).then_inc(at_act.sem, 1)

            def layer0_prepare(b):
                act.wait_ge(x0_turned.sem, x0_turned.of(b))
                copy(x0T[:], fp_pair).then_inc(x0T_ready.sem, 1)
                act.wait_ge(z0_ready.sem, z0_ready.of(b))
                act.activation(c0[:], c0[:], ACT.Exp, scale=-(1.0 - SLOPE)).then_inc(c0_ready.sem, 1)
                act.wait_ge(h0_made.sem, h0_made.of(b))
                for g in range(len(GROUPS)):
                    src = thirds(fp, g, D + 2)
                    act.activation(v0[:, tiles(g)], src[:, :, D + 1], ACT.Exp, bias=T0neg[:])
                    act.activation(v0s[:, tiles(g)], src[:, :, D + 1], ACT.Exp, bias=T0neg2[:], scale=SLOPE)
                    last = copy(h0[:, tiles(g), 0:D], src[:, :, 0:D])
                last.then_inc(h0_ready.sem, 1)

            def layer1_prepare(b):
                act.wait_ge(x1_turned.sem, x1_turned.of(b))
                copy(x1T[:], fp_pair).then_inc(x1T_ready.sem, 1)
                act.wait_ge(h1_made.sem, h1_made.of(b))
                for g in range(len(GROUPS)):
                    last = copy(st1[:, tiles(g), :], thirds(fp, g, D + 2 * H1)[:, :, D:D + 2 * H1])
                last.then_inc(st1_ready.sem, 1)
                for g in range(len(GROUPS)):
                    for n, t in enumerate(GROUPS[g]):
                        last = copy(h1[:, t, :, 0:O1], thirds(fp, g, D + 2 * H1)[:, n, 0:D].rearrange(
                            "p (h o) -> p h o", h=H1))
                last.then_inc(h1_ready.sem, 1)
                act.wait_ge(z1_ready.sem, z1_ready.of(b))
                act.activation(v1[:, 0], dt1[:], ACT.Exp)
                act.activation(v1[:, 1], dt1[:], ACT.Exp, scale=SLOPE)
                act.activation(c1[:], zs1[:], ACT.Exp, scale=-(1.0 - SLOPE)).then_inc(v1_ready.sem, 1)
                act.wait_ge(sumA_made.sem, sumA_made.of(b))
                for g in range(len(GROUPS)):
                    last = copy(sumA[:, tiles(g)], thirds(fp, g, H1 * C1).rearrange("p t (h c) -> p t h c", h=H1))
                last.then_inc(sumA_ready.sem, 1)

            def s1_half(b, n):
                h, half = n // 2, n % 2
                act.wait_ge(s1_spread.sem, s1_spread.of(b, n + 1))
                if h >= 2:
                    act.wait_ge(edges_ready.sem, edges_ready.of(b, (h - 1) * T))
                copy(s1row[:, h % 2, half * HALF:(half + 1) * HALF], fp[:, 0, :]).then_inc(s1_ready.sem, 1)

            def ramp_unit(b, u):
                h, jt, r = u // T, u % T, u // 2
                if r >= R_RING:
                    act.wait_ge(edges_ready.sem, edges_ready.of(b, 2 * (r - R_RING) + 2))
                act.wait_ge(s1_ready.sem, s1_ready.of(b, 2 * h + 2))
                act.activation(ramp[:, r % R_RING, :], s1row[:, h % 2, :], ACT.Relu, bias=tbig1[:, jt, h:h + 1],
                               scale=BIG).then_inc(ramp_ready.sem, 1)

            def layer1_finish(b):
                act.wait_ge(elu_min.sem, elu_min.of(b))
                act.activation(elu[:], elu[:], ACT.Exp).then_inc(elu_exp.sem, 1)

            def layer2(b):
                act.wait_ge(x2_turned.sem, x2_turned.of(b))
                copy(x2T[:], score_bank[0]).then_inc(x2T_ready.sem, 1)

            def layer3_prepare(b):
                act.wait_ge(x3_turned.sem, x3_turned.of(b))
                copy(x3T[:], score_bank[0]).then_inc(x3T_ready.sem, 1)
                act.wait_ge(w3_made.sem, w3_made.of(b))
                copy(w3[:, :, 0:O3], kp[:, 3:5, :].rearrange("p a (b o) -> p (a b) o", o=O3)).then_inc(w3_ready.sem, 1)
                for h in range(H3):
                    act.wait_ge(cut_turned.sem, cut_turned.of(b, 2 * h + 1))
                    copy(cutT[:, h, 0, :], kp[:, 1 + (2 * h) % 4, :].bitcast(BF16)).then_inc(cutT_act.sem, 1)

            def layer3_exp(b, w):
                h = w // T
                act.wait_ge(scores_made.sem, scores_made.of(b, w + 1))
                if w >= P_RING:
                    act.wait_ge(weight3_used.sem, weight3_used.of(b, w - P_RING + 1))
                if w == 0:
                    act.wait_ge(shift_ready.sem, shift_ready.of(b))
                act.activation(weight3[:, w % P_RING, :], score_bank[w % 2], ACT.Exp, bias=shift3[:, h:h + 1],
                               scale=ROOT).then_inc(exp3_ready.sem, 1)

            act.wait_ge(weights_ready, 1)

            def body(parity, f, k):
                if f is not None:
                    adjacency(f, parity)
                    layer0_prepare(f)
                if k is not None:
                    layer2(k)
                    layer3_prepare(k)
                if f is not None:
                    layer1_prepare(f)
                    for n in range(4):
                        s1_half(f, n)
                    ramp_unit(f, 1)
                for s in range(U3 + 1):
                    if k is not None and s < U3:
                        layer3_exp(k, s)
                    if f is not None:
                        if s + 1 < U3:
                            ramp_unit(f, 2 * s + 3)
                        if 1 <= s and s % 4 == 0 and 2 * (s // 4) + 3 < 2 * H1:
                            s1_half(f, 2 * (s // 4) + 2)
                            s1_half(f, 2 * (s // 4) + 3)
                if f is not None:
                    layer1_finish(f)

            schedule(act, body)

        @block.vector
        def _(dve):
            front, back = Steps(dve_front), Steps(dve_back)

            def spread_over(col, width):
                return col.unsqueeze(len(col.shape)).broadcast_to(list(col.shape) + [width])

            def per_tile(row):
                return row.unsqueeze(1).broadcast_to([P, T, D])

            def layernorm(chain, b, y, dst, stat, small, var_ready, rstd_ready, n):
                for t in range(T):
                    last = dve.bn_stats(stat[:, t, :], y[:, t, :])
                last.then_inc(chain.sem, 1)
                dve.wait_ge(chain.sem, chain.step())
                dve.tensor_tensor(small[:, 0, :], stat[:, :, 1], stat[:, :, 4], ALU.add)
                dve.tensor_tensor(small[:, 1, :], stat[:, :, 1], stat[:, :, 4], ALU.subtract)
                dve.tensor_tensor(small[:, 2, :], stat[:, :, 2], stat[:, :, 5], ALU.add).then_inc(chain.sem, 1)
                dve.wait_ge(chain.sem, chain.step())
                dve.tensor_tensor(small[:, 1, :], small[:, 1, :], small[:, 1, :], ALU.mult).then_inc(chain.sem, 1)
                dve.wait_ge(chain.sem, chain.step())
                dve.scalar_tensor_tensor(out=small[:, 3, :], in0=small[:, 1, :], scalar=D / 4.0,
                                         in1=small[:, 2, :], op0=ALU.mult, op1=ALU.add).then_inc(chain.sem, 1)
                dve.wait_ge(chain.sem, chain.step())
                dve.tensor_scalar(small[:, 4, :], small[:, 3, :], 1.0 / D, EPS, ALU.mult, ALU.add) \
                    .then_inc(var_ready.sem, 1)
                dve.tensor_scalar(small[:, 0, :], small[:, 0, :], 0.5, None, ALU.mult).then_inc(chain.sem, 1)
                dve.wait_ge(chain.sem, chain.step())
                dve.wait_ge(rstd_ready.sem, rstd_ready.of(b, n + 1))
                for t in range(T):
                    last = dve.tensor_scalar(dst[:, t, :], y[:, t, :], small[:, 0, t:t + 1], small[:, 5, t:t + 1],
                                             ALU.subtract, ALU.mult)
                return last

            def prepare_weights():
                dve.wait_ge(w_loaded, 160)
                dve.wait_ge(consts_made, 3)
                step = Steps(dve_setup)
                step.begin(0)
                for k, spread_w in ((0, src0), (1, dst0)):
                    dve.tensor_tensor(w_tmp[:], rhs0[:, 0:D], a0_row[:, k, :], ALU.mult).then_inc(step.sem, 1)
                    dve.wait_ge(step.sem, step.step())
                    dve.tensor_reduce(rhs0[:, D + k:D + k + 1], w_tmp[:], AX_X, ALU.add).then_inc(step.sem, 1)
                    dve.wait_ge(step.sem, step.step())
                    dve.tensor_copy(spread_w[:], rhs0[:, D + k:D + k + 1].broadcast_to([P, P]))
                for k in range(2):
                    dve.tensor_tensor(w_tmp[:].rearrange("p (h o) -> p h o", h=H1),
                                      rhs1[:, 0:D].rearrange("p (h o) -> p h o", h=H1),
                                      a1_row[:, :, k * O1:(k + 1) * O1], ALU.mult).then_inc(step.sem, 1)
                    dve.wait_ge(step.sem, step.step())
                    dve.tensor_reduce(rhs1[:, D + k * H1:D + (k + 1) * H1],
                                      w_tmp[:].rearrange("p (h o) -> p h o", h=H1), AX_X, ALU.add).then_inc(step.sem, 1)
                    dve.wait_ge(step.sem, step.step())
                dve.tensor_copy(src1[:], spread_over(rhs1[:, D:D + H1], P))
                dve.tensor_copy(identb[:], ident[:])
                dve.memset(h0[:, :, D:D + 1], 1.0)
                dve.memset(h1[:, :, :, O1:C1], 1.0)
                dve.memset(w3[:, :, O3:C3], 1.0)
                dve.wait_ge(self_turned, 1)
                dve.tensor_copy(rhs2[:, D:2 * D], fp[:, 0, 0:P]).then_inc(weights_ready, 1)

            def adjacency(b, parity):
                for jt in range(1, T, 2):
                    dve.wait_ge(a_turned.sem, a_turned.of(b, jt + 1))
                    dve.tensor_copy(AT[:, parity, jt, :], fp[:, jt % 3, :].bitcast(BF16)).then_inc(at_dve.sem, 1)

            def layer0_prepare(b):
                dve.wait_ge(t0_spread.sem, t0_spread.of(b))
                dve.tensor_reduce(T0[:], fp_pair, AX_X, ALU.max).then_inc(front.sem, 1)
                dve.wait_ge(front.sem, front.step())
                dve.tensor_scalar(T0neg[:], T0[:], -1.0, None, ALU.mult)
                dve.tensor_scalar(T0neg2[:], T0[:], -SLOPE, None, ALU.mult).then_inc(T0_ready.sem, 1)
                dve.wait_ge(s0_spread.sem, s0_spread.of(b))
                dve.tensor_scalar(c0[:], fp_pair, T0[:], 0.0, ALU.add, ALU.max).then_inc(z0_ready.sem, 1)

            def layer0_sum(b, parity):
                dve.wait_ge(c0_ready.sem, c0_ready.of(b))
                dve.wait_ge(h0_ready.sem, h0_ready.of(b))
                dve.wait_ge(at_act.sem, at_act.of(b))
                for jt in range(T):
                    w = weight0[:, jt % P0_RING, :]
                    if jt >= P0_RING:
                        dve.wait_ge(weight0_used.sem, weight0_used.of(b, jt - P0_RING + 1))
                    dve.tensor_scalar(w, c0[:], v0s[:, jt:jt + 1], v0[:, jt:jt + 1], ALU.mult, ALU.max).then_inc(front.sem, 1)
                    dve.wait_ge(front.sem, front.step())
                    dve.tensor_tensor(w, w, AT[:, parity, jt, :], ALU.mult).then_inc(weight0_ready.sem, 1)
                dve.wait_ge(weight0_used.sem, weight0_used.of(b))
                for g in range(len(GROUPS)):
                    last = dve.reciprocal(rec0[:, tiles(g)], thirds(fp, g, D + 1)[:, :, D])
                last.then_inc(front.sem, 1)
                dve.wait_ge(front.sem, front.step())
                for g in range(len(GROUPS)):
                    last = dve.tensor_tensor(yf[:, tiles(g), :], thirds(fp, g, D + 1)[:, :, 0:D],
                                             spread_over(rec0[:, tiles(g)], D), ALU.mult)
                last.then_inc(front.sem, 1)
                dve.wait_ge(front.sem, front.step())
                flat = "p t d -> p (t d)"
                dve.scalar_tensor_tensor(out=yf.rearrange(flat), in0=yf.rearrange(flat), scalar=0.0,
                                         in1=x0.rearrange(flat), op0=ALU.max, op1=ALU.add).then_inc(front.sem, 1)
                dve.wait_ge(front.sem, front.step())
                layernorm(front, b, yf, x1, fstat, fsmall, fvar_ready, frstd_ready, 0).then_inc(x1_ready.sem, 1)

            def layer1_prepare(b):
                dve.wait_ge(st1_ready.sem, st1_ready.of(b))
                dve.tensor_reduce(tmax1[:], st1[:, :, H1:2 * H1].rearrange("p t h -> p h t"), AX_X, ALU.max) \
                    .then_inc(tmax1_ready.sem, 1)
                dve.tensor_scalar(tneg1[:], st1[:, :, H1:2 * H1], -1.0, None, ALU.mult)
                dve.tensor_scalar(tbig1[:], st1[:, :, H1:2 * H1], BIG, None, ALU.mult)
                dve.wait_ge(tmax1_turned.sem, tmax1_turned.of(b))
                dve.tensor_reduce(tcol1[:], fp[0:H1, 0, 0:P], AX_X, ALU.max).then_inc(front.sem, 1)
                dve.wait_ge(front.sem, front.step())
                dve.tensor_scalar(tdiag1[:], ident[0:H1, 0:H1], tcol1[:], None, ALU.mult) \
                    .then_inc(tdiag1_ready.sem, 1)
                dve.wait_ge(T1_spread.sem, T1_spread.of(b))
                dve.tensor_copy(T1[:], fp[:, 1, 0:H1]).then_inc(front.sem, 1)
                dve.wait_ge(front.sem, front.step())
                T1_tiles = T1[:].unsqueeze(1).broadcast_to([P, T, H1])
                dve.tensor_tensor(dt1[:], st1[:, :, H1:2 * H1], T1_tiles, ALU.subtract)
                dve.tensor_tensor(zs1[:], st1[:, :, 0:H1], T1_tiles, ALU.add).then_inc(front.sem, 1)
                dve.wait_ge(front.sem, front.step())
                dve.tensor_scalar(zs1[:], zs1[:], 0.0, None, ALU.max).then_inc(z1_ready.sem, 1)
                dve.wait_ge(v1_ready.sem, v1_ready.of(b))
                dve.wait_ge(h1_ready.sem, h1_ready.of(b))
                flat = "p t h c -> p (t h) c"
                for k in range(2):
                    last = dve.tensor_tensor(vh[:, :, :, k, :].rearrange(flat), h1[:].rearrange(flat),
                                             spread_over(v1[:, k].rearrange("p t h -> p (t h)"), C1), ALU.mult)
                last.then_inc(front.sem, 1)
                dve.wait_ge(front.sem, front.step())
                flat = "p t h a c -> p (t h a) c"
                part = [vh_parts[:, :, :, :, k, :].rearrange(flat) for k in range(PARTS)]
                whole, rest = vh[:].rearrange(flat), vh_rest[:].rearrange(flat)
                dve.tensor_copy(part[0], whole).then_inc(front.sem, 1)
                dve.wait_ge(front.sem, front.step())
                dve.tensor_tensor(rest, whole, part[0], ALU.subtract).then_inc(front.sem, 1)
                dve.wait_ge(front.sem, front.step())
                dve.tensor_copy(part[1], rest).then_inc(front.sem, 1)
                dve.wait_ge(front.sem, front.step())
                dve.tensor_tensor(part[2], rest, part[1], ALU.subtract).then_inc(vh_ready.sem, 1)

            def layer1_unit(b, parity, u):
                h, jt = u // T, u % T
                if u >= B_RING:
                    dve.wait_ge(edges_used.sem, edges_used.of(b, u - B_RING + 1))
                if u % 2:
                    dve.wait_ge(ramp_ready.sem, ramp_ready.of(b, u // 2 + 1))
                    dve.tensor_tensor(edges[:, u % B_RING, :], ramp[:, (u // 2) % R_RING, :], AT[:, parity, jt, :],
                                      ALU.min).then_inc(edges_ready.sem, 1)
                else:
                    dve.wait_ge(s1_ready.sem, s1_ready.of(b, 2 * h + 2))
                    dve.scalar_tensor_tensor(out=edges[:, u % B_RING, :], in0=s1row[:, h % 2, :],
                                             scalar=tneg1[:, jt, h:h + 1], in1=AT[:, parity, jt, :], op0=ALU.is_gt,
                                             op1=ALU.mult).then_inc(edges_ready.sem, 1)

            def layer1_head_out(b, h):
                dve.wait_ge(edges_used.sem, edges_used.of(b, (h + 1) * T))
                for n in range(2):
                    src = fp[:, 1 + n, :].rearrange("p (t c) -> p t c", t=4)[:, :, 0:2 * PARTS * C1]
                    for a in range(2):
                        last = dve.tensor_reduce(
                            sumB[:, 4 * n:4 * n + 4, h, a, :],
                            src[:, :, a * PARTS * C1:(a + 1) * PARTS * C1].rearrange("p t (k c) -> p t c k", k=PARTS),
                            AX_X, ALU.add)
                last.then_inc(sumB_ready.sem, 1)

            def layer1_finish(b, parity):
                dve.wait_ge(sumA_ready.sem, sumA_ready.of(b))
                dve.wait_ge(sumB_ready.sem, sumB_ready.of(b))
                flat = "p t h c -> p (t h) c"
                A = sumA[:].rearrange(flat)
                Bv, Bs = (sumB[:, :, :, a, :].rearrange(flat) for a in range(2))
                dve.tensor_tensor(A, A, Bs, ALU.subtract).then_inc(front.sem, 1)
                dve.wait_ge(front.sem, front.step())
                dve.tensor_tensor(A, A, spread_over(c1[:].rearrange("p t h -> p (t h)"), C1), ALU.mult).then_inc(front.sem, 1)
                dve.wait_ge(front.sem, front.step())
                dve.tensor_tensor(A, A, Bv, ALU.add).then_inc(front.sem, 1)
                dve.wait_ge(front.sem, front.step())
                dve.reciprocal(rec1[:].rearrange("p t h -> p (t h)"), A[:, :, O1]).then_inc(front.sem, 1)
                dve.wait_ge(front.sem, front.step())
                o = yf.rearrange("p t (h o) -> p (t h) o", h=H1)
                dve.tensor_tensor(o, A[:, :, 0:O1],
                                  spread_over(rec1[:].rearrange("p t h -> p (t h)"), O1), ALU.mult).then_inc(front.sem, 1)
                dve.wait_ge(front.sem, front.step())
                dve.tensor_scalar(elu[:], yf[:], 0.0, None, ALU.min).then_inc(elu_min.sem, 1)
                flat = "p t d -> p (t d)"
                dve.scalar_tensor_tensor(out=yf.rearrange(flat), in0=yf.rearrange(flat), scalar=0.0,
                                         in1=x1.rearrange(flat), op0=ALU.max, op1=ALU.add).then_inc(front.sem, 1)
                dve.wait_ge(front.sem, front.step())
                dve.wait_ge(elu_exp.sem, elu_exp.of(b))
                dve.scalar_tensor_tensor(out=yf.rearrange(flat), in0=elu.rearrange(flat), scalar=-1.0,
                                         in1=yf.rearrange(flat), op0=ALU.add, op1=ALU.add).then_inc(front.sem, 1)
                dve.wait_ge(front.sem, front.step())
                layernorm(front, b, yf, x2[:, parity], fstat, fsmall, fvar_ready, frstd_ready, 1) \
                    .then_inc(x2_ready.sem, 1)

            def layer2(b, parity):
                dve.wait_ge(y2_made.sem, y2_made.of(b))
                src = kp[:, 1:5, :].rearrange("p a (n c) -> p (a n) c", n=2)
                dve.memset(y2_hi[:, :, D:D + 1], 1.0)
                dve.tensor_copy(y2_hi[:, :, 0:D], src[:, :, 0:D]).then_inc(back.sem, 1)
                dve.wait_ge(back.sem, back.step())
                dve.tensor_tensor(rest2[:], src[:, :, 0:D], y2_hi[:, :, 0:D], ALU.subtract).then_inc(back.sem, 1)
                dve.wait_ge(back.sem, back.step())
                dve.tensor_tensor(self2[:], src[:, :, D:2 * D], per_tile(bias2[:]), ALU.add)
                dve.tensor_copy(y2_lo[:, :, 0, :], rest2[:]).then_inc(back.sem, 1)
                dve.wait_ge(back.sem, back.step())
                dve.tensor_tensor(y2_lo[:, :, 1, :], rest2[:], y2_lo[:, :, 0, :], ALU.subtract) \
                    .then_inc(y2_ready.sem, 1)
                dve.wait_ge(sum2_made.sem, sum2_made.of(b))
                for g in range(len(GROUPS)):
                    last = dve.tensor_scalar(deg2[:, tiles(g)], thirds(kp, g, D + 1)[:, :, D], 1e-6, None, ALU.max)
                last.then_inc(back.sem, 1)
                dve.wait_ge(back.sem, back.step())
                dve.reciprocal(deg2[:], deg2[:]).then_inc(back.sem, 1)
                dve.wait_ge(back.sem, back.step())
                if stored.any_before(b):
                    dve.wait_ge(stored.sem, stored.before(b))
                for g in range(len(GROUPS)):
                    for n, t in enumerate(GROUPS[g]):
                        last = dve.scalar_tensor_tensor(out=yb[:, t, :], in0=thirds(kp, g, D + 1)[:, n, 0:D],
                                                        scalar=deg2[:, t:t + 1], in1=self2[:, t, :], op0=ALU.mult,
                                                        op1=ALU.add)
                last.then_inc(back.sem, 1)
                dve.wait_ge(back.sem, back.step())
                layernorm(back, b, yb, yb, bstat, bsmall, bvar_ready, brstd_ready, 0).then_inc(back.sem, 1)
                dve.wait_ge(back.sem, back.step())
                dve.tensor_tensor(yb[:], yb[:], per_tile(gamma2[:]), ALU.mult).then_inc(back.sem, 1)
                dve.wait_ge(back.sem, back.step())
                dve.tensor_tensor(yb[:], yb[:], per_tile(beta2[:]), ALU.add).then_inc(back.sem, 1)
                dve.wait_ge(back.sem, back.step())
                flat = "p t d -> p (t d)"
                dve.scalar_tensor_tensor(out=yb.rearrange(flat), in0=yb.rearrange(flat), scalar=0.0,
                                         in1=x2[:, parity].rearrange(flat), op0=ALU.max, op1=ALU.add).then_inc(back.sem, 1)
                dve.wait_ge(back.sem, back.step())
                layernorm(back, b, yb, x3, bstat, bsmall, bvar_ready, brstd_ready, 1).then_inc(x3_ready.sem, 1)

            def layer3_prepare(b):
                dve.wait_ge(w3_ready.sem, w3_ready.of(b))
                W = w3[:, :, 0:O3]
                dve.tensor_copy(cutA[:, :, 2, :], W).then_inc(back.sem, 1)
                dve.wait_ge(back.sem, back.step())
                dve.tensor_tensor(rest3[:], W, cutA[:, :, 2, :], ALU.subtract)
                dve.tensor_copy(cutB[:, :, 0:3, :],
                                cutA[:, :, 2, :].unsqueeze(2).broadcast_to([P, T * H3, 3, O3])).then_inc(back.sem, 1)
                dve.wait_ge(back.sem, back.step())
                dve.tensor_copy(cutA[:, :, 0, :], rest3[:]).then_inc(back.sem, 1)
                dve.wait_ge(back.sem, back.step())
                dve.tensor_copy(cutA[:, :, 3, :], cutA[:, :, 0, :])
                dve.tensor_copy(cutB[:, :, 3, :], cutA[:, :, 0, :])
                dve.tensor_tensor(cutA[:, :, 1, :], rest3[:], cutA[:, :, 0, :], ALU.subtract).then_inc(back.sem, 1)
                dve.wait_ge(back.sem, back.step())
                dve.tensor_tensor(rest3[:], W, W, ALU.mult).then_inc(back.sem, 1)
                dve.wait_ge(back.sem, back.step())
                dve.tensor_reduce(q3[:], rest3[:], AX_X, ALU.add).then_inc(back.sem, 1)
                dve.wait_ge(back.sem, back.step())
                dve.tensor_reduce(qmax3[:], q3[:].rearrange("p (t h) -> p h t", h=H3), AX_X, ALU.max) \
                    .then_inc(qmax_ready.sem, 1)
                dve.wait_ge(qmax_turned.sem, qmax_turned.of(b))
                dve.tensor_reduce(qcol3[:], kp[0:H3, 0, 0:P], AX_X, ALU.max).then_inc(back.sem, 1)
                dve.wait_ge(back.sem, back.step())
                dve.tensor_scalar(qdiag3[:], ident[0:H3, 0:H3], qcol3[:], None, ALU.mult) \
                    .then_inc(qdiag_ready.sem, 1)
                dve.wait_ge(q_spread.sem, q_spread.of(b))
                dve.tensor_scalar(shift3[:], kp[:, 0, P:P + H3], -ROOT, None, ALU.mult).then_inc(shift_ready.sem, 1)
                for h in range(H3):
                    dve.wait_ge(cut_turned.sem, cut_turned.of(b, 2 * h + 2))
                    dve.tensor_copy(cutT[:, h, 1, :], kp[:, 1 + (2 * h + 1) % 4, :].bitcast(BF16)) \
                        .then_inc(cutT_dve.sem, 1)

            def layer3_mask(b, parity, w):
                jt = w % T
                dve.wait_ge(exp3_ready.sem, exp3_ready.of(b, w + 1))
                tile = weight3[:, w % P_RING, :]
                dve.tensor_tensor(tile, tile, AT[:, parity, jt, :], ALU.mult).then_inc(weight3_ready.sem, 1)

            def layer3_head_out(b, h):
                dve.wait_ge(weight3_used.sem, weight3_used.of(b, (h + 1) * T))
                src = kp[:, 0, 0:T * C3].rearrange("p (t c) -> p t c", t=T)
                dve.reciprocal(rec3[:, h, :], src[:, :, O3]).then_inc(back.sem, 1)
                dve.wait_ge(back.sem, back.step())
                dve.tensor_tensor(yb[:, :, h * O3:(h + 1) * O3], src[:, :, 0:O3], spread_over(rec3[:, h, :], O3),
                                  ALU.mult).then_inc(sum3_ready.sem, 1)

            def layer3_finish(b):
                dve.wait_ge(sum3_ready.sem, sum3_ready.of(b))
                dve.tensor_tensor(yb[:], yb[:], x3[:], ALU.add).then_inc(back.sem, 1)
                dve.wait_ge(back.sem, back.step())
                layernorm(back, b, yb, x4, bstat, bsmall, bvar_ready, brstd_ready, 2).then_inc(x4_ready.sem, 1)

            prepare_weights()

            def body(parity, f, k):
                if f is not None:
                    front.begin(f)
                    adjacency(f, parity)
                    layer0_prepare(f)
                if k is not None:
                    back.begin(k)
                    layer2(k, 1 - parity)
                if f is not None:
                    layer0_sum(f, parity)
                if k is not None:
                    layer3_prepare(k)
                if f is not None:
                    layer1_prepare(f)
                for s in range(U3 + 3):
                    if f is not None and s < U3:
                        layer1_unit(f, parity, 2 * s)
                        layer1_unit(f, parity, 2 * s + 1)
                    if k is not None and 1 <= s <= U3:
                        layer3_mask(k, 1 - parity, s - 1)
                    if f is not None and s % 4 == 1 and s > 1:
                        layer1_head_out(f, s // 4 - 1)
                    if k is not None and s >= 10 and s % 8 == 2:
                        layer3_head_out(k, s // 8 - 1)
                if f is not None:
                    layer1_finish(f, parity)
                if k is not None:
                    layer3_finish(k)

            schedule(dve, body)


_INS = ["x", "adj", "L0_gnn_W", "L0_gnn_a", "L1_gnn_W", "L1_gnn_a", "L2_gnn_rel_weights", "L2_gnn_self_w",
        "L2_gnn_self_b", "L2_gnn_ln_gamma", "L2_gnn_ln_beta", "L3_gnn_W"]


def kernel(**inputs):
    import numpy as _np
    import concourse.bacc as _bacc
    from concourse import mybir as _mybir
    from concourse.bass_utils import run_bass_kernel_spmd as _run

    nc = _bacc.Bacc("TRN2", target_bir_lowering=False, num_devices=1)
    arrays, args = {}, []
    for name in _INS:
        a = _np.ascontiguousarray(inputs[name])
        arrays[f"in_{name}_dram"] = a
        args.append(nc.dram_tensor(f"in_{name}_dram", a.shape, _mybir.dt.from_np(a.dtype), kind="ExternalInput").ap())
    shape = tuple(inputs["x"].shape)
    args.append(nc.dram_tensor("out_0_dram", shape, _mybir.dt.float32, kind="ExternalOutput").ap())
    graph_stack(nc, *args)
    r = _run(nc, [arrays], core_ids=[0])
    return r.results[0]["out_0_dram"]
```

```python
from contextlib import ExitStack

import concourse.bass as bass
from concourse import mybir

ALU = mybir.AluOpType
ACT = mybir.ActivationFunctionType
AX_X = mybir.AxisListType.X
BF16 = mybir.dt.bfloat16
F32 = mybir.dt.float32

P = 128
SLOPE = 0.2
EPS = 1e-5
BIG = 2.0 ** 100
PARTS = 3


class Signal:

    def __init__(self, sem, per_batch):
        self.sem, self.per_batch = sem, per_batch

    def of(self, b, k=None):
        return b * self.per_batch + (self.per_batch if k is None else k)

    def any_before(self, b):
        return not (isinstance(b, int) and b <= 0)

    def before(self, b):
        return b * self.per_batch


class Steps:

    def __init__(self, sem, per_batch=None):
        self.sem, self.count, self.per_batch = sem, 0, per_batch

    def begin(self, b):
        if self.count and self.per_batch is None:
            self.per_batch = self.count
        assert self.count in (0, self.per_batch), (self.count, self.per_batch)
        self.b, self.count = b, 0

    def step(self):
        self.count += 1
        return self.count if self.per_batch is None else self.b * self.per_batch + self.count


def graph_stack(nc, x, adj, L0_gnn_W, L0_gnn_a, L1_gnn_W, L1_gnn_a, L2_gnn_rel_weights, L2_gnn_self_w,
                L2_gnn_self_b, L2_gnn_ln_gamma, L2_gnn_ln_beta, L3_gnn_W, out):
    NB, N, D = x.shape
    T = N // P
    H1, _, O1 = L1_gnn_W.shape
    H3, _, O3 = L3_gnn_W.shape
    HALF = N // 2
    C1 = O1 + 1
    C3 = O3 + 1
    U1, U3 = H1 * T, H3 * T
    PER = 3
    GROUPS = [range(g, min(g + PER, T)) for g in range(0, T, PER)]
    ROOT = float(O3) ** -0.5
    B_RING, P_RING, P0_RING, R_RING = 6, 4, 3, 3
    PV_LAG = 3
    SPREAD = 96
    nc.disable_value_cache = True
    RAMPS = [u for u in range(U1) if u % 2 or u % 8 == 2]
    POOL_MASKS = [w for w in range(U3) if w % 4 == 3]
    DVE_MASKS = [w for w in range(U3) if w not in POOL_MASKS]
    assert D == P and H1 * O1 == D and H3 * O3 == D and N == 1024 and NB % 2 == 0

    with ExitStack() as ctx:
        def sb(name, shape, dt=F32):
            return ctx.enter_context(nc.sbuf_tensor(name, shape, dt))

        def signal(name, per_batch):
            return Signal(ctx.enter_context(nc.semaphore(name)), per_batch)

        def sem(name):
            return ctx.enter_context(nc.semaphore(name))

        ident = sb("ident", [P, P])
        identb = sb("identb", [P, P], BF16)
        ones = sb("ones", [P, P])
        half_neg = sb("half_neg", [P, T])
        a0_row = sb("a0_row", [P, 2, D])
        a1_row = sb("a1_row", [P, H1, 2 * O1])
        w_tmp = sb("w_tmp", [P, D])
        rhs0 = sb("rhs0", [P, D + 2])
        src0 = sb("src0", [P, P])
        dst0 = sb("dst0", [P, P])
        rhs1 = sb("rhs1", [P, D + 2 * H1])
        pick1 = sb("pick1", [SPREAD, H1, P], BF16)
        self_w = sb("self_w", [P, D])
        rhs2 = sb("rhs2", [P, 2 * D])
        bias2 = sb("bias2", [P, D])
        gamma2 = sb("gamma2", [P, D])
        beta2 = sb("beta2", [P, D])
        rhs3 = sb("rhs3", [P, D])

        AT = sb("AT", [P, 2, T, N], BF16)
        x2 = sb("x2", [P, 2, T, D])

        A_rows = sb("A_rows", [P, T, N], BF16)
        x0 = sb("x0", [P, T, D])
        T0 = sb("T0", [P, 1])
        T0neg = sb("T0neg", [P, 1])
        T0neg2 = sb("T0neg2", [P, 1])
        v0 = sb("v0", [P, T])
        v0s = sb("v0s", [P, T])
        h0 = sb("h0", [P, T, D])
        weight0 = sb("weight0", [P, P0_RING, N])
        rec0 = sb("rec0", [P, T])
        yf = sb("yf", [P, T, D])
        x1 = sb("x1", [P, T, D])
        h1 = sb("h1", [P, T, H1, C1])
        st1 = sb("st1", [P, T, 2 * H1])
        tmax1 = sb("tmax1", [P, H1])
        tcol1 = sb("tcol1", [H1, 1])
        tdiag1 = sb("tdiag1", [H1, H1])
        T1 = sb("T1", [P, H1])
        tneg1 = sb("tneg1", [P, T, H1])
        tbig1 = sb("tbig1", [P, T, H1])
        dt1 = sb("dt1", [P, T, H1])
        zs1 = sb("zs1", [P, T, H1])
        v1 = sb("v1", [P, 2, T, H1])
        c1 = sb("c1", [P, T, H1])
        vh = sb("vh", [P, T, H1, 2, C1])
        vh_rest = sb("vh_rest", [P, T, H1, 2, C1])
        vh_parts = sb("vh_parts", [P, T, H1, 2, PARTS, C1], BF16)
        s1row = sb("s1row", [P, 2, N])
        s1_parts = sb("s1_parts", [SPREAD, N], BF16)
        ramp = sb("ramp", [P, R_RING, N], BF16)
        rec1 = sb("rec1", [P, T, H1])
        xfT = sb("xfT", [P, N])
        x0T = x1T = xfT
        edges = weight0[:].rearrange("p r n -> p (r n)").bitcast(BF16).rearrange(
            "p (r n) -> p r n", n=N)
        elu = weight0[:, 0, :].rearrange("p (t d) -> p t d", t=T)
        c0 = s1row[:, 0, :]
        weight0_sum = s1row[:, 1, :]
        num0T = xfT
        s1_rest = weight0[0:H1, 1, :]
        s1_mid = weight0[0:H1, 2, :].bitcast(BF16)[:, 0:N]
        sumB = vh
        sumA = vh_rest[:, :, :, 0, :]
        fstat = sb("fstat", [P, T, 6])
        fsmall = sb("fsmall", [P, 8, T])

        deg2 = sb("deg2", [P, T])
        yb = sb("yb", [P, T, D])
        x3 = sb("x3", [P, T, D])
        w3 = sb("w3", [P, T * H3, C3])
        cutT = sb("cutT", [P, H3, 2, N], BF16)
        q3 = sb("q3", [P, T * H3])
        qmax3 = sb("qmax3", [P, H3])
        qcol3 = sb("qcol3", [H3, 1])
        qdiag3 = sb("qdiag3", [H3, H3])
        shift3 = sb("shift3", [P, H3])
        weight3 = sb("weight3", [P, P_RING, N])
        rec3 = sb("rec3", [P, T, H3])
        xbT = sb("xbT", [P, N])
        x2T = x3T = xbT
        x4 = yb
        cutT_all = cutT[:].rearrange("p h a n -> p (h a n)")
        y2_hi = cutT_all[:, 0:T * (D + 1)].rearrange("p (t d) -> p t d", t=T)
        y2_lo = cutT_all[:, T * (D + 1):T * (3 * D + 1)].rearrange(
            "p (t k d) -> p t k d", t=T, k=2)
        self2 = cutT_all[:, 4 * N:6 * N].bitcast(F32).rearrange("p (t d) -> p t d", t=T)
        rest2 = cutT_all[:, 6 * N:8 * N].bitcast(F32).rearrange("p (t d) -> p t d", t=T)
        rest3 = rest2.rearrange("p t (h o) -> p (t h) o", h=H3)
        ring3 = weight3[:].rearrange("p r n -> p (r n)").bitcast(BF16).rearrange(
            "p (w t k o) -> p w t k o", w=2, t=T * H3, k=4)
        cutA, cutB = ring3[:, 0], ring3[:, 1]
        o3T = cutT[0:C3].rearrange("p h a n -> p (h a n)").bitcast(F32)
        bstat = sb("bstat", [P, T, 6])
        bsmall = sb("bsmall", [P, 8, T])

        fp = ctx.enter_context(nc.psum_tensor("fp", [P, 3, HALF], F32))
        kp = ctx.enter_context(nc.psum_tensor("kp", [P, 5, HALF], F32))
        fp_pair = fp[:, 1:3, :].rearrange("p a b -> p (a b)")
        kp_pair = kp[:, 0:2, :].rearrange("p a b -> p (a b)")

        def thirds(psum, g, width):
            n = len(GROUPS[g])
            return psum[:, g, 0:n * width].rearrange("p (t c) -> p t c", t=n)

        def tiles(g):
            return slice(GROUPS[g][0], GROUPS[g][-1] + 1)

        w_loaded = sem("w_loaded")
        consts_made = sem("consts_made")
        self_turned = sem("self_turned")
        weights_ready = sem("weights_ready")
        turnstile = sem("turnstile")
        a_loaded = signal("a_loaded", 16)
        x_loaded = signal("x_loaded", 16)
        a_turned = signal("a_turned", T)
        at_ready = signal("at_ready", T)
        x0_turned = signal("x0_turned", 1)
        x0T_ready = signal("x0T_ready", 1)
        t0_spread = signal("t0_spread", 1)
        T0_ready = signal("T0_ready", 1)
        s0_spread = signal("s0_spread", 1)
        z0_ready = signal("z0_ready", 1)
        c0_ready = signal("c0_ready", 1)
        h0_made = signal("h0_made", 1)
        h0_ready = signal("h0_ready", 1)
        weight0_ready = signal("weight0_ready", T)
        weight0_used = signal("weight0_used", T)
        weight0_added = signal("weight0_added", T - 1)
        den0_made = signal("den0_made", 1)
        num0T_ready = signal("num0T_ready", 1)
        num0_turned = signal("num0_turned", 1)
        x1_ready = signal("x1_ready", 1)
        x1_turned = signal("x1_turned", 1)
        x1T_ready = signal("x1T_ready", 1)
        h1_made = signal("h1_made", 1)
        h1_ready = signal("h1_ready", 1)
        st1_ready = signal("st1_ready", 1)
        tmax1_ready = signal("tmax1_ready", 1)
        tmax1_turned = signal("tmax1_turned", 1)
        tdiag1_ready = signal("tdiag1_ready", 1)
        T1_spread = signal("T1_spread", 1)
        z1_ready = signal("z1_ready", 1)
        v1_ready = signal("v1_ready", 1)
        vh_whole = signal("vh_whole", 1)
        vh_first = signal("vh_first", 1)
        vh_rested = signal("vh_rested", 1)
        vh_second = signal("vh_second", 1)
        vh_ready = signal("vh_ready", 1)
        s1_made = signal("s1_made", 1)
        s1_first = signal("s1_first", 1)
        s1_cut = signal("s1_cut", 1)
        sumA_made = signal("sumA_made", 1)
        sumA_ready = signal("sumA_ready", 1)
        s1_spread = signal("s1_spread", 2 * H1)
        s1_ready = signal("s1_ready", 2 * H1)
        ramp_ready = signal("ramp_ready", len(RAMPS))
        edges_ready = signal("edges_ready", U1)
        edges_used = signal("edges_used", U1)
        sumB_ready = signal("sumB_ready", H1)
        elu_min = signal("elu_min", 1)
        elu_exp = signal("elu_exp", 1)
        x2_ready = signal("x2_ready", 1)
        fvar_ready = signal("fvar_ready", 2)
        frstd_ready = signal("frstd_ready", 2)
        x2_turned = signal("x2_turned", 1)
        x2T_ready = signal("x2T_ready", 1)
        y2_made = signal("y2_made", 1)
        y2_ready = signal("y2_ready", 1)
        sum2_made = signal("sum2_made", 1)
        normed2 = signal("normed2", 1)
        bvar_ready = signal("bvar_ready", 3)
        brstd_ready = signal("brstd_ready", 3)
        x3_ready = signal("x3_ready", 1)
        x3_turned = signal("x3_turned", 1)
        x3T_ready = signal("x3T_ready", 1)
        w3_made = signal("w3_made", 1)
        w3_ready = signal("w3_ready", 1)
        qmax_ready = signal("qmax_ready", 1)
        qmax_turned = signal("qmax_turned", 1)
        qdiag_ready = signal("qdiag_ready", 1)
        q_spread = signal("q_spread", 1)
        shift_ready = signal("shift_ready", 1)
        cut_turned = signal("cut_turned", 2 * H3)
        cutT_act = signal("cutT_act", H3)
        cutT_dve = signal("cutT_dve", H3)
        scores_made = signal("scores_made", 2 * U3)
        exp3_ready = signal("exp3_ready", 2 * U3)
        masked_dve = signal("masked_dve", U3 - len(POOL_MASKS))
        masked_pool = signal("masked_pool", len(POOL_MASKS))
        weight3_used = signal("weight3_used", U3)
        sum3_ready = signal("sum3_ready", H3)
        sum3_turned = signal("sum3_turned", 1)
        o3_ready = signal("o3_ready", 1)
        y2_first = signal("y2_first", 1)
        x4_ready = signal("x4_ready", 1)
        stored = signal("stored", 16)
        dve_setup = sem("dve_setup")
        pool_front = sem("pool_front")
        pool_back = sem("pool_back")
        pool_front_last = sem("pool_front_last")
        pool_back_last = sem("pool_back_last")
        dve_front_last = sem("dve_front_last")
        dve_back_last = sem("dve_back_last")
        dve_front = sem("dve_front")
        dve_back = sem("dve_back")

        block = ctx.enter_context(nc.Block())

        def schedule(eng, body):
            body(0, 0, None, None)
            body(1, 1, 0, None)
            with eng.Fori(2, NB - 1, 2) as i:
                body(0, i, i - 1, i - 2)
                body(1, i + 1, i, i - 1)
            body(0, None, NB - 1, NB - 2)
            body(1, None, None, NB - 1)

        def rows(dram, b):
            return dram[bass.ds(b, 1)].rearrange("b (t p) d -> p (b t) d", p=P)

        @block.sync
        def _(sp):
            loads = [
                (rhs0[:, 0:D], L0_gnn_W),
                (a0_row[:], L0_gnn_a.rearrange("(k u) o -> o k u", k=2).broadcast_to([P, 2, D])),
                (rhs1[:, 0:D].rearrange("p (h o) -> p h o", h=H1), L1_gnn_W.rearrange("h f o -> f h o")),
                (a1_row[:], L1_gnn_a.rearrange("h k o -> o h k").broadcast_to([P, H1, 2 * O1])),
                (rhs2[:, 0:D], L2_gnn_rel_weights[1]),
                (self_w[:], L2_gnn_self_w),
                (bias2[:], L2_gnn_self_b.rearrange("(a d) -> a d", a=1).broadcast_to([P, D])),
                (gamma2[:], L2_gnn_ln_gamma.rearrange("(a d) -> a d", a=1).broadcast_to([P, D])),
                (beta2[:], L2_gnn_ln_beta.rearrange("(a d) -> a d", a=1).broadcast_to([P, D])),
                (rhs3[:].rearrange("p (h o) -> p h o", h=H3), L3_gnn_W.rearrange("h f o -> f h o")),
            ]
            for dst, src in loads:
                sp.dma_start(dst, src).then_inc(w_loaded, 16)

            def body(parity, f, k, m):
                if f is not None:
                    if x1_ready.any_before(f):
                        sp.wait_ge(x1_ready.sem, x1_ready.before(f))
                    sp.sem_inc(turnstile, 1)
                    sp.dma_start(x0[:], rows(x, f)).then_inc(x_loaded.sem, 16)
                if m is not None:
                    sp.wait_ge(x4_ready.sem, x4_ready.of(m))
                    sp.sem_inc(turnstile, 1)
                    sp.dma_start(rows(out, m), x4[:]).then_inc(stored.sem, 16)

            schedule(sp, body)
            sp.wait_ge(stored.sem, stored.of(NB - 1))

        @block.gpsimd
        def _(pool):
            pool.memset(ones[:], 1.0).then_inc(consts_made, 1)
            pool.memset(half_neg[:], -0.5).then_inc(consts_made, 1)
            pool.wait_ge(consts_made, 2)
            pool.affine_select(out=ident[:], in_=ones[:], compare_op=ALU.is_equal, fill=0.0, base=0,
                               pattern=[[-1, P]], channel_multiplier=1).then_inc(consts_made, 1)

            front, back = Steps(pool_front), Steps(pool_back)
            front_last, back_last = Steps(pool_front_last), Steps(pool_back_last, 1)

            def rstd(step, var_ready, rstd_ready, small, b, n):
                pool.wait_ge(var_ready.sem, var_ready.of(b, n + 1))
                pool.tensor_tensor(small[:, 5, :], small[:, 4, :], half_neg[:], ALU.pow).then_inc(step.sem, 1)
                pool.wait_ge(step.sem, step.step())
                pool.tensor_tensor(small[:, 6, :], small[:, 0, :], small[:, 5, :], ALU.mult) \
                    .then_inc(rstd_ready.sem, 1)

            def add_weight0(b, jt):
                pool.wait_ge(weight0_ready.sem, weight0_ready.of(b, jt + 1))
                so_far = weight0[:, 0, :] if jt == 1 else weight0_sum
                if jt > 1:
                    pool.wait_ge(weight0_added.sem, weight0_added.of(b, jt - 1))
                pool.tensor_tensor(weight0_sum, so_far, weight0[:, jt % P0_RING, :], ALU.add) \
                    .then_inc(weight0_added.sem, 1)

            def layer3_mask(b, parity, w):
                pool.wait_ge(exp3_ready.sem, exp3_ready.of(b, 2 * w + 2))
                tile = weight3[:, w % P_RING, :]
                pool.tensor_tensor(tile, tile, AT[:, parity, w % T, :], ALU.mult).then_inc(masked_pool.sem, 1)

            def body(parity, f, k, m):
                if f is not None:
                    if a_turned.any_before(f):
                        pool.wait_ge(a_turned.sem, a_turned.before(f))
                    pool.sem_inc(turnstile, 1)
                    pool.dma_start(A_rows[:], adj[bass.ds(f, 1)].rearrange("b (t p) n -> p (b t) n", p=P)) \
                        .then_inc(a_loaded.sem, 16)
                    front.begin(f)
                if k is not None:
                    back.begin(k)
                    front_last.begin(k)
                    rstd(front_last, fvar_ready, frstd_ready, fsmall, k, 1)
                if m is not None:
                    back_last.begin(m)
                    rstd(back_last, bvar_ready, brstd_ready, bsmall, m, 2)
                if f is not None:
                    add_weight0(f, 1)
                    add_weight0(f, 2)
                if k is not None:
                    rstd(back, bvar_ready, brstd_ready, bsmall, k, 0)
                if f is not None:
                    for jt in range(3, 6):
                        add_weight0(f, jt)
                if k is not None:
                    rstd(back, bvar_ready, brstd_ready, bsmall, k, 1)
                if f is not None:
                    for jt in range(6, T):
                        add_weight0(f, jt)
                    rstd(front, fvar_ready, frstd_ready, fsmall, f, 0)
                if k is not None:
                    for w in POOL_MASKS:
                        layer3_mask(k, 1 - parity, w)

            schedule(pool, body)

        @block.tensor
        def _(pe):
            def turn_rows(src, dst, done):
                for t in range(T):
                    last = pe.transpose(dst[:, t * P:(t + 1) * P], src[:, t, :], ident[:])
                last.then_inc(done.sem, 1)

            def project(xT, rhs, width, dst, done):
                for g in range(len(GROUPS)):
                    for n, t in enumerate(GROUPS[g]):
                        last = pe.matmul(dst[:, g, n * width:(n + 1) * width], xT[:, t * P:(t + 1) * P], rhs,
                                         start=True, stop=True)
                last.then_inc(done.sem, 1)

            def turn_adjacency_tile(b, jt):
                if jt == 0:
                    pe.wait_ge(a_loaded.sem, a_loaded.of(b))
                    if sumB_ready.any_before(b):
                        pe.wait_ge(sumB_ready.sem, sumB_ready.before(b))
                if jt >= 3:
                    pe.wait_ge(at_ready.sem, at_ready.of(b, jt - 2))
                dst = fp[:, jt % 3, :].bitcast(BF16)
                for t in range(T):
                    last = pe.transpose(dst[:, t * P:(t + 1) * P], A_rows[:, t, jt * P:(jt + 1) * P], identb[:])
                last.then_inc(a_turned.sem, 1)

            def spread(lhsT, rhs, dst):
                for n in range(2):
                    last = pe.matmul(dst[:, n * HALF:(n + 1) * HALF], lhsT, rhs[:, n * HALF:(n + 1) * HALF],
                                     start=True, stop=True)
                return last

            def layer0_turn(b):
                pe.wait_ge(x_loaded.sem, x_loaded.of(b))
                pe.wait_ge(at_ready.sem, at_ready.of(b))
                turn_rows(x0, fp_pair, x0_turned)
                pe.wait_ge(x0T_ready.sem, x0T_ready.of(b))
                spread(dst0[:], x0T, fp_pair).then_inc(t0_spread.sem, 1)

            def layer0_project(b):
                pe.wait_ge(T0_ready.sem, T0_ready.of(b))
                spread(src0[:], x0T, fp_pair).then_inc(s0_spread.sem, 1)
                pe.wait_ge(z0_ready.sem, z0_ready.of(b))
                project(x0T, rhs0[:], D + 2, fp, h0_made)

            def layer0_unit(b, jt):
                if jt == 0:
                    pe.wait_ge(h0_ready.sem, h0_ready.of(b))
                pe.wait_ge(weight0_ready.sem, weight0_ready.of(b, jt + 1))
                for n in range(2):
                    last = pe.matmul(fp[:, 1 + n, :], h0[:, jt, :], weight0[:, jt % P0_RING, n * HALF:(n + 1) * HALF],
                                     start=(jt == 0), stop=(jt == T - 1))
                last.then_inc(weight0_used.sem, 1)

            def layer0_finish(b):
                pe.wait_ge(num0T_ready.sem, num0T_ready.of(b))
                for t in range(T):
                    last = pe.transpose(fp_pair[:, t * P:(t + 1) * P], num0T[:, t * P:(t + 1) * P], ident[:])
                last.then_inc(num0_turned.sem, 1)
                pe.wait_ge(weight0_added.sem, weight0_added.of(b))
                for t in range(T):
                    last = pe.matmul(fp[:, 0, t:t + 1], weight0_sum[:, t * P:(t + 1) * P], ones[:, 0:1],
                                     start=True, stop=True)
                last.then_inc(den0_made.sem, 1)

            def layer1_turn(b):
                pe.wait_ge(x1_ready.sem, x1_ready.of(b))
                turn_rows(x1, fp_pair, x1_turned)
                pe.wait_ge(x1T_ready.sem, x1T_ready.of(b))
                project(x1T, rhs1[:], D + 2 * H1, fp, h1_made)
                pe.wait_ge(h1_ready.sem, h1_ready.of(b))
                for n in range(2):
                    last = pe.matmul(fp[0:H1, 1 + n, :], rhs1[:, D:D + H1], x1T[:, n * HALF:(n + 1) * HALF],
                                     start=True, stop=True)
                last.then_inc(s1_made.sem, 1)
                pe.wait_ge(tmax1_ready.sem, tmax1_ready.of(b))
                pe.transpose(fp[0:H1, 0, 0:P], tmax1[:], ident[:]).then_inc(tmax1_turned.sem, 1)
                pe.wait_ge(tdiag1_ready.sem, tdiag1_ready.of(b))
                pe.matmul(fp[:, 0, P:P + H1], ones[0:H1, :], tdiag1[:], start=True, stop=True) \
                    .then_inc(T1_spread.sem, 1)

            def layer1_sum_all(b, parity):
                pe.wait_ge(s1_cut.sem, s1_cut.of(b))
                pe.wait_ge(vh_ready.sem, vh_ready.of(b))
                for g in range(len(GROUPS)):
                    for n, t in enumerate(GROUPS[g]):
                        for jt in range(T):
                            for k in range(PARTS):
                                last = pe.matmul(fp[:, g, n * H1 * C1:(n + 1) * H1 * C1].rearrange(
                                                     "p (h c) -> p h c", h=H1),
                                                 AT[:, parity, jt, t * P:(t + 1) * P], vh_parts[:, jt, :, 1, k, :],
                                                 start=(jt == 0 and k == 0), stop=(jt == T - 1 and k == PARTS - 1))
                last.then_inc(sumA_made.sem, 1)
                pe.wait_ge(sumA_ready.sem, sumA_ready.of(b))

            def spread_s1(b, n):
                if n:
                    pe.wait_ge(s1_ready.sem, s1_ready.of(b, n))
                h, half = n // 2, n % 2
                pe.matmul(fp[:, 0, :], pick1[:, h, :], s1_parts[:, half * HALF:(half + 1) * HALF],
                          start=True, stop=True).then_inc(s1_spread.sem, 1)

            def layer1_unit(b, u):
                h, jt = u // T, u % T
                pe.wait_ge(edges_ready.sem, edges_ready.of(b, u + 1))
                if jt == 0 and h:
                    pe.wait_ge(sumB_ready.sem, sumB_ready.of(b, h))
                for t in range(T):
                    col = (t % 4) * P
                    last = pe.matmul(fp[:, 1 + t // 4, col:col + 2 * PARTS * C1],
                                     edges[:, u % B_RING, t * P:(t + 1) * P],
                                     vh_parts[:, jt, h, :, :, :].rearrange("p a k c -> p (a k c)"),
                                     start=(jt == 0 and t % 4 == 0), stop=(jt == T - 1), skip_group_check=True)
                last.then_inc(edges_used.sem, 1)

            def layer2_turn(b, parity):
                pe.wait_ge(x2_ready.sem, x2_ready.of(b))
                turn_rows(x2[:, parity], kp_pair, x2_turned)
                pe.wait_ge(x2T_ready.sem, x2T_ready.of(b))
                if o3_ready.any_before(b):
                    pe.wait_ge(o3_ready.sem, o3_ready.before(b))
                for t in range(T):
                    last = pe.matmul(kp[:, 1 + t // 2, (t % 2) * 2 * D:(t % 2 + 1) * 2 * D],
                                     x2T[:, t * P:(t + 1) * P], rhs2[:], start=True, stop=True)
                last.then_inc(y2_made.sem, 1)

            def layer2_sum(b, parity):
                pe.wait_ge(y2_ready.sem, y2_ready.of(b))
                for g in range(len(GROUPS)):
                    for n, t in enumerate(GROUPS[g]):
                        col = n * (D + 1)
                        for jt in range(T):
                            lhsT = AT[:, parity, jt, t * P:(t + 1) * P]
                            pe.matmul(kp[:, g, col:col + D + 1], lhsT, y2_hi[:, jt, :], start=(jt == 0), stop=False,
                                      skip_group_check=True)
                            for k in range(2):
                                last = pe.matmul(kp[:, g, col:col + D], lhsT, y2_lo[:, jt, k, :], start=False,
                                                 stop=(jt == T - 1 and k == 1), skip_group_check=True)
                last.then_inc(sum2_made.sem, 1)

            def layer3_turn(b):
                pe.wait_ge(x3_ready.sem, x3_ready.of(b))
                turn_rows(x3, kp_pair, x3_turned)
                pe.wait_ge(x3T_ready.sem, x3T_ready.of(b))
                for t in range(T):
                    last = pe.matmul(kp[:, 3 + t // 4, (t % 4) * D:(t % 4 + 1) * D], x3T[:, t * P:(t + 1) * P],
                                     rhs3[:], start=True, stop=True)
                last.then_inc(w3_made.sem, 1)

            def layer3_turn_cuts(b):
                pe.wait_ge(qmax_ready.sem, qmax_ready.of(b))
                pe.transpose(kp[0:H3, 0, 0:P], qmax3[:], ident[:]).then_inc(qmax_turned.sem, 1)
                pe.wait_ge(w3_ready.sem, w3_ready.of(b))
                for n in range(2 * H3):
                    h, which = n // 2, n % 2
                    if n >= 4:
                        copied = cutT_dve if which else cutT_act
                        pe.wait_ge(copied.sem, copied.of(b, h - 1))
                    dst = kp[:, 1 + n % 4, :].bitcast(BF16)
                    rows_cut = (cutB if which else cutA).rearrange("p (t h) k o -> p t h (k o)", h=H3)
                    for t in range(T):
                        last = pe.transpose(dst[:, t * P:(t + 1) * P], rows_cut[:, t, h, :], identb[:])
                    last.then_inc(cut_turned.sem, 1)
                    if n == 1:
                        pe.wait_ge(qdiag_ready.sem, qdiag_ready.of(b))
                        pe.matmul(kp[:, 0, P:P + H3], ones[0:H3, :], qdiag3[:], start=True, stop=True) \
                            .then_inc(q_spread.sem, 1)

            def layer3_scores(b, w):
                h, jt = w // T, w % T
                if w == 0:
                    pe.wait_ge(cutT_act.sem, cutT_act.of(b))
                    pe.wait_ge(cutT_dve.sem, cutT_dve.of(b))
                    pe.wait_ge(shift_ready.sem, shift_ready.of(b))
                tile = slice(jt * P, (jt + 1) * P)
                for n in range(2):
                    q = 2 * w + n
                    if q >= 3:
                        pe.wait_ge(exp3_ready.sem, exp3_ready.of(b, q - 2))
                    cols = slice(n * HALF, (n + 1) * HALF)
                    pe.matmul(kp[:, 2 + q % 3, :], cutT[:, h, 1, tile], cutT[:, h, 0, cols], start=True, stop=False)
                    pe.matmul(kp[:, 2 + q % 3, :], cutT[0:2 * O3, h, 0, tile], cutT[0:2 * O3, h, 1, cols],
                              start=False, stop=True).then_inc(scores_made.sem, 1)

            def layer3_values(b, w):
                h, jt = w // T, w % T
                if w in POOL_MASKS:
                    pe.wait_ge(masked_pool.sem, masked_pool.of(b, POOL_MASKS.index(w) + 1))
                else:
                    pe.wait_ge(masked_dve.sem, masked_dve.of(b, DVE_MASKS.index(w) + 1))
                if jt == 0 and h:
                    pe.wait_ge(sum3_ready.sem, sum3_ready.of(b, h))
                for n in range(2):
                    last = pe.matmul(kp[0:C3, n, :], w3[:, jt * H3 + h, :],
                                     weight3[:, w % P_RING, n * HALF:(n + 1) * HALF],
                                     start=(jt == 0), stop=(jt == T - 1))
                last.then_inc(weight3_used.sem, 1)

            def layer3_turn_back(b):
                pe.wait_ge(sum3_ready.sem, sum3_ready.of(b))
                pe.sem_inc(turnstile, 1)
                for g in range(len(GROUPS)):
                    for n, t in enumerate(GROUPS[g]):
                        for h in range(H3):
                            col = (n * H3 + h) * C3
                            last = pe.transpose(kp[:, 2 + g, col:col + C3], o3T[:, h * N + t * P:h * N + (t + 1) * P],
                                                ident[0:C3, 0:C3])
                last.then_inc(sum3_turned.sem, 1)

            pe.wait_ge(w_loaded, 160)
            pe.wait_ge(consts_made, 3)
            pe.transpose(fp[:, 0, 0:P], self_w[:], ident[:]).then_inc(self_turned, 1)
            pe.wait_ge(weights_ready, 1)

            def body(parity, f, k, m):
                if m is not None:
                    layer3_turn_back(m)
                if f is not None:
                    for jt in range(T):
                        turn_adjacency_tile(f, jt)
                    layer0_turn(f)
                if k is not None:
                    layer2_turn(k, 1 - parity)
                if f is not None:
                    layer0_project(f)
                if k is not None:
                    layer2_sum(k, 1 - parity)
                if f is not None:
                    for jt in range(T):
                        layer0_unit(f, jt)
                if k is not None:
                    layer3_turn(k)
                if f is not None:
                    layer0_finish(f)
                if k is not None:
                    layer3_turn_cuts(k)
                if f is not None:
                    layer1_turn(f)
                    layer1_sum_all(f, parity)
                    for n in range(4):
                        spread_s1(f, n)
                for s in range(U3 + PV_LAG):
                    if k is not None and s < U3:
                        layer3_scores(k, s)
                    if f is not None and 1 <= s <= U3:
                        layer1_unit(f, 2 * s - 2)
                        layer1_unit(f, 2 * s - 1)
                        if s % 4 == 0 and 2 * (s // 4) + 3 < 2 * H1:
                            spread_s1(f, 2 * (s // 4) + 2)
                            spread_s1(f, 2 * (s // 4) + 3)
                    if k is not None and s >= PV_LAG:
                        layer3_values(k, s - PV_LAG)

            schedule(pe, body)

        @block.scalar
        def _(act):
            def copy(dst, src):
                return act.activation(dst, src, ACT.Copy)

            def adjacency_tile(b, parity, jt):
                act.wait_ge(a_turned.sem, a_turned.of(b, jt + 1))
                if jt == 0 and sum2_made.any_before(b - 1):
                    act.wait_ge(sum2_made.sem, sum2_made.before(b - 1))
                    act.wait_ge(masked_dve.sem, masked_dve.before(b - 1))
                    act.wait_ge(masked_pool.sem, masked_pool.before(b - 1))
                copy(AT[:, parity, jt, :], fp[:, jt % 3, :].bitcast(BF16)).then_inc(at_ready.sem, 1)

            def normalise(rstd_ready, done, b, n, y, dst, small):
                act.wait_ge(rstd_ready.sem, rstd_ready.of(b, n + 1))
                for t in range(T):
                    last = act.activation(dst[:, t, :], y[:, t, :], ACT.Identity, bias=small[:, 6, t:t + 1],
                                          scale=small[:, 5, t:t + 1])
                last.then_inc(done.sem, 1)

            def layer0_turn(b):
                act.wait_ge(x0_turned.sem, x0_turned.of(b))
                copy(x0T[:], fp_pair).then_inc(x0T_ready.sem, 1)

            def layer0_prepare(b):
                act.wait_ge(z0_ready.sem, z0_ready.of(b))
                act.activation(c0, c0, ACT.Exp, scale=-(1.0 - SLOPE)).then_inc(c0_ready.sem, 1)
                act.wait_ge(h0_made.sem, h0_made.of(b))
                for g in range(len(GROUPS)):
                    src = thirds(fp, g, D + 2)
                    act.activation(v0[:, tiles(g)], src[:, :, D + 1], ACT.Exp, bias=T0neg[:])
                    act.activation(v0s[:, tiles(g)], src[:, :, D + 1], ACT.Exp, bias=T0neg2[:], scale=SLOPE)
                    last = copy(h0[:, tiles(g), :], src[:, :, 0:D])
                last.then_inc(h0_ready.sem, 1)

            def layer0_finish(b):
                act.wait_ge(weight0_used.sem, weight0_used.of(b))
                copy(num0T[:], fp_pair).then_inc(num0T_ready.sem, 1)

            def layer1_turn(b):
                act.wait_ge(x1_turned.sem, x1_turned.of(b))
                copy(x1T[:], fp_pair).then_inc(x1T_ready.sem, 1)
                act.wait_ge(h1_made.sem, h1_made.of(b))
                for g in range(len(GROUPS)):
                    last = copy(st1[:, tiles(g), :], thirds(fp, g, D + 2 * H1)[:, :, D:D + 2 * H1])
                last.then_inc(st1_ready.sem, 1)
                for g in range(len(GROUPS)):
                    for n, t in enumerate(GROUPS[g]):
                        last = copy(h1[:, t, :, 0:O1], thirds(fp, g, D + 2 * H1)[:, n, 0:D].rearrange(
                            "p (h o) -> p h o", h=H1))
                last.then_inc(h1_ready.sem, 1)
                act.wait_ge(s1_made.sem, s1_made.of(b))
                copy(s1_parts[0:H1, :], fp_pair[0:H1, :]).then_inc(s1_first.sem, 1)
                act.wait_ge(z1_ready.sem, z1_ready.of(b))
                act.activation(v1[:, 0], dt1[:], ACT.Exp)
                act.activation(v1[:, 1], dt1[:], ACT.Exp, scale=SLOPE)
                act.activation(c1[:], zs1[:], ACT.Exp, scale=-(1.0 - SLOPE)).then_inc(v1_ready.sem, 1)

            def layer1_cut(b):
                flat = "p t h a c -> p (t h a) c"
                act.wait_ge(vh_whole.sem, vh_whole.of(b))
                copy(vh_parts[:, :, :, :, 0, :].rearrange(flat), vh[:].rearrange(flat)).then_inc(vh_first.sem, 1)
                act.wait_ge(vh_rested.sem, vh_rested.of(b))
                copy(vh_parts[:, :, :, :, 1, :].rearrange(flat), vh_rest[:].rearrange(flat)) \
                    .then_inc(vh_second.sem, 1)

            def layer1_sum_all(b):
                act.wait_ge(sumA_made.sem, sumA_made.of(b))
                for g in range(len(GROUPS)):
                    last = copy(sumA[:, tiles(g)], thirds(fp, g, H1 * C1).rearrange("p t (h c) -> p t h c", h=H1))
                last.then_inc(sumA_ready.sem, 1)

            def s1_half(b, n):
                h, half = n // 2, n % 2
                act.wait_ge(s1_spread.sem, s1_spread.of(b, n + 1))
                if h >= 2:
                    act.wait_ge(edges_ready.sem, edges_ready.of(b, (h - 1) * T))
                copy(s1row[:, h % 2, half * HALF:(half + 1) * HALF], fp[:, 0, :]).then_inc(s1_ready.sem, 1)

            def ramp_unit(b, u):
                h, jt, r = u // T, u % T, RAMPS.index(u)
                if r >= R_RING:
                    act.wait_ge(edges_ready.sem, edges_ready.of(b, RAMPS[r - R_RING] + 1))
                act.wait_ge(s1_ready.sem, s1_ready.of(b, 2 * h + 2))
                act.activation(ramp[:, r % R_RING, :], s1row[:, h % 2, :], ACT.Relu, bias=tbig1[:, jt, h:h + 1],
                               scale=BIG).then_inc(ramp_ready.sem, 1)

            def layer1_finish(b):
                act.wait_ge(elu_min.sem, elu_min.of(b))
                act.activation(elu, elu, ACT.Exp).then_inc(elu_exp.sem, 1)

            def layer2_turn(b):
                act.wait_ge(x2_turned.sem, x2_turned.of(b))
                copy(x2T[:], kp_pair).then_inc(x2T_ready.sem, 1)

            def layer3_turn(b):
                act.wait_ge(x3_turned.sem, x3_turned.of(b))
                copy(x3T[:], kp_pair).then_inc(x3T_ready.sem, 1)
                act.wait_ge(w3_made.sem, w3_made.of(b))
                src = kp[:, 3:5, :].rearrange("p a (b o) -> p (a b) o", o=O3)
                copy(cutA[:, :, 2, :], src)
                copy(w3[:, :, 0:O3], src).then_inc(w3_ready.sem, 1)

            def layer3_turn_cuts(b):
                for h in range(H3):
                    act.wait_ge(cut_turned.sem, cut_turned.of(b, 2 * h + 1))
                    copy(cutT[:, h, 0, :], kp[:, 1 + (2 * h) % 4, :].bitcast(BF16)).then_inc(cutT_act.sem, 1)

            def layer3_exp(b, w):
                h = w // T
                if w >= P_RING:
                    act.wait_ge(weight3_used.sem, weight3_used.of(b, w - P_RING + 1))
                if w == 0:
                    act.wait_ge(shift_ready.sem, shift_ready.of(b))
                for n in range(2):
                    q = 2 * w + n
                    act.wait_ge(scores_made.sem, scores_made.of(b, q + 1))
                    act.activation(weight3[:, w % P_RING, n * HALF:(n + 1) * HALF], kp[:, 2 + q % 3, :], ACT.Exp,
                                   bias=shift3[:, h:h + 1], scale=ROOT).then_inc(exp3_ready.sem, 1)

            def layer3_head_out(b, h):
                act.wait_ge(weight3_used.sem, weight3_used.of(b, (h + 1) * T))
                copy(o3T[:, h * N:(h + 1) * N], kp_pair[0:C3, :]).then_inc(sum3_ready.sem, 1)

            act.wait_ge(weights_ready, 1)

            def body(parity, f, k, m):
                if f is not None:
                    for jt in range(4):
                        adjacency_tile(f, parity, jt)
                if k is not None:
                    layer1_finish(k)
                if f is not None:
                    for jt in range(4, T):
                        adjacency_tile(f, parity, jt)
                    layer0_turn(f)
                if k is not None:
                    normalise(frstd_ready, x2_ready, k, 1, yf, x2[:, 1 - parity], fsmall)
                    layer2_turn(k)
                if m is not None:
                    normalise(brstd_ready, x4_ready, m, 2, yb, x4, bsmall)
                if f is not None:
                    layer0_prepare(f)
                if k is not None:
                    normalise(brstd_ready, normed2, k, 0, yb, yb, bsmall)
                    normalise(brstd_ready, x3_ready, k, 1, yb, x3, bsmall)
                if f is not None:
                    layer0_finish(f)
                if k is not None:
                    layer3_turn(k)
                if f is not None:
                    normalise(frstd_ready, x1_ready, f, 0, yf, x1, fsmall)
                if k is not None:
                    layer3_turn_cuts(k)
                if f is not None:
                    layer1_turn(f)
                    layer1_cut(f)
                    layer1_sum_all(f)
                    for n in range(4):
                        s1_half(f, n)
                    for u in RAMPS[:2]:
                        ramp_unit(f, u)
                ramps = 2
                for s in range(U3 + PV_LAG + 1):
                    if k is not None and s < U3:
                        layer3_exp(k, s)
                    if f is not None:
                        while ramps < len(RAMPS) and RAMPS[ramps] <= 2 * s + 3:
                            ramp_unit(f, RAMPS[ramps])
                            ramps += 1
                        if s >= 1 and s % 4 == 0 and 2 * (s // 4) + 3 < 2 * H1:
                            s1_half(f, 2 * (s // 4) + 2)
                            s1_half(f, 2 * (s // 4) + 3)
                    if k is not None and s >= T and (s - PV_LAG) % T == 0:
                        layer3_head_out(k, (s - PV_LAG) // T - 1)

            schedule(act, body)

        @block.vector
        def _(dve):
            front, back = Steps(dve_front), Steps(dve_back)
            front_last, back_last = Steps(dve_front_last), Steps(dve_back_last, 6)

            def spread_over(col, width):
                return col.unsqueeze(len(col.shape)).broadcast_to(list(col.shape) + [width])

            def per_tile(row):
                return row.unsqueeze(1).broadcast_to([P, T, D])

            def layer_stats(chain, y, stat, small, var_ready):
                for t in range(T):
                    last = dve.bn_stats(stat[:, t, :], y[:, t, :])
                last.then_inc(chain.sem, 1)
                dve.wait_ge(chain.sem, chain.step())
                dve.tensor_tensor(small[:, 3, :], stat[:, :, 1], stat[:, :, 4], ALU.add)
                dve.tensor_tensor(small[:, 1, :], stat[:, :, 1], stat[:, :, 4], ALU.subtract)
                dve.tensor_tensor(small[:, 2, :], stat[:, :, 2], stat[:, :, 5], ALU.add).then_inc(chain.sem, 1)
                dve.wait_ge(chain.sem, chain.step())
                dve.tensor_scalar(small[:, 0, :], small[:, 3, :], -0.5, None, ALU.mult)
                dve.scalar_tensor_tensor(out=small[:, 7, :], in0=small[:, 1, :], scalar=D / 4.0,
                                         in1=small[:, 1, :], op0=ALU.mult, op1=ALU.mult).then_inc(chain.sem, 1)
                dve.wait_ge(chain.sem, chain.step())
                dve.tensor_tensor(small[:, 2, :], small[:, 7, :], small[:, 2, :], ALU.add).then_inc(chain.sem, 1)
                dve.wait_ge(chain.sem, chain.step())
                dve.tensor_scalar(small[:, 4, :], small[:, 2, :], 1.0 / D, EPS, ALU.mult, ALU.add) \
                    .then_inc(var_ready.sem, 1)

            def prepare_weights():
                dve.wait_ge(w_loaded, 160)
                dve.wait_ge(consts_made, 3)
                step = Steps(dve_setup)
                step.begin(0)
                for k, spread_w in ((0, src0), (1, dst0)):
                    dve.tensor_tensor(w_tmp[:], rhs0[:, 0:D], a0_row[:, k, :], ALU.mult).then_inc(step.sem, 1)
                    dve.wait_ge(step.sem, step.step())
                    dve.tensor_reduce(rhs0[:, D + k:D + k + 1], w_tmp[:], AX_X, ALU.add).then_inc(step.sem, 1)
                    dve.wait_ge(step.sem, step.step())
                    dve.tensor_copy(spread_w[:], rhs0[:, D + k:D + k + 1].broadcast_to([P, P]))
                for k in range(2):
                    dve.tensor_tensor(w_tmp[:].rearrange("p (h o) -> p h o", h=H1),
                                      rhs1[:, 0:D].rearrange("p (h o) -> p h o", h=H1),
                                      a1_row[:, :, k * O1:(k + 1) * O1], ALU.mult).then_inc(step.sem, 1)
                    dve.wait_ge(step.sem, step.step())
                    dve.tensor_reduce(rhs1[:, D + k * H1:D + (k + 1) * H1],
                                      w_tmp[:].rearrange("p (h o) -> p h o", h=H1), AX_X, ALU.add).then_inc(step.sem, 1)
                    dve.wait_ge(step.sem, step.step())
                dve.memset(pick1[:], 0.0)
                dve.memset(s1_parts[:], 0.0).then_inc(step.sem, 1)
                dve.wait_ge(step.sem, step.step())
                for k in range(PARTS):
                    part = slice(32 * k, 32 * k + H1)
                    dve.tensor_copy(pick1[part, :, :], spread_over(ident[part, part], P))
                dve.tensor_copy(identb[:], ident[:])
                dve.memset(h1[:, :, :, O1:C1], 1.0)
                dve.memset(w3[:, :, O3:C3], 1.0)
                dve.wait_ge(self_turned, 1)
                dve.tensor_copy(rhs2[:, D:2 * D], fp[:, 0, 0:P]).then_inc(weights_ready, 1)

            def layer0_top(b):
                dve.wait_ge(t0_spread.sem, t0_spread.of(b))
                dve.tensor_reduce(T0[:], fp_pair, AX_X, ALU.max).then_inc(front.sem, 1)
                dve.wait_ge(front.sem, front.step())
                dve.tensor_scalar(T0neg[:], T0[:], -1.0, None, ALU.mult)
                dve.tensor_scalar(T0neg2[:], T0[:], -SLOPE, None, ALU.mult).then_inc(T0_ready.sem, 1)

            def layer0_z(b):
                dve.wait_ge(s0_spread.sem, s0_spread.of(b))
                dve.tensor_scalar(c0, fp_pair, T0[:], 0.0, ALU.add, ALU.max).then_inc(z0_ready.sem, 1)

            def layer0_unit(b, parity, jt):
                if jt == 0:
                    dve.wait_ge(c0_ready.sem, c0_ready.of(b))
                    dve.wait_ge(h0_ready.sem, h0_ready.of(b))
                    dve.wait_ge(at_ready.sem, at_ready.of(b))
                w = weight0[:, jt % P0_RING, :]
                if jt >= P0_RING:
                    dve.wait_ge(weight0_used.sem, weight0_used.of(b, jt - P0_RING + 1))
                    dve.wait_ge(weight0_added.sem, weight0_added.of(b, max(jt - P0_RING, 1)))
                dve.tensor_scalar(w, c0, v0s[:, jt:jt + 1], v0[:, jt:jt + 1], ALU.mult, ALU.max) \
                    .then_inc(front.sem, 1)
                dve.wait_ge(front.sem, front.step())
                dve.tensor_tensor(w, w, AT[:, parity, jt, :], ALU.mult).then_inc(weight0_ready.sem, 1)

            def layer0_finish(b):
                dve.wait_ge(den0_made.sem, den0_made.of(b))
                dve.reciprocal(rec0[:], fp[:, 0, 0:T]).then_inc(front.sem, 1)
                dve.wait_ge(front.sem, front.step())
                dve.wait_ge(num0_turned.sem, num0_turned.of(b))
                dve.tensor_tensor(yf[:], fp_pair.rearrange("p (t d) -> p t d", t=T), spread_over(rec0[:], D),
                                  ALU.mult).then_inc(front.sem, 1)
                dve.wait_ge(front.sem, front.step())
                flat = "p t d -> p (t d)"
                dve.scalar_tensor_tensor(out=yf.rearrange(flat), in0=yf.rearrange(flat), scalar=0.0,
                                         in1=x0.rearrange(flat), op0=ALU.max, op1=ALU.add).then_inc(front.sem, 1)
                dve.wait_ge(front.sem, front.step())
                layer_stats(front, yf, fstat, fsmall, fvar_ready)

            def layer1_top(b):
                dve.wait_ge(st1_ready.sem, st1_ready.of(b))
                dve.tensor_reduce(tmax1[:], st1[:, :, H1:2 * H1].rearrange("p t h -> p h t"), AX_X, ALU.max) \
                    .then_inc(tmax1_ready.sem, 1)
                dve.tensor_scalar(tneg1[:], st1[:, :, H1:2 * H1], -1.0, None, ALU.mult)
                dve.tensor_scalar(tbig1[:], st1[:, :, H1:2 * H1], BIG, None, ALU.mult)
                dve.wait_ge(tmax1_turned.sem, tmax1_turned.of(b))
                dve.tensor_reduce(tcol1[:], fp[0:H1, 0, 0:P], AX_X, ALU.max).then_inc(front.sem, 1)
                dve.wait_ge(front.sem, front.step())
                dve.tensor_scalar(tdiag1[:], ident[0:H1, 0:H1], tcol1[:], None, ALU.mult) \
                    .then_inc(tdiag1_ready.sem, 1)
                dve.wait_ge(T1_spread.sem, T1_spread.of(b))
                dve.tensor_copy(T1[:], fp[:, 0, P:P + H1]).then_inc(front.sem, 1)
                dve.wait_ge(front.sem, front.step())
                T1_tiles = T1[:].unsqueeze(1).broadcast_to([P, T, H1])
                dve.tensor_tensor(dt1[:], st1[:, :, H1:2 * H1], T1_tiles, ALU.subtract)
                dve.tensor_tensor(zs1[:], st1[:, :, 0:H1], T1_tiles, ALU.add).then_inc(front.sem, 1)
                dve.wait_ge(front.sem, front.step())
                dve.tensor_scalar(zs1[:], zs1[:], 0.0, None, ALU.max).then_inc(z1_ready.sem, 1)

            def layer1_columns(b):
                dve.wait_ge(v1_ready.sem, v1_ready.of(b))
                dve.wait_ge(h1_ready.sem, h1_ready.of(b))
                flat = "p t h c -> p (t h) c"
                for k in range(2):
                    last = dve.tensor_tensor(vh[:, :, :, k, :].rearrange(flat), h1[:].rearrange(flat),
                                             spread_over(v1[:, k].rearrange("p t h -> p (t h)"), C1), ALU.mult)
                last.then_inc(vh_whole.sem, 1)
                dve.wait_ge(s1_first.sem, s1_first.of(b))
                dve.tensor_tensor(s1_rest, fp_pair[0:H1, :], s1_parts[0:H1, :], ALU.subtract).then_inc(front.sem, 1)
                dve.wait_ge(front.sem, front.step())
                dve.tensor_copy(s1_mid, s1_rest).then_inc(front.sem, 1)
                dve.wait_ge(front.sem, front.step())
                dve.tensor_copy(s1_parts[32:32 + H1, :], s1_mid)
                dve.tensor_tensor(s1_parts[64:64 + H1, :], s1_rest, s1_mid, ALU.subtract).then_inc(s1_cut.sem, 1)
                flat = "p t h a c -> p (t h a) c"
                part = [vh_parts[:, :, :, :, k, :].rearrange(flat) for k in range(PARTS)]
                whole, rest = vh[:].rearrange(flat), vh_rest[:].rearrange(flat)
                dve.wait_ge(vh_first.sem, vh_first.of(b))
                dve.tensor_tensor(rest, whole, part[0], ALU.subtract).then_inc(vh_rested.sem, 1)
                dve.wait_ge(vh_second.sem, vh_second.of(b))
                dve.tensor_tensor(part[2], rest, part[1], ALU.subtract).then_inc(vh_ready.sem, 1)

            def layer1_unit(b, parity, u):
                h, jt = u // T, u % T
                if u >= B_RING:
                    dve.wait_ge(edges_used.sem, edges_used.of(b, u - B_RING + 1))
                if u in RAMPS:
                    r = RAMPS.index(u)
                    dve.wait_ge(ramp_ready.sem, ramp_ready.of(b, r + 1))
                    dve.tensor_tensor(edges[:, u % B_RING, :], ramp[:, r % R_RING, :], AT[:, parity, jt, :],
                                      ALU.min).then_inc(edges_ready.sem, 1)
                else:
                    dve.wait_ge(s1_ready.sem, s1_ready.of(b, 2 * h + 2))
                    dve.scalar_tensor_tensor(out=edges[:, u % B_RING, :], in0=s1row[:, h % 2, :],
                                             scalar=tneg1[:, jt, h:h + 1], in1=AT[:, parity, jt, :], op0=ALU.is_gt,
                                             op1=ALU.mult).then_inc(edges_ready.sem, 1)

            def layer1_head_out(b, h):
                dve.wait_ge(edges_used.sem, edges_used.of(b, (h + 1) * T))
                for n in range(2):
                    src = fp[:, 1 + n, :].rearrange("p (t c) -> p t c", t=4)[:, :, 0:2 * PARTS * C1]
                    for a in range(2):
                        last = dve.tensor_reduce(
                            sumB[:, 4 * n:4 * n + 4, h, a, :],
                            src[:, :, a * PARTS * C1:(a + 1) * PARTS * C1].rearrange("p t (k c) -> p t c k", k=PARTS),
                            AX_X, ALU.add)
                last.then_inc(sumB_ready.sem, 1)

            def layer1_finish(b):
                dve.wait_ge(sumA_ready.sem, sumA_ready.of(b))
                dve.wait_ge(sumB_ready.sem, sumB_ready.of(b))
                flat = "p t h c -> p (t h) c"
                A = sumA[:].rearrange(flat)
                Bv, Bs = (sumB[:, :, :, a, :].rearrange(flat) for a in range(2))
                dve.tensor_tensor(A, A, Bs, ALU.subtract).then_inc(front_last.sem, 1)
                dve.wait_ge(front_last.sem, front_last.step())
                dve.tensor_tensor(A, A, spread_over(c1[:].rearrange("p t h -> p (t h)"), C1), ALU.mult).then_inc(front_last.sem, 1)
                dve.wait_ge(front_last.sem, front_last.step())
                dve.tensor_tensor(A, A, Bv, ALU.add).then_inc(front_last.sem, 1)
                dve.wait_ge(front_last.sem, front_last.step())
                dve.reciprocal(rec1[:].rearrange("p t h -> p (t h)"), A[:, :, O1]).then_inc(front_last.sem, 1)
                dve.wait_ge(front_last.sem, front_last.step())
                o = yf.rearrange("p t (h o) -> p (t h) o", h=H1)
                dve.tensor_tensor(o, A[:, :, 0:O1],
                                  spread_over(rec1[:].rearrange("p t h -> p (t h)"), O1), ALU.mult).then_inc(front_last.sem, 1)
                dve.wait_ge(front_last.sem, front_last.step())
                dve.tensor_scalar(elu[:], yf[:], 0.0, None, ALU.min).then_inc(elu_min.sem, 1)
                flat = "p t d -> p (t d)"
                dve.scalar_tensor_tensor(out=yf.rearrange(flat), in0=yf.rearrange(flat), scalar=0.0,
                                         in1=x1.rearrange(flat), op0=ALU.max, op1=ALU.add).then_inc(front_last.sem, 1)
                dve.wait_ge(front_last.sem, front_last.step())
                dve.wait_ge(elu_exp.sem, elu_exp.of(b))
                dve.scalar_tensor_tensor(out=yf.rearrange(flat), in0=elu.rearrange(flat), scalar=-1.0,
                                         in1=yf.rearrange(flat), op0=ALU.add, op1=ALU.add).then_inc(front_last.sem, 1)
                dve.wait_ge(front_last.sem, front_last.step())
                layer_stats(front_last, yf, fstat, fsmall, fvar_ready)

            def layer2_columns(b):
                dve.wait_ge(y2_made.sem, y2_made.of(b))
                src = kp[:, 1:5, :].rearrange("p a (n c) -> p (a n) c", n=2)
                dve.memset(y2_hi[:, :, D:D + 1], 1.0)
                dve.tensor_copy(y2_hi[:, :, 0:D], src[:, :, 0:D]).then_inc(back.sem, 1)
                dve.wait_ge(back.sem, back.step())
                dve.tensor_tensor(rest2, src[:, :, 0:D], y2_hi[:, :, 0:D], ALU.subtract)
                dve.tensor_tensor(self2, src[:, :, D:2 * D], per_tile(bias2[:]), ALU.add).then_inc(back.sem, 1)
                dve.wait_ge(back.sem, back.step())
                dve.tensor_copy(y2_lo[:, :, 0, :], rest2).then_inc(back.sem, 1)
                dve.wait_ge(back.sem, back.step())
                dve.tensor_tensor(y2_lo[:, :, 1, :], rest2, y2_lo[:, :, 0, :], ALU.subtract) \
                    .then_inc(y2_ready.sem, 1)

            def layer2_out(b):
                dve.wait_ge(sum2_made.sem, sum2_made.of(b))
                for g in range(len(GROUPS)):
                    last = dve.tensor_scalar(deg2[:, tiles(g)], thirds(kp, g, D + 1)[:, :, D], 1e-6, None, ALU.max)
                last.then_inc(back.sem, 1)
                dve.wait_ge(back.sem, back.step())
                dve.reciprocal(deg2[:], deg2[:]).then_inc(back.sem, 1)
                dve.wait_ge(back.sem, back.step())
                if stored.any_before(b):
                    dve.wait_ge(stored.sem, stored.before(b))
                for g in range(len(GROUPS)):
                    for n, t in enumerate(GROUPS[g]):
                        last = dve.scalar_tensor_tensor(out=yb[:, t, :], in0=thirds(kp, g, D + 1)[:, n, 0:D],
                                                        scalar=deg2[:, t:t + 1], in1=self2[:, t, :], op0=ALU.mult,
                                                        op1=ALU.add)
                last.then_inc(back.sem, 1)
                dve.wait_ge(back.sem, back.step())
                layer_stats(back, yb, bstat, bsmall, bvar_ready)

            def layer2_residual(b, parity):
                dve.wait_ge(normed2.sem, normed2.of(b))
                dve.tensor_tensor(yb[:], yb[:], per_tile(gamma2[:]), ALU.mult).then_inc(back.sem, 1)
                dve.wait_ge(back.sem, back.step())
                dve.tensor_tensor(yb[:], yb[:], per_tile(beta2[:]), ALU.add).then_inc(back.sem, 1)
                dve.wait_ge(back.sem, back.step())
                flat = "p t d -> p (t d)"
                dve.scalar_tensor_tensor(out=yb.rearrange(flat), in0=yb.rearrange(flat), scalar=0.0,
                                         in1=x2[:, parity].rearrange(flat), op0=ALU.max, op1=ALU.add) \
                    .then_inc(back.sem, 1)
                dve.wait_ge(back.sem, back.step())
                layer_stats(back, yb, bstat, bsmall, bvar_ready)

            def layer3_cut(b):
                dve.wait_ge(w3_ready.sem, w3_ready.of(b))
                W = w3[:, :, 0:O3]
                dve.tensor_tensor(rest3, W, cutA[:, :, 2, :], ALU.subtract).then_inc(back.sem, 1)
                dve.wait_ge(back.sem, back.step())
                dve.tensor_copy(cutA[:, :, 0, :], rest3)
                dve.tensor_copy(cutB[:, :, 0:3, :],
                                cutA[:, :, 2, :].unsqueeze(2).broadcast_to([P, T * H3, 3, O3])) \
                    .then_inc(back.sem, 1)
                dve.wait_ge(back.sem, back.step())
                dve.tensor_copy(cutA[:, :, 3, :], cutA[:, :, 0, :])
                dve.tensor_copy(cutB[:, :, 3, :], cutA[:, :, 0, :])
                dve.tensor_tensor(cutA[:, :, 1, :], rest3, cutA[:, :, 0, :], ALU.subtract).then_inc(back.sem, 1)
                dve.wait_ge(back.sem, back.step())
                dve.tensor_tensor(rest3, W, W, ALU.mult).then_inc(back.sem, 1)
                dve.wait_ge(back.sem, back.step())
                dve.tensor_reduce(q3[:], rest3, AX_X, ALU.add).then_inc(back.sem, 1)
                dve.wait_ge(back.sem, back.step())
                dve.tensor_reduce(qmax3[:], q3[:].rearrange("p (t h) -> p h t", h=H3), AX_X, ALU.max) \
                    .then_inc(qmax_ready.sem, 1)

            def layer3_shift(b):
                dve.wait_ge(qmax_turned.sem, qmax_turned.of(b))
                dve.tensor_reduce(qcol3[:], kp[0:H3, 0, 0:P], AX_X, ALU.max).then_inc(back.sem, 1)
                dve.wait_ge(back.sem, back.step())
                dve.tensor_scalar(qdiag3[:], ident[0:H3, 0:H3], qcol3[:], None, ALU.mult) \
                    .then_inc(qdiag_ready.sem, 1)
                dve.wait_ge(q_spread.sem, q_spread.of(b))
                dve.tensor_scalar(shift3[:], kp[:, 0, P:P + H3], -ROOT, None, ALU.mult).then_inc(shift_ready.sem, 1)
                for h in range(H3):
                    dve.wait_ge(cut_turned.sem, cut_turned.of(b, 2 * h + 2))
                    dve.tensor_copy(cutT[:, h, 1, :], kp[:, 1 + (2 * h + 1) % 4, :].bitcast(BF16)) \
                        .then_inc(cutT_dve.sem, 1)

            def layer3_mask(b, parity, w):
                dve.wait_ge(exp3_ready.sem, exp3_ready.of(b, 2 * w + 2))
                tile = weight3[:, w % P_RING, :]
                dve.tensor_tensor(tile, tile, AT[:, parity, w % T, :], ALU.mult).then_inc(masked_dve.sem, 1)

            def layer3_finish(b):
                dve.wait_ge(sum3_turned.sem, sum3_turned.of(b))
                src = [thirds(kp[:, 2:5], g, H3 * C3).rearrange("p t (h c) -> p t h c", h=H3)
                       for g in range(len(GROUPS))]
                for g in range(len(GROUPS)):
                    last = dve.reciprocal(rec3[:, tiles(g), :], src[g][:, :, :, O3])
                last.then_inc(back_last.sem, 1)
                dve.wait_ge(back_last.sem, back_last.step())
                for g in range(len(GROUPS)):
                    last = dve.tensor_tensor(yb[:, tiles(g), :].rearrange("p t (h o) -> p t h o", h=H3),
                                             src[g][:, :, :, 0:O3], spread_over(rec3[:, tiles(g), :], O3), ALU.mult)
                last.then_inc(o3_ready.sem, 1)
                dve.wait_ge(o3_ready.sem, o3_ready.of(b))
                dve.tensor_tensor(yb[:], yb[:], x3[:], ALU.add).then_inc(back_last.sem, 1)
                dve.wait_ge(back_last.sem, back_last.step())
                layer_stats(back_last, yb, bstat, bsmall, bvar_ready)

            prepare_weights()

            def body(parity, f, k, m):
                if k is not None:
                    front_last.begin(k)
                    layer1_finish(k)
                if m is not None:
                    back_last.begin(m)
                    layer3_finish(m)
                if f is not None:
                    front.begin(f)
                    layer0_top(f)
                if k is not None:
                    back.begin(k)
                    layer2_columns(k)
                if f is not None:
                    layer0_z(f)
                    for jt in range(3):
                        layer0_unit(f, parity, jt)
                if k is not None:
                    layer2_out(k)
                if f is not None:
                    for jt in range(3, 6):
                        layer0_unit(f, parity, jt)
                if k is not None:
                    layer2_residual(k, 1 - parity)
                if f is not None:
                    for jt in range(6, T):
                        layer0_unit(f, parity, jt)
                if k is not None:
                    dve.wait_ge(x2_ready.sem, x2_ready.of(k))
                if f is not None:
                    layer0_finish(f)
                if k is not None:
                    layer3_cut(k)
                    layer3_shift(k)
                if f is not None:
                    layer1_top(f)
                    layer1_columns(f)
                for s in range(U3 + 3):
                    if f is not None and s < U3:
                        layer1_unit(f, parity, 2 * s)
                        layer1_unit(f, parity, 2 * s + 1)
                    if k is not None and 1 <= s <= U3 and s - 1 in DVE_MASKS:
                        layer3_mask(k, 1 - parity, s - 1)
                    if f is not None and s % 4 == 1 and s > 1:
                        layer1_head_out(f, s // 4 - 1)

            schedule(dve, body)


_INS = ["x", "adj", "L0_gnn_W", "L0_gnn_a", "L1_gnn_W", "L1_gnn_a", "L2_gnn_rel_weights", "L2_gnn_self_w",
        "L2_gnn_self_b", "L2_gnn_ln_gamma", "L2_gnn_ln_beta", "L3_gnn_W"]


def kernel(**inputs):
    import numpy as _np
    import concourse.bacc as _bacc
    from concourse import mybir as _mybir
    from concourse.bass_utils import run_bass_kernel_spmd as _run

    nc = _bacc.Bacc("TRN2", target_bir_lowering=False, num_devices=1)
    arrays, args = {}, []
    for name in _INS:
        a = _np.ascontiguousarray(inputs[name])
        arrays[f"in_{name}_dram"] = a
        args.append(nc.dram_tensor(f"in_{name}_dram", a.shape, _mybir.dt.from_np(a.dtype), kind="ExternalInput").ap())
    shape = tuple(inputs["x"].shape)
    args.append(nc.dram_tensor("out_0_dram", shape, _mybir.dt.float32, kind="ExternalOutput").ap())
    graph_stack(nc, *args)
    r = _run(nc, [arrays], core_ids=[0])
    return r.results[0]["out_0_dram"]
```

```python
from contextlib import ExitStack

import concourse.bass as bass
from concourse import mybir

ALU = mybir.AluOpType
ACT = mybir.ActivationFunctionType
AX_X = mybir.AxisListType.X
BF16 = mybir.dt.bfloat16
F32 = mybir.dt.float32

P = 128
SLOPE = 0.2
EPS = 1e-5
BIG = 2.0 ** 100
PARTS = 3


class Signal:

    def __init__(self, sem, per_batch):
        self.sem, self.per_batch = sem, per_batch

    def of(self, b, k=None):
        return b * self.per_batch + (self.per_batch if k is None else k)

    def any_before(self, b):
        return not (isinstance(b, int) and b <= 0)

    def before(self, b):
        return b * self.per_batch


class Steps:

    def __init__(self, sem, per_batch=None):
        self.sem, self.count, self.per_batch = sem, 0, per_batch

    def begin(self, b):
        if self.count and self.per_batch is None:
            self.per_batch = self.count
        assert self.count in (0, self.per_batch), (self.count, self.per_batch)
        self.b, self.count = b, 0

    def step(self):
        self.count += 1
        return self.count if self.per_batch is None else self.b * self.per_batch + self.count


def graph_stack(nc, x, adj, L0_gnn_W, L0_gnn_a, L1_gnn_W, L1_gnn_a, L2_gnn_rel_weights, L2_gnn_self_w,
                L2_gnn_self_b, L2_gnn_ln_gamma, L2_gnn_ln_beta, L3_gnn_W, out):
    NB, N, D = x.shape
    T = N // P
    H1, _, O1 = L1_gnn_W.shape
    H3, _, O3 = L3_gnn_W.shape
    HALF = N // 2
    C1 = O1 + 1
    C3 = O3 + 1
    TURNS = 2 * T - 1
    U1, U3 = H1 * T, H3 * T
    PER = 3
    GROUPS = [range(g, min(g + PER, T)) for g in range(0, T, PER)]
    ROOT = float(O3) ** -0.5
    B_RING, P_RING, P0_RING, R_RING, S_RING = 6, 4, 3, 5, 3
    PV_LAG = 3
    SPREAD = 96
    nc.disable_value_cache = True
    RAMPS = [u for u in range(U1) if u % 4]
    POOL_MASKS = [w for w in range(U3) if w % 4 == 3]
    DVE_MASKS = [w for w in range(U3) if w not in POOL_MASKS]
    assert D == P and H1 * O1 == D and H3 * O3 == D and N == 1024 and (NB - 4) % 3 == 0

    with ExitStack() as ctx:
        def sb(name, shape, dt=F32):
            return ctx.enter_context(nc.sbuf_tensor(name, shape, dt))

        def signal(name, per_batch):
            return Signal(ctx.enter_context(nc.semaphore(name)), per_batch)

        def sem(name):
            return ctx.enter_context(nc.semaphore(name))

        ident = sb("ident", [P, P])
        identb = sb("identb", [P, P], BF16)
        ones = sb("ones", [P, P])
        half_neg = sb("half_neg", [P, T])
        a0_row = sb("a0_row", [P, 2, D])
        a1_row = sb("a1_row", [P, H1, 2 * O1])
        w_tmp = sb("w_tmp", [P, D])
        rhs0 = sb("rhs0", [P, D + 2])
        src0 = sb("src0", [P, P])
        dst0 = sb("dst0", [P, P])
        rhs1 = sb("rhs1", [P, D + 2 * H1])
        pick1 = sb("pick1", [SPREAD, H1, P], BF16)
        self_w = sb("self_w", [P, D])
        rhs2 = sb("rhs2", [P, 2 * D])
        bias2 = sb("bias2", [P, D])
        gamma2 = sb("gamma2", [P, D])
        beta2 = sb("beta2", [P, D])
        rhs3 = sb("rhs3", [P, D])

        AT = sb("AT", [P, 3, T, N], BF16)
        x2 = sb("x2", [P, T, D])

        x0 = sb("x0", [P, T, D])
        T0 = sb("T0", [P, 1])
        T0neg = sb("T0neg", [P, 1])
        T0neg2 = sb("T0neg2", [P, 1])
        v0 = sb("v0", [P, T])
        v0s = sb("v0s", [P, T])
        h0 = sb("h0", [P, T, D])
        weight0 = sb("weight0", [P, P0_RING, N])
        rec0 = sb("rec0", [P, T])
        yf = sb("yf", [P, T, D])
        x1 = sb("x1", [P, T, D])
        h1 = sb("h1", [P, T, H1, C1])
        st1 = sb("st1", [P, T, 2 * H1])
        tmax1 = sb("tmax1", [P, H1])
        tcol1 = sb("tcol1", [H1, 1])
        tdiag1 = sb("tdiag1", [H1, H1])
        T1 = sb("T1", [P, H1])
        tneg1 = sb("tneg1", [P, T, H1])
        tbig1 = sb("tbig1", [P, T, H1])
        dt1 = sb("dt1", [P, T, H1])
        zs1 = sb("zs1", [P, T, H1])
        v1 = sb("v1", [P, 2, T, H1])
        c1 = sb("c1", [P, T, H1])
        vh = sb("vh", [P, T, H1, 2, C1])
        vh_rest = sb("vh_rest", [P, T, H1, 2, C1])
        vh_parts = sb("vh_parts", [P, T, H1, PARTS, 2, C1], BF16)
        s1row = sb("s1row", [P, S_RING, N])
        s1_parts = sb("s1_parts", [SPREAD, N], BF16)
        ramp = sb("ramp", [P, R_RING, N], BF16)
        rec1 = sb("rec1", [P, T, H1])
        xfT = sb("xfT", [P, N])
        x0T = x1T = xfT
        edges = weight0[:].rearrange("p r n -> p (r n)").bitcast(BF16).rearrange(
            "p (r n) -> p r n", n=N)
        elu = weight0[:, 0, :].rearrange("p (t d) -> p t d", t=T)
        c0 = s1row[:, 0, :]
        weight0_sum = s1row[:, 1, :]
        num0T = xfT
        s1_rest = weight0[0:H1, 1, :]
        s1_mid = weight0[0:H1, 2, :].bitcast(BF16)[:, 0:N]
        sumB = vh
        sumA = vh_rest[:, :, :, 0, :]
        fstat = sb("fstat", [P, T, 6])
        fsmall = sb("fsmall", [P, 8, T])

        deg2 = sb("deg2", [P, T])
        yb = sb("yb", [P, T, D])
        x3 = sb("x3", [P, T, D])
        w3 = sb("w3", [P, T * H3, C3])
        cutT = sb("cutT", [P, H3, 2, N], BF16)
        q3 = sb("q3", [P, T * H3])
        qmax3 = sb("qmax3", [P, H3])
        qcol3 = sb("qcol3", [H3, 1])
        qdiag3 = sb("qdiag3", [H3, H3])
        shift3 = sb("shift3", [P, H3])
        weight3 = sb("weight3", [P, P_RING, N])
        rec3 = sb("rec3", [P, T, H3])
        xbT = sb("xbT", [P, N])
        x2T = x3T = xbT
        x4 = yb
        squares3 = yb.rearrange("p t (h o) -> p (t h) o", h=H3)
        cutT_all = cutT[:].rearrange("p h a n -> p (h a n)")
        y2_hi = cutT_all[:, 0:T * (D + 1)].rearrange("p (t d) -> p t d", t=T)
        y2_lo = cutT_all[:, T * (D + 1):T * (3 * D + 1)].rearrange(
            "p (t k d) -> p t k d", t=T, k=2)
        self2 = cutT_all[:, 4 * N:6 * N].bitcast(F32).rearrange("p (t d) -> p t d", t=T)
        rest2 = cutT_all[:, 6 * N:8 * N].bitcast(F32).rearrange("p (t d) -> p t d", t=T)
        rest3 = rest2.rearrange("p t (h o) -> p (t h) o", h=H3)
        ring3 = weight3[:].rearrange("p r n -> p (r n)").bitcast(BF16).rearrange(
            "p (w t k o) -> p w t k o", w=2, t=T * H3, k=4)
        cutA, cutB = ring3[:, 0], ring3[:, 1]
        o3T = cutT[0:C3].rearrange("p h a n -> p (h a n)").bitcast(F32)
        bstat = sb("bstat", [P, T, 6])
        bsmall = sb("bsmall", [P, 8, T])

        fp = ctx.enter_context(nc.psum_tensor("fp", [P, 3, HALF], F32))
        kp = ctx.enter_context(nc.psum_tensor("kp", [P, 5, HALF], F32))
        fp_pair = fp[:, 1:3, :].rearrange("p a b -> p (a b)")
        kp_pair = kp[:, 0:2, :].rearrange("p a b -> p (a b)")

        SUM_A_BANKS = [3, 4, 3]

        def thirds(psum, g, width):
            n = len(GROUPS[g])
            return psum[:, g, 0:n * width].rearrange("p (t c) -> p t c", t=n)

        def tiles(g):
            return slice(GROUPS[g][0], GROUPS[g][-1] + 1)

        w_loaded = sem("w_loaded")
        consts_made = sem("consts_made")
        self_turned = sem("self_turned")
        weights_ready = sem("weights_ready")
        turnstile = sem("turnstile")
        a_loaded = signal("a_loaded", 16)
        x_loaded = signal("x_loaded", 16)
        a_turned = signal("a_turned", TURNS)
        at_ready = signal("at_ready", TURNS)
        x0_turned = signal("x0_turned", 1)
        x0T_ready = signal("x0T_ready", 1)
        t0_spread = signal("t0_spread", 1)
        T0_ready = signal("T0_ready", 1)
        s0_spread = signal("s0_spread", 1)
        z0_ready = signal("z0_ready", 1)
        c0_ready = signal("c0_ready", 1)
        h0_made = signal("h0_made", 1)
        h0_ready = signal("h0_ready", 1)
        weight0_ready = signal("weight0_ready", T)
        weight0_used = signal("weight0_used", T)
        weight0_added = signal("weight0_added", T - 1)
        den0_made = signal("den0_made", 1)
        num0T_ready = signal("num0T_ready", 1)
        num0_turned = signal("num0_turned", 1)
        x1_ready = signal("x1_ready", 1)
        x1_turned = signal("x1_turned", 1)
        x1T_ready = signal("x1T_ready", 1)
        h1_made = signal("h1_made", 1)
        h1_ready = signal("h1_ready", 1)
        st1_ready = signal("st1_ready", 1)
        tmax1_ready = signal("tmax1_ready", 1)
        tmax1_turned = signal("tmax1_turned", 1)
        tdiag1_ready = signal("tdiag1_ready", 1)
        T1_spread = signal("T1_spread", 1)
        z1_ready = signal("z1_ready", 1)
        v1_ready = signal("v1_ready", 1)
        vh_whole = signal("vh_whole", 1)
        vh_first = signal("vh_first", 1)
        vh_rested = signal("vh_rested", 1)
        vh_second = signal("vh_second", 1)
        vh_ready = signal("vh_ready", 1)
        s1_made = signal("s1_made", 1)
        s1_first = signal("s1_first", 1)
        s1_cut = signal("s1_cut", 1)
        sumA_made = signal("sumA_made", 3)
        sumA_ready = signal("sumA_ready", 3)
        s1_spread = signal("s1_spread", 2 * H1)
        s1_ready = signal("s1_ready", 2 * H1)
        ramp_ready = signal("ramp_ready", len(RAMPS))
        edges_ready = signal("edges_ready", U1)
        edges_used = signal("edges_used", U1)
        sumB_ready = signal("sumB_ready", H1)
        elu_min = signal("elu_min", 1)
        elu_exp = signal("elu_exp", 1)
        x2_ready = signal("x2_ready", 1)
        fvar_ready = signal("fvar_ready", 2)
        frstd_ready = signal("frstd_ready", 2)
        x2_turned = signal("x2_turned", 1)
        x2T_ready = signal("x2T_ready", 1)
        y2_made = signal("y2_made", 1)
        y2_ready = signal("y2_ready", 1)
        sum2_made = signal("sum2_made", 1)
        normed2 = signal("normed2", 1)
        bvar_ready = signal("bvar_ready", 3)
        brstd_ready = signal("brstd_ready", 3)
        x3_ready = signal("x3_ready", 1)
        x3_turned = signal("x3_turned", 1)
        x3T_ready = signal("x3T_ready", 1)
        w3_made = signal("w3_made", 1)
        w3_ready = signal("w3_ready", 1)
        cuts_ready = signal("cuts_ready", 1)
        qmax_ready = signal("qmax_ready", 1)
        qmax_turned = signal("qmax_turned", 1)
        qdiag_ready = signal("qdiag_ready", 1)
        q_spread = signal("q_spread", 1)
        shift_ready = signal("shift_ready", 1)
        cut_turned = signal("cut_turned", 2 * H3)
        cutT_act = signal("cutT_act", H3)
        cutT_dve = signal("cutT_dve", H3)
        scores_made = signal("scores_made", 2 * U3)
        exp3_ready = signal("exp3_ready", 2 * U3)
        masked_dve = signal("masked_dve", U3 - len(POOL_MASKS))
        masked_pool = signal("masked_pool", len(POOL_MASKS))
        weight3_used = signal("weight3_used", U3)
        sum3_ready = signal("sum3_ready", H3)
        sum3_turned = signal("sum3_turned", 1)
        o3_ready = signal("o3_ready", 1)
        y4_ready = signal("y4_ready", 1)
        scaled4 = signal("scaled4", 1)
        scaled2 = signal("scaled2", 1)
        affine2_ready = signal("affine2_ready", 1)
        squares_ready = signal("squares_ready", 1)
        lowest_cut = signal("lowest_cut", 1)
        y2_first = signal("y2_first", 1)
        x4_ready = signal("x4_ready", 1)
        stored = signal("stored", 16)
        dve_setup = sem("dve_setup")
        pool_front = sem("pool_front")
        pool_back = sem("pool_back")
        pool_front_last = sem("pool_front_last")
        pool_back_last = sem("pool_back_last")
        dve_front_last = sem("dve_front_last")
        dve_back_last = sem("dve_back_last")
        dve_front = sem("dve_front")
        dve_back = sem("dve_back")

        block = ctx.enter_context(nc.Block())

        def schedule(eng, section_a, section_b):
            section_b(2, 0, None, None)
            section_a(0, 0, None, None)
            section_b(0, 1, 0, None)
            section_a(1, 1, 0, None)
            section_b(1, 2, 1, 0)
            with eng.Fori(2, NB - 4, 3) as i:
                for step in range(3):
                    r = (2 + step) % 3
                    section_a(r, i + step, i + step - 1, i + step - 2)
                    section_b(r, i + step + 1, i + step, i + step - 1)
            section_a((NB - 2) % 3, NB - 2, NB - 3, NB - 4)
            section_b((NB - 2) % 3, NB - 1, NB - 2, NB - 3)
            section_a((NB - 1) % 3, NB - 1, NB - 2, NB - 3)
            section_b((NB - 1) % 3, None, NB - 1, NB - 2)
            section_a(NB % 3, None, NB - 1, NB - 2)
            section_b(NB % 3, None, None, NB - 1)
            section_a((NB + 1) % 3, None, None, NB - 1)

        HALVES_AHEAD = 2 * S_RING
        RAMPS_AHEAD = R_RING
        A_STEPS = U1 // 2 + 1
        B_STEPS = U3 + PV_LAG + 1
        A_PE = dict(turn2=0, turn_back=0, project2=3, sum2=[6, 6, 7, 8, 9, 9, 9, 10],
                    sum1=[11, 13, 13, 13, 14, 15, 17, 17], turn3=21, project3=22, cuts=27, maxima3=28, shift3=29)
        A_ACT = dict(turn2=0, normed2=15, sum1=[15, 17, 19], norm3=20, turn3=21, project3=22, cuts=27)
        A_DVE = dict(finish3=2, columns2=3, columns2_low=4, residual3=6, out2=11, stats2=12, relu2=18,
                     cut3=23, cut3_low=23, lengths3=25, cuts=27, maxima3=28, shift3=30)
        B_PE = dict(turn0=0, targets0=1, sources0=2, project0=4, adjacency=6, unit0=11, finish0=16, turn1=21,
                    project1=22, sources1=23, maxima1=24, spread1=25, spread_s1=28)
        B_ACT = dict(elu=4, turn0=0, prepare0=2, norm2=7, project0=4, adjacency=6, finish0=15, norm1=20, turn1=21,
                     project1=22, sources1=23, exps1=26, cut1=28, cut1_second=30, s1_half=28, ramps=31)
        B_DVE = dict(top0=1, z0=2, finish1=3, divide1=4, elu1=5, unit0=10, finish0=16, top1=23, maxima1=24,
                     shifts1=25, sources1=25, columns1=27, cut1=29, cut1_third=31)
        B_POOL = dict(norm2=7, add0=11, norm1=17)

        def rows(dram, b):
            return dram[bass.ds(b, 1)].rearrange("b (t p) d -> p (b t) d", p=P)

        @block.sync
        def _(sp):
            loads = [
                (rhs0[:, 0:D], L0_gnn_W),
                (a0_row[:], L0_gnn_a.rearrange("(k u) o -> o k u", k=2).broadcast_to([P, 2, D])),
                (rhs1[:, 0:D].rearrange("p (h o) -> p h o", h=H1), L1_gnn_W.rearrange("h f o -> f h o")),
                (a1_row[:], L1_gnn_a.rearrange("h k o -> o h k").broadcast_to([P, H1, 2 * O1])),
                (rhs2[:, 0:D], L2_gnn_rel_weights[1]),
                (self_w[:], L2_gnn_self_w),
                (bias2[:], L2_gnn_self_b.rearrange("(a d) -> a d", a=1).broadcast_to([P, D])),
                (gamma2[:], L2_gnn_ln_gamma.rearrange("(a d) -> a d", a=1).broadcast_to([P, D])),
                (beta2[:], L2_gnn_ln_beta.rearrange("(a d) -> a d", a=1).broadcast_to([P, D])),
                (rhs3[:].rearrange("p (h o) -> p h o", h=H3), L3_gnn_W.rearrange("h f o -> f h o")),
            ]
            for dst, src in loads:
                sp.dma_start(dst, src).then_inc(w_loaded, 16)

            def load_x(b):
                if x1_ready.any_before(b):
                    sp.wait_ge(x1_ready.sem, x1_ready.before(b))
                sp.sem_inc(turnstile, 1)
                sp.dma_start(x0[:], rows(x, b)).then_inc(x_loaded.sem, 16)

            def section_a(r, f, k, m):
                if m is not None:
                    sp.wait_ge(x4_ready.sem, x4_ready.of(m))
                    sp.sem_inc(turnstile, 1)
                    sp.dma_start(rows(out, m), x4[:]).then_inc(stored.sem, 16)

            def section_b(r, n, f, k):
                if n is not None:
                    load_x(n)

            schedule(sp, section_a, section_b)
            sp.wait_ge(stored.sem, stored.of(NB - 1))

        @block.gpsimd
        def _(pool):
            pool.memset(ones[:], 1.0).then_inc(consts_made, 1)
            pool.memset(half_neg[:], -0.5).then_inc(consts_made, 1)
            pool.wait_ge(consts_made, 2)
            pool.affine_select(out=ident[:], in_=ones[:], compare_op=ALU.is_equal, fill=0.0, base=0,
                               pattern=[[-1, P]], channel_multiplier=1).then_inc(consts_made, 1)

            front, back = Steps(pool_front), Steps(pool_back)
            front_last, back_last = Steps(pool_front_last), Steps(pool_back_last, 1)

            def rstd(step, var_ready, rstd_ready, small, b, n):
                pool.wait_ge(var_ready.sem, var_ready.of(b, n + 1))
                pool.tensor_tensor(small[:, 5, :], small[:, 4, :], half_neg[:], ALU.pow).then_inc(step.sem, 1)
                pool.wait_ge(step.sem, step.step())
                pool.tensor_tensor(small[:, 6, :], small[:, 0, :], small[:, 5, :], ALU.mult) \
                    .then_inc(rstd_ready.sem, 1)

            def add_weight0(b, jt):
                pool.wait_ge(weight0_ready.sem, weight0_ready.of(b, jt + 1))
                so_far = weight0[:, 0, :] if jt == 1 else weight0_sum
                if jt > 1:
                    pool.wait_ge(weight0_added.sem, weight0_added.of(b, jt - 1))
                pool.tensor_tensor(weight0_sum, so_far, weight0[:, jt % P0_RING, :], ALU.add) \
                    .then_inc(weight0_added.sem, 1)

            def layer3_mask(b, third, w):
                pool.wait_ge(exp3_ready.sem, exp3_ready.of(b, 2 * w + 2))
                tile = weight3[:, w % P_RING, :]
                pool.tensor_tensor(tile, tile, AT[:, third, w % T, :], ALU.mult).then_inc(masked_pool.sem, 1)

            def load_adjacency(b, third):
                if not isinstance(b, int) or b >= 3:
                    pool.wait_ge(sum2_made.sem, sum2_made.of(b - 3))
                    pool.wait_ge(masked_dve.sem, masked_dve.of(b - 3))
                    pool.wait_ge(masked_pool.sem, masked_pool.of(b - 3))
                pool.sem_inc(turnstile, 1)
                pool.dma_start(AT[:, third], adj[bass.ds(b, 1)].rearrange("b (t p) n -> p (b t) n", p=P)) \
                    .then_inc(a_loaded.sem, 16)

            def layer3_residual(b):
                pool.wait_ge(o3_ready.sem, o3_ready.of(b))
                pool.tensor_tensor(yb[:], yb[:], x3[:], ALU.add).then_inc(y4_ready.sem, 1)

            def layer3_normalise(b):
                pool.wait_ge(brstd_ready.sem, brstd_ready.of(b, 3))
                pool.tensor_tensor(yb[:], yb[:], bsmall[:, 5, :].unsqueeze(2).broadcast_to([P, T, D]), ALU.mult) \
                    .then_inc(scaled4.sem, 1)
                pool.wait_ge(scaled4.sem, scaled4.of(b))
                pool.tensor_tensor(x4[:], yb[:], bsmall[:, 6, :].unsqueeze(2).broadcast_to([P, T, D]), ALU.add) \
                    .then_inc(x4_ready.sem, 1)

            def layer2_affine(b):
                pool.wait_ge(normed2.sem, normed2.of(b))
                pool.tensor_tensor(yb[:], yb[:], gamma2[:].unsqueeze(1).broadcast_to([P, T, D]), ALU.mult) \
                    .then_inc(scaled2.sem, 1)
                pool.wait_ge(scaled2.sem, scaled2.of(b))
                pool.tensor_tensor(yb[:], yb[:], beta2[:].unsqueeze(1).broadcast_to([P, T, D]), ALU.add) \
                    .then_inc(affine2_ready.sem, 1)

            def layer3_squares(b):
                pool.wait_ge(w3_ready.sem, w3_ready.of(b))
                pool.tensor_tensor(squares3, w3[:, :, 0:O3], w3[:, :, 0:O3], ALU.mult).then_inc(squares_ready.sem, 1)

            def layer3_cut_lowest(b):
                pool.wait_ge(cuts_ready.sem, cuts_ready.of(b))
                pool.tensor_tensor(cutA[:, :, 1, :], rest3, cutA[:, :, 0, :], ALU.subtract).then_inc(lowest_cut.sem, 1)

            load_adjacency(0, 0)

            def section_a(r, f, k, m):
                if f is not None and not (isinstance(f, int) and f + 1 >= NB):
                    load_adjacency(f + 1, (r + 1) % 3)
                if m is not None:
                    back_last.begin(m)
                if k is not None:
                    back.begin(k)
                if m is not None:
                    layer3_residual(m)
                    rstd(back_last, bvar_ready, brstd_ready, bsmall, m, 2)
                    layer3_normalise(m)
                if k is not None:
                    rstd(back, bvar_ready, brstd_ready, bsmall, k, 0)
                    layer2_affine(k)
                    rstd(back, bvar_ready, brstd_ready, bsmall, k, 1)
                    layer3_squares(k)
                    layer3_cut_lowest(k)

            def section_b(r, n, f, k):
                if f is not None:
                    front_last.begin(f)
                if n is not None:
                    front.begin(n)
                for s in range(B_STEPS):
                    if f is not None and s == B_POOL["norm2"]:
                        rstd(front_last, fvar_ready, frstd_ready, fsmall, f, 1)
                    for jt in range(1, T):
                        if n is not None and s == B_POOL["add0"] + (jt - 1) // 2:
                            add_weight0(n, jt)
                    if n is not None and s == B_POOL["norm1"]:
                        rstd(front, fvar_ready, frstd_ready, fsmall, n, 0)
                    if k is not None and s - 1 in POOL_MASKS:
                        layer3_mask(k, (r + 2) % 3, s - 1)

            schedule(pool, section_a, section_b)

        @block.tensor
        def _(pe):
            def turn_rows(src, dst, done):
                for t in range(T):
                    last = pe.transpose(dst[:, t * P:(t + 1) * P], src[:, t, :], ident[:])
                last.then_inc(done.sem, 1)

            def project(xT, rhs, width, dst, done):
                for g in range(len(GROUPS)):
                    for n, t in enumerate(GROUPS[g]):
                        last = pe.matmul(dst[:, g, n * width:(n + 1) * width], xT[:, t * P:(t + 1) * P], rhs,
                                         start=True, stop=True)
                last.then_inc(done.sem, 1)

            def turn_adjacency(b, third, q):
                jt, row = q // 2, q % 2
                if q == 0:
                    pe.wait_ge(a_loaded.sem, a_loaded.of(b))
                    pe.wait_ge(h0_ready.sem, h0_ready.of(b))
                if q >= 3:
                    pe.wait_ge(at_ready.sem, at_ready.of(b, q - 2))
                dst = fp[:, q % 3, :].bitcast(BF16)
                for t in range(jt + row, T):
                    src = AT[:, third, jt, t * P:(t + 1) * P] if row else AT[:, third, t, jt * P:(jt + 1) * P]
                    last = pe.transpose(dst[:, t * P:(t + 1) * P], src, identb[:])
                last.then_inc(a_turned.sem, 1)

            def spread(lhsT, rhs, dst):
                for n in range(2):
                    last = pe.matmul(dst[:, n * HALF:(n + 1) * HALF], lhsT, rhs[:, n * HALF:(n + 1) * HALF],
                                     start=True, stop=True)
                return last

            def layer0_turn(b):
                pe.wait_ge(x_loaded.sem, x_loaded.of(b))
                if sumB_ready.any_before(b):
                    pe.wait_ge(sumB_ready.sem, sumB_ready.before(b))
                turn_rows(x0, fp_pair, x0_turned)

            def layer0_targets(b):
                pe.wait_ge(x0T_ready.sem, x0T_ready.of(b))
                spread(dst0[:], x0T, fp_pair).then_inc(t0_spread.sem, 1)

            def layer0_sources(b):
                pe.wait_ge(T0_ready.sem, T0_ready.of(b))
                spread(src0[:], x0T, fp_pair).then_inc(s0_spread.sem, 1)

            def layer0_project(b):
                pe.wait_ge(z0_ready.sem, z0_ready.of(b))
                project(x0T, rhs0[:], D + 2, fp, h0_made)

            def layer0_unit(b, jt):
                if jt == 0:
                    pe.wait_ge(at_ready.sem, at_ready.of(b))
                pe.wait_ge(weight0_ready.sem, weight0_ready.of(b, jt + 1))
                for n in range(2):
                    last = pe.matmul(fp[:, 1 + n, :], h0[:, jt, :], weight0[:, jt % P0_RING, n * HALF:(n + 1) * HALF],
                                     start=(jt == 0), stop=(jt == T - 1))
                last.then_inc(weight0_used.sem, 1)

            def layer0_finish(b):
                pe.wait_ge(num0T_ready.sem, num0T_ready.of(b))
                for t in range(T):
                    last = pe.transpose(fp_pair[:, t * P:(t + 1) * P], num0T[:, t * P:(t + 1) * P], ident[:])
                last.then_inc(num0_turned.sem, 1)
                pe.wait_ge(weight0_added.sem, weight0_added.of(b))
                for t in range(T):
                    last = pe.matmul(fp[:, 0, t:t + 1], weight0_sum[:, t * P:(t + 1) * P], ones[:, 0:1],
                                     start=True, stop=True)
                last.then_inc(den0_made.sem, 1)

            def layer1_turn(b):
                pe.wait_ge(x1_ready.sem, x1_ready.of(b))
                turn_rows(x1, fp_pair, x1_turned)

            def layer1_project(b):
                pe.wait_ge(x1T_ready.sem, x1T_ready.of(b))
                project(x1T, rhs1[:], D + 2 * H1, fp, h1_made)

            def layer1_sources(b):
                pe.wait_ge(h1_ready.sem, h1_ready.of(b))
                for n in range(2):
                    last = pe.matmul(fp[0:H1, 1 + n, :], rhs1[:, D:D + H1], x1T[:, n * HALF:(n + 1) * HALF],
                                     start=True, stop=True)
                last.then_inc(s1_made.sem, 1)

            def layer1_turn_maxima(b):
                pe.wait_ge(tmax1_ready.sem, tmax1_ready.of(b))
                pe.transpose(fp[0:H1, 0, 0:P], tmax1[:], ident[:]).then_inc(tmax1_turned.sem, 1)

            def layer1_spread_maxima(b):
                pe.wait_ge(tdiag1_ready.sem, tdiag1_ready.of(b))
                pe.matmul(fp[:, 0, P:P + H1], ones[0:H1, :], tdiag1[:], start=True, stop=True) \
                    .then_inc(T1_spread.sem, 1)

            def layer1_sum_all(b, third, t):
                if t == 0:
                    pe.wait_ge(vh_ready.sem, vh_ready.of(b))
                    if y2_ready.any_before(b):
                        pe.wait_ge(y2_ready.sem, y2_ready.before(b))
                if t == 2 * PER:
                    pe.wait_ge(sumA_ready.sem, sumA_ready.of(b, 1))
                n = t % PER
                for jt in range(T):
                    for k in range(PARTS):
                        last = pe.matmul(kp[:, SUM_A_BANKS[t // PER], n * H1 * C1:(n + 1) * H1 * C1].rearrange(
                                             "p (h c) -> p h c", h=H1),
                                         AT[:, third, jt, t * P:(t + 1) * P], vh_parts[:, jt, :, k, 1, :],
                                         start=(jt == 0 and k == 0), stop=(jt == T - 1 and k == PARTS - 1))
                if t in (2, 5, T - 1):
                    last.then_inc(sumA_made.sem, 1)

            def spread_s1(b, n):
                if n:
                    pe.wait_ge(s1_ready.sem, s1_ready.of(b, n))
                else:
                    pe.wait_ge(z1_ready.sem, z1_ready.of(b))
                    pe.wait_ge(s1_cut.sem, s1_cut.of(b))
                h, half = n // 2, n % 2
                pe.matmul(fp[:, 0, :], pick1[:, h, :], s1_parts[:, half * HALF:(half + 1) * HALF],
                          start=True, stop=True).then_inc(s1_spread.sem, 1)

            def layer1_unit(b, u):
                h, jt = u // T, u % T
                pe.wait_ge(edges_ready.sem, edges_ready.of(b, u + 1))
                if jt == 0 and h:
                    pe.wait_ge(sumB_ready.sem, sumB_ready.of(b, h))
                if jt == 0 and h == 0:
                    pe.wait_ge(vh_ready.sem, vh_ready.of(b))
                for t in range(T):
                    col = (t % 4) * P
                    last = pe.matmul(fp[:, 1 + t // 4, col:col + 2 * PARTS * C1],
                                     edges[:, u % B_RING, t * P:(t + 1) * P],
                                     vh_parts[:, jt, h, :, :, :].rearrange("p k a c -> p (k a c)"),
                                     start=(jt == 0 and t % 4 == 0), stop=(jt == T - 1), skip_group_check=True)
                last.then_inc(edges_used.sem, 1)

            def layer2_turn(b):
                pe.wait_ge(x2_ready.sem, x2_ready.of(b))
                if sum3_ready.any_before(b):
                    pe.wait_ge(sum3_ready.sem, sum3_ready.before(b))
                turn_rows(x2, kp_pair, x2_turned)

            def layer2_project(b):
                pe.wait_ge(x2T_ready.sem, x2T_ready.of(b))
                if o3_ready.any_before(b):
                    pe.wait_ge(o3_ready.sem, o3_ready.before(b))
                for t in range(T):
                    last = pe.matmul(kp[:, 1 + t // 2, (t % 2) * 2 * D:(t % 2 + 1) * 2 * D],
                                     x2T[:, t * P:(t + 1) * P], rhs2[:], start=True, stop=True)
                last.then_inc(y2_made.sem, 1)

            def layer2_sum(b, third, t):
                if t == 0:
                    pe.wait_ge(y2_ready.sem, y2_ready.of(b))
                g, col = t // PER, t % PER * (D + 1)
                for jt in range(T):
                    lhsT = AT[:, third, jt, t * P:(t + 1) * P]
                    pe.matmul(kp[:, g, col:col + D + 1], lhsT, y2_hi[:, jt, :], start=(jt == 0), stop=False,
                              skip_group_check=True)
                    for k in range(2):
                        last = pe.matmul(kp[:, g, col:col + D], lhsT, y2_lo[:, jt, k, :], start=False,
                                         stop=(jt == T - 1 and k == 1), skip_group_check=True)
                if t == T - 1:
                    last.then_inc(sum2_made.sem, 1)

            def layer3_turn(b):
                pe.wait_ge(x3_ready.sem, x3_ready.of(b))
                turn_rows(x3, kp_pair, x3_turned)

            def layer3_project(b):
                pe.wait_ge(x3T_ready.sem, x3T_ready.of(b))
                for t in range(T):
                    last = pe.matmul(kp[:, 3 + t // 4, (t % 4) * D:(t % 4 + 1) * D], x3T[:, t * P:(t + 1) * P],
                                     rhs3[:], start=True, stop=True)
                last.then_inc(w3_made.sem, 1)

            def layer3_turn_maxima(b):
                pe.wait_ge(qmax_ready.sem, qmax_ready.of(b))
                pe.transpose(kp[0:H3, 0, 0:P], qmax3[:], ident[:]).then_inc(qmax_turned.sem, 1)

            def layer3_spread_maxima(b):
                pe.wait_ge(qdiag_ready.sem, qdiag_ready.of(b))
                pe.matmul(kp[:, 0, P:P + H3], ones[0:H3, :], qdiag3[:], start=True, stop=True) \
                    .then_inc(q_spread.sem, 1)

            def layer3_turn_cuts(b, h):
                pe.wait_ge(cuts_ready.sem, cuts_ready.of(b))
                pe.wait_ge(lowest_cut.sem, lowest_cut.of(b))
                for which, cut in enumerate((cutA, cutB)):
                    if h >= 2:
                        copied = cutT_dve if which else cutT_act
                        pe.wait_ge(copied.sem, copied.of(b, h - 1))
                    dst = kp[:, 1 + (2 * h + which) % 4, :].bitcast(BF16)
                    rows_cut = cut.rearrange("p (t h) k o -> p t h (k o)", h=H3)
                    for t in range(T):
                        last = pe.transpose(dst[:, t * P:(t + 1) * P], rows_cut[:, t, h, :], identb[:])
                    last.then_inc(cut_turned.sem, 1)

            def layer3_scores(b, w):
                h, jt = w // T, w % T
                if w == 0:
                    pe.wait_ge(cutT_act.sem, cutT_act.of(b))
                    pe.wait_ge(cutT_dve.sem, cutT_dve.of(b))
                    pe.wait_ge(shift_ready.sem, shift_ready.of(b))
                tile = slice(jt * P, (jt + 1) * P)
                for n in range(2):
                    q = 2 * w + n
                    if q >= 3:
                        pe.wait_ge(exp3_ready.sem, exp3_ready.of(b, q - 2))
                    cols = slice(n * HALF, (n + 1) * HALF)
                    pe.matmul(kp[:, 2 + q % 3, :], cutT[:, h, 1, tile], cutT[:, h, 0, cols], start=True, stop=False)
                    pe.matmul(kp[:, 2 + q % 3, :], cutT[0:2 * O3, h, 0, tile], cutT[0:2 * O3, h, 1, cols],
                              start=False, stop=True).then_inc(scores_made.sem, 1)

            def layer3_values(b, w):
                h, jt = w // T, w % T
                if w in POOL_MASKS:
                    pe.wait_ge(masked_pool.sem, masked_pool.of(b, POOL_MASKS.index(w) + 1))
                else:
                    pe.wait_ge(masked_dve.sem, masked_dve.of(b, DVE_MASKS.index(w) + 1))
                if jt == 0 and h:
                    pe.wait_ge(sum3_ready.sem, sum3_ready.of(b, h))
                for n in range(2):
                    last = pe.matmul(kp[0:C3, n, :], w3[:, jt * H3 + h, :],
                                     weight3[:, w % P_RING, n * HALF:(n + 1) * HALF],
                                     start=(jt == 0), stop=(jt == T - 1))
                last.then_inc(weight3_used.sem, 1)

            def layer3_turn_back(b):
                pe.wait_ge(sum3_ready.sem, sum3_ready.of(b))
                pe.sem_inc(turnstile, 1)
                for g in range(len(GROUPS)):
                    for n, t in enumerate(GROUPS[g]):
                        for h in range(H3):
                            col = (n * H3 + h) * C3
                            last = pe.transpose(kp[:, 2 + g, col:col + C3], o3T[:, h * N + t * P:h * N + (t + 1) * P],
                                                ident[0:C3, 0:C3])
                last.then_inc(sum3_turned.sem, 1)

            pe.wait_ge(w_loaded, 160)
            pe.wait_ge(consts_made, 3)
            pe.transpose(fp[:, 0, 0:P], self_w[:], ident[:]).then_inc(self_turned, 1)
            pe.wait_ge(weights_ready, 1)

            def section_a(r, f, k, m):
                for s in range(A_STEPS):
                    if k is not None and s == A_PE["turn2"]:
                        layer2_turn(k)
                    if m is not None and s == A_PE["turn_back"]:
                        layer3_turn_back(m)
                    if k is not None and s == A_PE["project2"]:
                        layer2_project(k)
                    for t in range(T):
                        if k is not None and s == A_PE["sum2"][t]:
                            layer2_sum(k, (r + 2) % 3, t)
                    for t in range(T):
                        if f is not None and s == A_PE["sum1"][t]:
                            layer1_sum_all(f, r % 3, t)
                    if k is not None and s == A_PE["turn3"]:
                        layer3_turn(k)
                    if k is not None and s == A_PE["project3"]:
                        if f is not None:
                            pe.wait_ge(sumA_ready.sem, sumA_ready.of(f))
                        layer3_project(k)
                    if k is not None and A_PE["cuts"] <= s < A_PE["cuts"] + H3:
                        layer3_turn_cuts(k, s - A_PE["cuts"])
                    if k is not None and s == A_PE["maxima3"]:
                        layer3_turn_maxima(k)
                    if k is not None and s == A_PE["shift3"]:
                        layer3_spread_maxima(k)
                    if f is not None and s >= 1:
                        layer1_unit(f, 2 * s - 2)
                        layer1_unit(f, 2 * s - 1)
                    if f is not None and s % 4 == 1 and S_RING <= s // 4 + 2 < H1:
                        spread_s1(f, 2 * (s // 4) + 4)
                    if f is not None and s % 4 == 0 and S_RING <= s // 4 + 1 < H1:
                        spread_s1(f, 2 * (s // 4) + 3)

            def section_b(r, n, f, k):
                third = (r + 1) % 3
                for s in range(B_STEPS):
                    if k is not None and s < U3:
                        layer3_scores(k, s)
                    if n is not None:
                        if s == B_PE["turn0"]:
                            layer0_turn(n)
                        if s == B_PE["targets0"]:
                            layer0_targets(n)
                        if s == B_PE["sources0"]:
                            layer0_sources(n)
                        if s == B_PE["project0"]:
                            layer0_project(n)
                        for q in range(TURNS):
                            if s == B_PE["adjacency"] + q // 4 and q % 4 < 2:
                                turn_adjacency(n, third, q)
                        for jt in range(0, T, 2):
                            if s == B_PE["unit0"] + jt // 2:
                                layer0_unit(n, jt)
                        if s == B_PE["finish0"]:
                            layer0_finish(n)
                        if s == B_PE["turn1"]:
                            layer1_turn(n)
                        if s == B_PE["project1"]:
                            layer1_project(n)
                        if s == B_PE["sources1"]:
                            layer1_sources(n)
                        if s == B_PE["maxima1"]:
                            layer1_turn_maxima(n)
                        if s == B_PE["spread1"]:
                            layer1_spread_maxima(n)
                    if k is not None and PV_LAG <= s < U3 + PV_LAG:
                        layer3_values(k, s - PV_LAG)
                    if n is not None:
                        for q in range(TURNS):
                            if s == B_PE["adjacency"] + q // 4 and q % 4 >= 2:
                                turn_adjacency(n, third, q)
                        for jt in range(1, T, 2):
                            if s == B_PE["unit0"] + jt // 2:
                                layer0_unit(n, jt)
                        if B_PE["spread_s1"] <= s < B_PE["spread_s1"] + HALVES_AHEAD:
                            spread_s1(n, s - B_PE["spread_s1"])

            schedule(pe, section_a, section_b)

        @block.scalar
        def _(act):
            def copy(dst, src):
                return act.activation(dst, src, ACT.Copy)

            def adjacency_back(b, third, q):
                jt, row = q // 2, q % 2
                act.wait_ge(a_turned.sem, a_turned.of(b, min(2 * jt + 2, TURNS)))
                src = fp[:, q % 3, :].bitcast(BF16)[:, (jt + row) * P:N]
                dst = AT[:, third, jt + 1:T, jt * P:(jt + 1) * P] if row else AT[:, third, jt, jt * P:N]
                if row:
                    src = src.rearrange("p (t i) -> p t i", i=P)
                copy(dst, src).then_inc(at_ready.sem, 1)

            def normalise(rstd_ready, done, b, n, y, dst, small):
                act.wait_ge(rstd_ready.sem, rstd_ready.of(b, n + 1))
                for t in range(T):
                    last = act.activation(dst[:, t, :], y[:, t, :], ACT.Identity, bias=small[:, 6, t:t + 1],
                                          scale=small[:, 5, t:t + 1])
                last.then_inc(done.sem, 1)

            def layer0_turn(b):
                act.wait_ge(x0_turned.sem, x0_turned.of(b))
                copy(x0T[:], fp_pair).then_inc(x0T_ready.sem, 1)

            def layer0_prepare(b):
                act.wait_ge(z0_ready.sem, z0_ready.of(b))
                act.activation(c0, c0, ACT.Exp, scale=-(1.0 - SLOPE)).then_inc(c0_ready.sem, 1)

            def layer0_project(b):
                act.wait_ge(h0_made.sem, h0_made.of(b))
                for g in range(len(GROUPS)):
                    src = thirds(fp, g, D + 2)
                    act.activation(v0[:, tiles(g)], src[:, :, D + 1], ACT.Exp, bias=T0neg[:])
                    act.activation(v0s[:, tiles(g)], src[:, :, D + 1], ACT.Exp, bias=T0neg2[:], scale=SLOPE)
                    last = copy(h0[:, tiles(g), :], src[:, :, 0:D])
                last.then_inc(h0_ready.sem, 1)

            def layer0_finish(b):
                act.wait_ge(weight0_used.sem, weight0_used.of(b))
                copy(num0T[:], fp_pair).then_inc(num0T_ready.sem, 1)

            def layer1_turn(b):
                act.wait_ge(x1_turned.sem, x1_turned.of(b))
                copy(x1T[:], fp_pair).then_inc(x1T_ready.sem, 1)

            def layer1_project(b):
                act.wait_ge(h1_made.sem, h1_made.of(b))
                for g in range(len(GROUPS)):
                    last = copy(st1[:, tiles(g), :], thirds(fp, g, D + 2 * H1)[:, :, D:D + 2 * H1])
                last.then_inc(st1_ready.sem, 1)
                for g in range(len(GROUPS)):
                    for n, t in enumerate(GROUPS[g]):
                        last = copy(h1[:, t, :, 0:O1], thirds(fp, g, D + 2 * H1)[:, n, 0:D].rearrange(
                            "p (h o) -> p h o", h=H1))
                last.then_inc(h1_ready.sem, 1)

            def layer1_sources(b):
                act.wait_ge(s1_made.sem, s1_made.of(b))
                copy(s1_parts[0:H1, :], fp_pair[0:H1, :]).then_inc(s1_first.sem, 1)

            def layer1_exps(b):
                act.wait_ge(z1_ready.sem, z1_ready.of(b))
                act.activation(v1[:, 0], dt1[:], ACT.Exp)
                act.activation(v1[:, 1], dt1[:], ACT.Exp, scale=SLOPE)
                act.activation(c1[:], zs1[:], ACT.Exp, scale=-(1.0 - SLOPE)).then_inc(v1_ready.sem, 1)

            def layer1_cut(b):
                flat = "p t h a c -> p (t h) (a c)"
                act.wait_ge(vh_whole.sem, vh_whole.of(b))
                copy(vh_parts[:, :, :, 0, :, :].rearrange(flat), vh[:].rearrange(flat)).then_inc(vh_first.sem, 1)

            def layer1_cut_second(b):
                flat = "p t h a c -> p (t h) (a c)"
                act.wait_ge(vh_rested.sem, vh_rested.of(b))
                copy(vh_parts[:, :, :, 1, :, :].rearrange(flat), vh_rest[:].rearrange(flat)) \
                    .then_inc(vh_second.sem, 1)

            def layer1_sum_all(b, g):
                act.wait_ge(sumA_made.sem, sumA_made.of(b, g + 1))
                n = len(GROUPS[g])
                copy(sumA[:, tiles(g)], kp[:, SUM_A_BANKS[g], 0:n * H1 * C1].rearrange(
                         "p (t h c) -> p t h c", t=n, h=H1)) \
                    .then_inc(sumA_ready.sem, 1)

            def s1_half(b, n):
                h, half = n // 2, n % 2
                act.wait_ge(s1_spread.sem, s1_spread.of(b, n + 1))
                if h >= S_RING:
                    act.wait_ge(edges_ready.sem, edges_ready.of(b, (h - S_RING + 1) * T))
                copy(s1row[:, h % S_RING, half * HALF:(half + 1) * HALF], fp[:, 0, :]).then_inc(s1_ready.sem, 1)

            def ramp_unit(b, u):
                h, jt, r = u // T, u % T, RAMPS.index(u)
                if r >= R_RING:
                    act.wait_ge(edges_ready.sem, edges_ready.of(b, RAMPS[r - R_RING] + 1))
                act.wait_ge(s1_ready.sem, s1_ready.of(b, 2 * h + 2))
                act.activation(ramp[:, r % R_RING, :], s1row[:, h % S_RING, :], ACT.Relu, bias=tbig1[:, jt, h:h + 1],
                               scale=BIG).then_inc(ramp_ready.sem, 1)

            def layer1_finish(b):
                act.wait_ge(elu_min.sem, elu_min.of(b))
                act.activation(elu, elu, ACT.Exp).then_inc(elu_exp.sem, 1)

            def layer2_turn(b):
                act.wait_ge(x2_turned.sem, x2_turned.of(b))
                copy(x2T[:], kp_pair).then_inc(x2T_ready.sem, 1)

            def layer3_turn(b):
                act.wait_ge(x3_turned.sem, x3_turned.of(b))
                copy(x3T[:], kp_pair).then_inc(x3T_ready.sem, 1)

            def layer3_project(b):
                act.wait_ge(w3_made.sem, w3_made.of(b))
                src = kp[:, 3:5, :].rearrange("p a (b o) -> p (a b) o", o=O3)
                copy(cutA[:, :, 2, :], src)
                copy(w3[:, :, 0:O3], src).then_inc(w3_ready.sem, 1)

            def layer3_turn_cuts(b, h):
                act.wait_ge(cut_turned.sem, cut_turned.of(b, 2 * h + 1))
                copy(cutT[:, h, 0, :], kp[:, 1 + (2 * h) % 4, :].bitcast(BF16)).then_inc(cutT_act.sem, 1)

            def layer3_exp(b, w):
                h = w // T
                if w >= P_RING:
                    act.wait_ge(weight3_used.sem, weight3_used.of(b, w - P_RING + 1))
                if w == 0:
                    act.wait_ge(shift_ready.sem, shift_ready.of(b))
                for n in range(2):
                    q = 2 * w + n
                    act.wait_ge(scores_made.sem, scores_made.of(b, q + 1))
                    act.activation(weight3[:, w % P_RING, n * HALF:(n + 1) * HALF], kp[:, 2 + q % 3, :], ACT.Exp,
                                   bias=shift3[:, h:h + 1], scale=ROOT).then_inc(exp3_ready.sem, 1)

            def layer3_head_out(b, h):
                act.wait_ge(weight3_used.sem, weight3_used.of(b, (h + 1) * T))
                copy(o3T[:, h * N:(h + 1) * N], kp_pair[0:C3, :]).then_inc(sum3_ready.sem, 1)

            act.wait_ge(weights_ready, 1)

            def section_a(r, f, k, m):
                ramps = RAMPS_AHEAD
                for s in range(A_STEPS):
                    if f is not None and s % 4 == 3 and S_RING <= (s + 5) // 4 < H1:
                        s1_half(f, 2 * ((s + 5) // 4))
                    if f is not None and s % 4 == 1 and S_RING <= (s + 3) // 4 < H1:
                        s1_half(f, 2 * ((s + 3) // 4) + 1)
                    while f is not None and ramps < len(RAMPS) and RAMPS[ramps] <= 2 * s + 3:
                        ramp_unit(f, RAMPS[ramps])
                        ramps += 1
                    for g in range(len(GROUPS)):
                        if f is not None and s == A_ACT["sum1"][g]:
                            layer1_sum_all(f, g)
                    if k is not None and s == A_ACT["turn2"]:
                        layer2_turn(k)
                    if k is not None:
                        if s == A_ACT["normed2"]:
                            normalise(brstd_ready, normed2, k, 0, yb, yb, bsmall)
                        if s == A_ACT["norm3"]:
                            normalise(brstd_ready, x3_ready, k, 1, yb, x3, bsmall)
                        if s == A_ACT["turn3"]:
                            layer3_turn(k)
                        if s == A_ACT["project3"]:
                            layer3_project(k)
                        if A_ACT["cuts"] <= s < A_ACT["cuts"] + H3:
                            layer3_turn_cuts(k, s - A_ACT["cuts"])

            def section_b(r, n, f, k):
                third = (r + 1) % 3
                for s in range(B_STEPS):
                    if k is not None and s >= T and (s - PV_LAG) % T == 0:
                        layer3_head_out(k, (s - PV_LAG) // T - 1)
                    if k is not None and s < U3:
                        layer3_exp(k, s)
                    if f is not None and s == B_ACT["elu"]:
                        layer1_finish(f)
                    if f is not None and s == B_ACT["norm2"]:
                        normalise(frstd_ready, x2_ready, f, 1, yf, x2, fsmall)
                    if n is not None:
                        if s == B_ACT["turn0"]:
                            layer0_turn(n)
                        if s == B_ACT["prepare0"]:
                            layer0_prepare(n)
                        if s == B_ACT["project0"]:
                            layer0_project(n)
                        for q in range(TURNS):
                            if s == B_ACT["adjacency"] + q // 4:
                                adjacency_back(n, third, q)
                        if s == B_ACT["finish0"]:
                            layer0_finish(n)
                        if s == B_ACT["norm1"]:
                            normalise(frstd_ready, x1_ready, n, 0, yf, x1, fsmall)
                        if s == B_ACT["turn1"]:
                            layer1_turn(n)
                        if s == B_ACT["project1"]:
                            layer1_project(n)
                        if s == B_ACT["sources1"]:
                            layer1_sources(n)
                        if s == B_ACT["exps1"]:
                            layer1_exps(n)
                        if s == B_ACT["cut1"]:
                            layer1_cut(n)
                        if s == B_ACT["cut1_second"]:
                            layer1_cut_second(n)
                    if n is not None and B_ACT["s1_half"] <= s < B_ACT["s1_half"] + HALVES_AHEAD:
                        s1_half(n, s - B_ACT["s1_half"])
                    for r_ahead in range(RAMPS_AHEAD):
                        if n is not None and s == B_ACT["ramps"] + r_ahead // 2:
                            ramp_unit(n, RAMPS[r_ahead])

            schedule(act, section_a, section_b)

        @block.vector
        def _(dve):
            front, back = Steps(dve_front), Steps(dve_back)
            front_last, back_last = Steps(dve_front_last), Steps(dve_back_last, 5)

            def spread_over(col, width):
                return col.unsqueeze(len(col.shape)).broadcast_to(list(col.shape) + [width])

            def per_tile(row):
                return row.unsqueeze(1).broadcast_to([P, T, D])

            def layer_stats(chain, y, stat, small, var_ready):
                for t in range(T):
                    last = dve.bn_stats(stat[:, t, :], y[:, t, :])
                last.then_inc(chain.sem, 1)
                dve.wait_ge(chain.sem, chain.step())
                dve.tensor_tensor(small[:, 3, :], stat[:, :, 1], stat[:, :, 4], ALU.add)
                dve.tensor_tensor(small[:, 1, :], stat[:, :, 1], stat[:, :, 4], ALU.subtract)
                dve.tensor_tensor(small[:, 2, :], stat[:, :, 2], stat[:, :, 5], ALU.add).then_inc(chain.sem, 1)
                dve.wait_ge(chain.sem, chain.step())
                dve.tensor_scalar(small[:, 0, :], small[:, 3, :], -0.5, None, ALU.mult)
                dve.scalar_tensor_tensor(out=small[:, 7, :], in0=small[:, 1, :], scalar=D / 4.0,
                                         in1=small[:, 1, :], op0=ALU.mult, op1=ALU.mult).then_inc(chain.sem, 1)
                dve.wait_ge(chain.sem, chain.step())
                dve.tensor_tensor(small[:, 2, :], small[:, 7, :], small[:, 2, :], ALU.add).then_inc(chain.sem, 1)
                dve.wait_ge(chain.sem, chain.step())
                dve.tensor_scalar(small[:, 4, :], small[:, 2, :], 1.0 / D, EPS, ALU.mult, ALU.add) \
                    .then_inc(var_ready.sem, 1)

            def prepare_weights():
                dve.wait_ge(w_loaded, 160)
                dve.wait_ge(consts_made, 3)
                step = Steps(dve_setup)
                step.begin(0)
                for k, spread_w in ((0, src0), (1, dst0)):
                    dve.tensor_tensor(w_tmp[:], rhs0[:, 0:D], a0_row[:, k, :], ALU.mult).then_inc(step.sem, 1)
                    dve.wait_ge(step.sem, step.step())
                    dve.tensor_reduce(rhs0[:, D + k:D + k + 1], w_tmp[:], AX_X, ALU.add).then_inc(step.sem, 1)
                    dve.wait_ge(step.sem, step.step())
                    dve.tensor_copy(spread_w[:], rhs0[:, D + k:D + k + 1].broadcast_to([P, P]))
                for k in range(2):
                    dve.tensor_tensor(w_tmp[:].rearrange("p (h o) -> p h o", h=H1),
                                      rhs1[:, 0:D].rearrange("p (h o) -> p h o", h=H1),
                                      a1_row[:, :, k * O1:(k + 1) * O1], ALU.mult).then_inc(step.sem, 1)
                    dve.wait_ge(step.sem, step.step())
                    dve.tensor_reduce(rhs1[:, D + k * H1:D + (k + 1) * H1],
                                      w_tmp[:].rearrange("p (h o) -> p h o", h=H1), AX_X, ALU.add).then_inc(step.sem, 1)
                    dve.wait_ge(step.sem, step.step())
                dve.memset(pick1[:], 0.0)
                dve.memset(s1_parts[:], 0.0).then_inc(step.sem, 1)
                dve.wait_ge(step.sem, step.step())
                for k in range(PARTS):
                    part = slice(32 * k, 32 * k + H1)
                    dve.tensor_copy(pick1[part, :, :], spread_over(ident[part, part], P))
                dve.tensor_copy(identb[:], ident[:])
                dve.memset(h1[:, :, :, O1:C1], 1.0)
                dve.memset(w3[:, :, O3:C3], 1.0)
                dve.wait_ge(self_turned, 1)
                dve.tensor_copy(rhs2[:, D:2 * D], fp[:, 0, 0:P]).then_inc(weights_ready, 1)

            def layer0_top(b):
                dve.wait_ge(t0_spread.sem, t0_spread.of(b))
                dve.tensor_reduce(T0[:], fp_pair, AX_X, ALU.max).then_inc(front.sem, 1)
                dve.wait_ge(front.sem, front.step())
                dve.tensor_scalar(T0neg[:], T0[:], -1.0, None, ALU.mult)
                dve.tensor_scalar(T0neg2[:], T0[:], -SLOPE, None, ALU.mult).then_inc(T0_ready.sem, 1)

            def layer0_z(b):
                dve.wait_ge(s0_spread.sem, s0_spread.of(b))
                dve.tensor_scalar(c0, fp_pair, T0[:], 0.0, ALU.add, ALU.max).then_inc(z0_ready.sem, 1)

            def layer0_unit(b, third, jt):
                if jt == 0:
                    dve.wait_ge(c0_ready.sem, c0_ready.of(b))
                    dve.wait_ge(h0_ready.sem, h0_ready.of(b))
                    dve.wait_ge(at_ready.sem, at_ready.of(b))
                w = weight0[:, jt % P0_RING, :]
                if jt >= P0_RING:
                    dve.wait_ge(weight0_used.sem, weight0_used.of(b, jt - P0_RING + 1))
                    dve.wait_ge(weight0_added.sem, weight0_added.of(b, max(jt - P0_RING, 1)))
                dve.tensor_scalar(w, c0, v0s[:, jt:jt + 1], v0[:, jt:jt + 1], ALU.mult, ALU.max) \
                    .then_inc(front.sem, 1)
                dve.wait_ge(front.sem, front.step())
                dve.tensor_tensor(w, w, AT[:, third, jt, :], ALU.mult).then_inc(weight0_ready.sem, 1)

            def layer0_finish(b):
                dve.wait_ge(den0_made.sem, den0_made.of(b))
                dve.reciprocal(rec0[:], fp[:, 0, 0:T]).then_inc(front.sem, 1)
                dve.wait_ge(front.sem, front.step())
                dve.wait_ge(num0_turned.sem, num0_turned.of(b))
                dve.tensor_tensor(yf[:], fp_pair.rearrange("p (t d) -> p t d", t=T), spread_over(rec0[:], D),
                                  ALU.mult).then_inc(front.sem, 1)
                dve.wait_ge(front.sem, front.step())
                flat = "p t d -> p (t d)"
                dve.scalar_tensor_tensor(out=yf.rearrange(flat), in0=yf.rearrange(flat), scalar=0.0,
                                         in1=x0.rearrange(flat), op0=ALU.max, op1=ALU.add).then_inc(front.sem, 1)
                dve.wait_ge(front.sem, front.step())
                layer_stats(front, yf, fstat, fsmall, fvar_ready)

            def layer1_top(b):
                dve.wait_ge(st1_ready.sem, st1_ready.of(b))
                dve.tensor_reduce(tmax1[:], st1[:, :, H1:2 * H1].rearrange("p t h -> p h t"), AX_X, ALU.max) \
                    .then_inc(tmax1_ready.sem, 1)
                dve.tensor_scalar(tneg1[:], st1[:, :, H1:2 * H1], -1.0, None, ALU.mult)
                dve.tensor_scalar(tbig1[:], st1[:, :, H1:2 * H1], BIG, None, ALU.mult)

            def layer1_turned_maxima(b):
                dve.wait_ge(tmax1_turned.sem, tmax1_turned.of(b))
                dve.tensor_reduce(tcol1[:], fp[0:H1, 0, 0:P], AX_X, ALU.max).then_inc(front.sem, 1)
                dve.wait_ge(front.sem, front.step())
                dve.tensor_scalar(tdiag1[:], ident[0:H1, 0:H1], tcol1[:], None, ALU.mult) \
                    .then_inc(tdiag1_ready.sem, 1)

            def layer1_shifts(b):
                dve.wait_ge(T1_spread.sem, T1_spread.of(b))
                dve.tensor_copy(T1[:], fp[:, 0, P:P + H1]).then_inc(front.sem, 1)
                dve.wait_ge(front.sem, front.step())
                T1_tiles = T1[:].unsqueeze(1).broadcast_to([P, T, H1])
                dve.tensor_tensor(dt1[:], st1[:, :, H1:2 * H1], T1_tiles, ALU.subtract)
                dve.tensor_tensor(zs1[:], st1[:, :, 0:H1], T1_tiles, ALU.add).then_inc(front.sem, 1)
                dve.wait_ge(front.sem, front.step())
                dve.tensor_scalar(zs1[:], zs1[:], 0.0, None, ALU.max).then_inc(z1_ready.sem, 1)

            def layer1_columns(b):
                dve.wait_ge(v1_ready.sem, v1_ready.of(b))
                dve.wait_ge(h1_ready.sem, h1_ready.of(b))
                flat = "p t h c -> p (t h) c"
                for k in range(2):
                    last = dve.tensor_tensor(vh[:, :, :, k, :].rearrange(flat), h1[:].rearrange(flat),
                                             spread_over(v1[:, k].rearrange("p t h -> p (t h)"), C1), ALU.mult)
                last.then_inc(vh_whole.sem, 1)

            def layer1_cut_sources(b):
                dve.wait_ge(s1_first.sem, s1_first.of(b))
                dve.tensor_tensor(s1_rest, fp_pair[0:H1, :], s1_parts[0:H1, :], ALU.subtract).then_inc(front.sem, 1)
                dve.wait_ge(front.sem, front.step())
                dve.tensor_copy(s1_mid, s1_rest).then_inc(front.sem, 1)
                dve.wait_ge(front.sem, front.step())
                dve.tensor_copy(s1_parts[32:32 + H1, :], s1_mid)
                dve.tensor_tensor(s1_parts[64:64 + H1, :], s1_rest, s1_mid, ALU.subtract).then_inc(s1_cut.sem, 1)

            def layer1_cut(b):
                flat = "p t h a c -> p (t h) (a c)"
                dve.wait_ge(vh_first.sem, vh_first.of(b))
                dve.tensor_tensor(vh_rest[:].rearrange(flat), vh[:].rearrange(flat),
                                  vh_parts[:, :, :, 0, :, :].rearrange(flat), ALU.subtract).then_inc(vh_rested.sem, 1)

            def layer1_cut_third(b):
                flat = "p t h a c -> p (t h) (a c)"
                dve.wait_ge(vh_second.sem, vh_second.of(b))
                dve.tensor_tensor(vh_parts[:, :, :, 2, :, :].rearrange(flat), vh_rest[:].rearrange(flat),
                                  vh_parts[:, :, :, 1, :, :].rearrange(flat), ALU.subtract).then_inc(vh_ready.sem, 1)

            def layer1_unit(b, third, u):
                h, jt = u // T, u % T
                if u >= B_RING:
                    dve.wait_ge(edges_used.sem, edges_used.of(b, u - B_RING + 1))
                if u in RAMPS:
                    r = RAMPS.index(u)
                    dve.wait_ge(ramp_ready.sem, ramp_ready.of(b, r + 1))
                    dve.tensor_tensor(edges[:, u % B_RING, :], ramp[:, r % R_RING, :], AT[:, third, jt, :],
                                      ALU.min).then_inc(edges_ready.sem, 1)
                else:
                    dve.wait_ge(s1_ready.sem, s1_ready.of(b, 2 * h + 2))
                    dve.scalar_tensor_tensor(out=edges[:, u % B_RING, :], in0=s1row[:, h % S_RING, :],
                                             scalar=tneg1[:, jt, h:h + 1], in1=AT[:, third, jt, :], op0=ALU.is_gt,
                                             op1=ALU.mult).then_inc(edges_ready.sem, 1)

            def layer1_head_out(b, h):
                dve.wait_ge(edges_used.sem, edges_used.of(b, (h + 1) * T))
                parts = fp_pair.rearrange("p (t c) -> p t c", t=T)[:, :, 0:2 * PARTS * C1].rearrange(
                    "p t (k c) -> p t c k", k=PARTS)
                dve.tensor_reduce(sumB[:, :, h, :, :].rearrange("p t a c -> p t (a c)"), parts, AX_X, ALU.add) \
                    .then_inc(sumB_ready.sem, 1)

            def layer1_finish(b):
                dve.wait_ge(sumA_ready.sem, sumA_ready.of(b))
                dve.wait_ge(sumB_ready.sem, sumB_ready.of(b))
                flat = "p t h c -> p (t h) c"
                A = sumA[:].rearrange(flat)
                Bv, Bs = (sumB[:, :, :, a, :].rearrange(flat) for a in range(2))
                dve.tensor_tensor(A, A, Bs, ALU.subtract).then_inc(front_last.sem, 1)
                dve.wait_ge(front_last.sem, front_last.step())
                dve.tensor_tensor(A, A, spread_over(c1[:].rearrange("p t h -> p (t h)"), C1), ALU.mult).then_inc(front_last.sem, 1)
                dve.wait_ge(front_last.sem, front_last.step())
                dve.tensor_tensor(A, A, Bv, ALU.add).then_inc(front_last.sem, 1)
                dve.wait_ge(front_last.sem, front_last.step())

            def layer1_divide(b):
                A = sumA[:].rearrange("p t h c -> p (t h) c")
                dve.reciprocal(rec1[:].rearrange("p t h -> p (t h)"), A[:, :, O1]).then_inc(front_last.sem, 1)
                dve.wait_ge(front_last.sem, front_last.step())
                o = yf.rearrange("p t (h o) -> p (t h) o", h=H1)
                dve.tensor_tensor(o, A[:, :, 0:O1],
                                  spread_over(rec1[:].rearrange("p t h -> p (t h)"), O1), ALU.mult).then_inc(front_last.sem, 1)
                dve.wait_ge(front_last.sem, front_last.step())
                dve.tensor_scalar(elu[:], yf[:], 0.0, None, ALU.min).then_inc(elu_min.sem, 1)
                flat = "p t d -> p (t d)"
                dve.scalar_tensor_tensor(out=yf.rearrange(flat), in0=yf.rearrange(flat), scalar=0.0,
                                         in1=x1.rearrange(flat), op0=ALU.max, op1=ALU.add).then_inc(front_last.sem, 1)
                dve.wait_ge(front_last.sem, front_last.step())

            def layer1_elu(b):
                flat = "p t d -> p (t d)"
                dve.wait_ge(elu_exp.sem, elu_exp.of(b))
                dve.scalar_tensor_tensor(out=yf.rearrange(flat), in0=elu.rearrange(flat), scalar=-1.0,
                                         in1=yf.rearrange(flat), op0=ALU.add, op1=ALU.add).then_inc(front_last.sem, 1)
                dve.wait_ge(front_last.sem, front_last.step())
                layer_stats(front_last, yf, fstat, fsmall, fvar_ready)

            def layer2_columns(b):
                dve.wait_ge(y2_made.sem, y2_made.of(b))
                src = kp[:, 1:5, :].rearrange("p a (n c) -> p (a n) c", n=2)
                dve.memset(y2_hi[:, :, D:D + 1], 1.0)
                dve.tensor_copy(y2_hi[:, :, 0:D], src[:, :, 0:D]).then_inc(back.sem, 1)
                dve.wait_ge(back.sem, back.step())
                dve.tensor_tensor(rest2, src[:, :, 0:D], y2_hi[:, :, 0:D], ALU.subtract)
                dve.tensor_tensor(self2, src[:, :, D:2 * D], per_tile(bias2[:]), ALU.add).then_inc(back.sem, 1)
                dve.wait_ge(back.sem, back.step())

            def layer2_columns_low(b):
                dve.tensor_copy(y2_lo[:, :, 0, :], rest2).then_inc(back.sem, 1)
                dve.wait_ge(back.sem, back.step())
                dve.tensor_tensor(y2_lo[:, :, 1, :], rest2, y2_lo[:, :, 0, :], ALU.subtract) \
                    .then_inc(y2_ready.sem, 1)

            def layer2_out(b):
                dve.wait_ge(sum2_made.sem, sum2_made.of(b))
                for g in range(len(GROUPS)):
                    last = dve.tensor_scalar(deg2[:, tiles(g)], thirds(kp, g, D + 1)[:, :, D], 1e-6, None, ALU.max)
                last.then_inc(back.sem, 1)
                dve.wait_ge(back.sem, back.step())
                dve.reciprocal(deg2[:], deg2[:]).then_inc(back.sem, 1)
                dve.wait_ge(back.sem, back.step())
                if stored.any_before(b):
                    dve.wait_ge(stored.sem, stored.before(b))
                for g in range(len(GROUPS)):
                    for n, t in enumerate(GROUPS[g]):
                        last = dve.scalar_tensor_tensor(out=yb[:, t, :], in0=thirds(kp, g, D + 1)[:, n, 0:D],
                                                        scalar=deg2[:, t:t + 1], in1=self2[:, t, :], op0=ALU.mult,
                                                        op1=ALU.add)
                last.then_inc(back.sem, 1)
                dve.wait_ge(back.sem, back.step())

            def layer2_stats(b):
                layer_stats(back, yb, bstat, bsmall, bvar_ready)

            def layer2_relu(b):
                dve.wait_ge(affine2_ready.sem, affine2_ready.of(b))
                flat = "p t d -> p (t d)"
                dve.scalar_tensor_tensor(out=yb.rearrange(flat), in0=yb.rearrange(flat), scalar=0.0,
                                         in1=x2.rearrange(flat), op0=ALU.max, op1=ALU.add) \
                    .then_inc(back.sem, 1)
                dve.wait_ge(back.sem, back.step())
                layer_stats(back, yb, bstat, bsmall, bvar_ready)

            def layer3_cut(b):
                dve.wait_ge(w3_ready.sem, w3_ready.of(b))
                W = w3[:, :, 0:O3]
                dve.tensor_tensor(rest3, W, cutA[:, :, 2, :], ALU.subtract).then_inc(back.sem, 1)
                dve.wait_ge(back.sem, back.step())
                dve.tensor_copy(cutA[:, :, 0, :], rest3)
                dve.tensor_copy(cutB[:, :, 0:3, :],
                                cutA[:, :, 2, :].unsqueeze(2).broadcast_to([P, T * H3, 3, O3])) \
                    .then_inc(back.sem, 1)
                dve.wait_ge(back.sem, back.step())

            def layer3_cut_low(b):
                dve.tensor_copy(cutA[:, :, 3, :], cutA[:, :, 0, :])
                dve.tensor_copy(cutB[:, :, 3, :], cutA[:, :, 0, :]).then_inc(cuts_ready.sem, 1)

            def layer3_lengths(b):
                dve.wait_ge(squares_ready.sem, squares_ready.of(b))
                dve.tensor_reduce(q3[:], squares3, AX_X, ALU.add).then_inc(back.sem, 1)
                dve.wait_ge(back.sem, back.step())
                dve.tensor_reduce(qmax3[:], q3[:].rearrange("p (t h) -> p h t", h=H3), AX_X, ALU.max) \
                    .then_inc(qmax_ready.sem, 1)

            def layer3_turned_maxima(b):
                dve.wait_ge(qmax_turned.sem, qmax_turned.of(b))
                dve.tensor_reduce(qcol3[:], kp[0:H3, 0, 0:P], AX_X, ALU.max).then_inc(back.sem, 1)
                dve.wait_ge(back.sem, back.step())
                dve.tensor_scalar(qdiag3[:], ident[0:H3, 0:H3], qcol3[:], None, ALU.mult) \
                    .then_inc(qdiag_ready.sem, 1)

            def layer3_shift(b):
                dve.wait_ge(q_spread.sem, q_spread.of(b))
                dve.tensor_scalar(shift3[:], kp[:, 0, P:P + H3], -ROOT, None, ALU.mult).then_inc(shift_ready.sem, 1)

            def layer3_turn_cuts(b, h):
                dve.wait_ge(cut_turned.sem, cut_turned.of(b, 2 * h + 2))
                dve.tensor_copy(cutT[:, h, 1, :], kp[:, 1 + (2 * h + 1) % 4, :].bitcast(BF16)) \
                    .then_inc(cutT_dve.sem, 1)

            def layer3_mask(b, third, w):
                dve.wait_ge(exp3_ready.sem, exp3_ready.of(b, 2 * w + 2))
                tile = weight3[:, w % P_RING, :]
                dve.tensor_tensor(tile, tile, AT[:, third, w % T, :], ALU.mult).then_inc(masked_dve.sem, 1)

            def layer3_finish(b):
                dve.wait_ge(sum3_turned.sem, sum3_turned.of(b))
                src = [thirds(kp[:, 2:5], g, H3 * C3).rearrange("p t (h c) -> p t h c", h=H3)
                       for g in range(len(GROUPS))]
                for g in range(len(GROUPS)):
                    last = dve.reciprocal(rec3[:, tiles(g), :], src[g][:, :, :, O3])
                last.then_inc(back_last.sem, 1)
                dve.wait_ge(back_last.sem, back_last.step())
                for g in range(len(GROUPS)):
                    last = dve.tensor_tensor(yb[:, tiles(g), :].rearrange("p t (h o) -> p t h o", h=H3),
                                             src[g][:, :, :, 0:O3], spread_over(rec3[:, tiles(g), :], O3), ALU.mult)
                last.then_inc(o3_ready.sem, 1)

            def layer3_residual(b):
                dve.wait_ge(y4_ready.sem, y4_ready.of(b))
                layer_stats(back_last, yb, bstat, bsmall, bvar_ready)

            prepare_weights()

            def section_a(r, f, k, m):
                if m is not None:
                    back_last.begin(m)
                if k is not None:
                    back.begin(k)
                for s in range(A_STEPS):
                    if f is not None and s < U1 // 2:
                        layer1_unit(f, r, 2 * s)
                        layer1_unit(f, r, 2 * s + 1)
                    if f is not None and s % 4 == 0 and s > 1:
                        layer1_head_out(f, s // 4 - 1)
                    if m is not None and s == A_DVE["finish3"]:
                        layer3_finish(m)
                    if m is not None and s == A_DVE["residual3"]:
                        layer3_residual(m)
                    if k is not None:
                        if s == A_DVE["columns2"]:
                            layer2_columns(k)
                        if s == A_DVE["columns2_low"]:
                            layer2_columns_low(k)
                        if s == A_DVE["out2"]:
                            layer2_out(k)
                        if s == A_DVE["stats2"]:
                            layer2_stats(k)
                        if s == A_DVE["relu2"]:
                            layer2_relu(k)
                        if s == A_DVE["cut3"]:
                            layer3_cut(k)
                        if s == A_DVE["cut3_low"]:
                            layer3_cut_low(k)
                        if s == A_DVE["lengths3"]:
                            layer3_lengths(k)
                        if A_DVE["cuts"] <= s < A_DVE["cuts"] + H3:
                            layer3_turn_cuts(k, s - A_DVE["cuts"])
                        if s == A_DVE["maxima3"]:
                            layer3_turned_maxima(k)
                        if s == A_DVE["shift3"]:
                            layer3_shift(k)

            def section_b(r, n, f, k):
                third = (r + 1) % 3
                if f is not None:
                    front_last.begin(f)
                if n is not None:
                    front.begin(n)
                for s in range(B_STEPS):
                    if k is not None and 1 <= s <= U3 and s - 1 in DVE_MASKS:
                        layer3_mask(k, (r + 2) % 3, s - 1)
                    if f is not None:
                        if s == B_DVE["finish1"]:
                            layer1_finish(f)
                        if s == B_DVE["divide1"]:
                            layer1_divide(f)
                        if s == B_DVE["elu1"]:
                            layer1_elu(f)
                    if n is not None:
                        if s == B_DVE["top0"]:
                            layer0_top(n)
                        if s == B_DVE["z0"]:
                            layer0_z(n)
                        for jt in range(T):
                            if s == B_DVE["unit0"] + jt // 2:
                                layer0_unit(n, third, jt)
                        if s == B_DVE["finish0"]:
                            if x2_ready.any_before(n):
                                dve.wait_ge(x2_ready.sem, x2_ready.before(n))
                            layer0_finish(n)
                        if s == B_DVE["top1"]:
                            layer1_top(n)
                        if s == B_DVE["maxima1"]:
                            layer1_turned_maxima(n)
                        if s == B_DVE["shifts1"]:
                            layer1_shifts(n)
                        if s == B_DVE["sources1"]:
                            layer1_cut_sources(n)
                        if s == B_DVE["columns1"]:
                            layer1_columns(n)
                        if s == B_DVE["cut1"]:
                            layer1_cut(n)
                        if s == B_DVE["cut1_third"]:
                            layer1_cut_third(n)

            schedule(dve, section_a, section_b)


_INS = ["x", "adj", "L0_gnn_W", "L0_gnn_a", "L1_gnn_W", "L1_gnn_a", "L2_gnn_rel_weights", "L2_gnn_self_w",
        "L2_gnn_self_b", "L2_gnn_ln_gamma", "L2_gnn_ln_beta", "L3_gnn_W"]


def kernel(**inputs):
    import numpy as _np
    import concourse.bacc as _bacc
    from concourse import mybir as _mybir
    from concourse.bass_utils import run_bass_kernel_spmd as _run

    nc = _bacc.Bacc("TRN2", target_bir_lowering=False, num_devices=1)
    arrays, args = {}, []
    for name in _INS:
        a = _np.ascontiguousarray(inputs[name])
        arrays[f"in_{name}_dram"] = a
        args.append(nc.dram_tensor(f"in_{name}_dram", a.shape, _mybir.dt.from_np(a.dtype), kind="ExternalInput").ap())
    shape = tuple(inputs["x"].shape)
    args.append(nc.dram_tensor("out_0_dram", shape, _mybir.dt.float32, kind="ExternalOutput").ap())
    graph_stack(nc, *args)
    r = _run(nc, [arrays], core_ids=[0])
    return r.results[0]["out_0_dram"]
```
